# Optimizing a Trainium2 kernel written in Bass

```python
import numpy as np
import jax
import jax.numpy as jnp

def _softmax(x, axis=-1):
    return jax.nn.softmax(x, axis=axis)

def _gelu(x):
    return jax.nn.gelu(x, approximate=True)

def _silu(x):
    return jax.nn.silu(x)

def _sigmoid(x):
    return jax.nn.sigmoid(x)

def _layernorm(x, axis=-1, eps=1e-05):
    m = jnp.mean(x, axis=axis, keepdims=True)
    v = jnp.var(x, axis=axis, keepdims=True)
    return (x - m) / jnp.sqrt(v + eps)

def _scatter_add(tgt, idx, src, axis=0):
    return tgt.at[idx].add(src)

def _segment_sum(src, seg, n):
    return jax.ops.segment_sum(src, seg, n)
kernel_name = 'mk_hybrid_d2_jaxref_r8_33ad2d'

def setup_inputs(seed: int=0):
    np.random.seed(seed)
    _w = jnp.asarray

    def _L0_attn_a_setup():
        import jax, jax.numpy as jnp
        import numpy as np
        D_MODEL = 256
        N_HEADS = 16
        SEQ_LEN = 256
        BATCH = 2
        BIAS_MAX = 8.0

        def alibi_bias(n_heads, seq_len, dtype):
            pos = jnp.arange(1 - seq_len, 1, dtype=dtype)
            m = jnp.arange(1, n_heads + 1, dtype=dtype) * (BIAS_MAX / n_heads)
            slopes = 1.0 / 2.0 ** m
            return pos[None, :] * slopes[:, None]
        key = jax.random.key(seed)
        k1, k2, k3 = jax.random.split(key, 3)
        s = 1.0 / np.sqrt(D_MODEL)
        x = jax.random.normal(k1, (BATCH, SEQ_LEN, D_MODEL), dtype=jnp.float32)
        Wqkv = jax.random.normal(k2, (3 * D_MODEL, D_MODEL), dtype=jnp.float32) * s
        b_qkv = jnp.zeros((3 * D_MODEL,), dtype=jnp.float32)
        Wout = jax.random.normal(k3, (D_MODEL, D_MODEL), dtype=jnp.float32) * s
        b_out = jnp.zeros((D_MODEL,), dtype=jnp.float32)
        return {'x': x, 'Wqkv': Wqkv, 'b_qkv': b_qkv, 'Wout': Wout, 'b_out': b_out}
    _L0_attn_a_in = _L0_attn_a_setup()

    def _L0_attn_b_setup():
        import jax, jax.numpy as jnp
        import numpy as np
        key = jax.random.key(seed)
        x = jax.random.normal(key, (8, 96, 256), dtype=jnp.float32)
        return {'x': x}
    _L0_attn_b_in = _L0_attn_b_setup()

    def _L0_ffn_setup():
        import jax, jax.numpy as jnp
        import numpy as np
        HIDDEN = 256
        INTER = 1024
        RETRIEVAL = 128
        NUM_EXPERTS = 512
        NUM_KEYS = 64
        TOP_K = 8
        B, S = (4, 256)
        key = jax.random.key(seed)
        ks = jax.random.split(key, 8)
        sc = 0.02
        return {'hidden_states': jax.random.normal(ks[0], (B, S, HIDDEN), jnp.float32), 'W_q': jax.random.normal(ks[1], (HIDDEN, RETRIEVAL), jnp.float32) * sc, 'keys': jax.random.normal(ks[2], (2, RETRIEVAL // 2, NUM_KEYS), jnp.float32) * sc, 'down_embed': jax.random.normal(ks[3], (NUM_EXPERTS, HIDDEN), jnp.float32) * sc, 'up_embed': jax.random.normal(ks[4], (NUM_EXPERTS, HIDDEN), jnp.float32) * sc, 'gate_w': jax.random.normal(ks[5], (HIDDEN, INTER), jnp.float32) * sc, 'up_w': jax.random.normal(ks[6], (HIDDEN, INTER), jnp.float32) * sc, 'down_w': jax.random.normal(ks[7], (INTER, HIDDEN), jnp.float32) * sc}
    _L0_ffn_in = _L0_ffn_setup()

    def _L1_attn_a_setup():
        import jax, jax.numpy as jnp
        import numpy as np
        B, S, D = (2, 256, 256)
        N_HEADS, N_KV_HEADS = (16, 4)
        HEAD_DIM = D // N_HEADS

        def _apply_rope(xh, positions):
            Dh = xh.shape[-1]
            half = Dh // 2
            freqs = 1.0 / 10000.0 ** (jnp.arange(half, dtype=jnp.float32) / half)
            angles = positions[:, None].astype(jnp.float32) * freqs[None, :]
            cos, sin = (jnp.cos(angles), jnp.sin(angles))
            xp = xh.reshape(*xh.shape[:-1], half, 2)
            x0, x1 = (xp[..., 0], xp[..., 1])
            r0 = x0 * cos - x1 * sin
            r1 = x0 * sin + x1 * cos
            return jnp.stack([r0, r1], axis=-1).reshape(xh.shape)
        key = jax.random.key(seed)
        ks = jax.random.split(key, 5)
        x = jax.random.normal(ks[0], (B, S, D), dtype=jnp.float32)
        W_q = jax.random.normal(ks[1], (D, D), dtype=jnp.float32) * 0.02
        W_k = jax.random.normal(ks[2], (D, N_KV_HEADS * HEAD_DIM), dtype=jnp.float32) * 0.02
        W_v = jax.random.normal(ks[3], (D, N_KV_HEADS * HEAD_DIM), dtype=jnp.float32) * 0.02
        W_o = jax.random.normal(ks[4], (D, D), dtype=jnp.float32) * 0.02
        return {'x': x, 'W_q': W_q, 'W_k': W_k, 'W_v': W_v, 'W_o': W_o}
    _L1_attn_a_in = _L1_attn_a_setup()

    def _L1_attn_b_setup():
        import jax, jax.numpy as jnp
        import numpy as np
        B, T, C = (4, 512, 256)
        key = jax.random.key(seed)
        k0, k1, k2, k3 = jax.random.split(key, 4)
        s = 0.02
        x = jax.random.normal(k0, (B, T, C), jnp.float32)
        W_act = jax.random.normal(k1, (C, 2 * C), jnp.float32) * s
        W_val = jax.random.normal(k2, (C, C), jnp.float32) * s
        W_rec = jax.random.normal(k3, (C, 2 * C), jnp.float32) * s
        return {'x': x, 'W_act': W_act, 'W_val': W_val, 'W_rec': W_rec}
    _L1_attn_b_in = _L1_attn_b_setup()

    def _L1_ffn_setup():
        import jax, jax.numpy as jnp
        import numpy as np

        def _sparsify_2to4(h):
            B, S, I = h.shape
            g = h.reshape(B, S, I // 4, 4)
            a = jnp.abs(g)
            _, idx = jax.lax.top_k(a, 2)
            pos = jnp.arange(4)
            mask = (pos == idx[..., 0:1]) | (pos == idx[..., 1:2])
            return (g * mask.astype(g.dtype)).reshape(B, S, I)
        key = jax.random.key(seed)
        k1, k2, k3, k4 = jax.random.split(key, 4)
        B, S, H, I = (4, 256, 256, 1024)
        x = jax.random.normal(k1, (B, S, H), dtype=jnp.float32)
        w_gate = jax.random.normal(k2, (H, I), dtype=jnp.float32) / np.sqrt(H)
        w_up = jax.random.normal(k3, (H, I), dtype=jnp.float32) / np.sqrt(H)
        w_down = jax.random.normal(k4, (I, H), dtype=jnp.float32) / np.sqrt(I)
        return {'x': x, 'w_gate': w_gate, 'w_up': w_up, 'w_down': w_down}
    _L1_ffn_in = _L1_ffn_setup()
    _d = {'L0_attn_a_x': _L0_attn_a_in['x'], 'L0_attn_a_Wqkv': _L0_attn_a_in['Wqkv'], 'L0_attn_a_b_qkv': _L0_attn_a_in['b_qkv'], 'L0_attn_a_Wout': _L0_attn_a_in['Wout'], 'L0_attn_a_b_out': _L0_attn_a_in['b_out'], 'L0_ffn_W_q': _L0_ffn_in['W_q'], 'L0_ffn_keys': _L0_ffn_in['keys'], 'L0_ffn_down_embed': _L0_ffn_in['down_embed'], 'L0_ffn_up_embed': _L0_ffn_in['up_embed'], 'L0_ffn_gate_w': _L0_ffn_in['gate_w'], 'L0_ffn_up_w': _L0_ffn_in['up_w'], 'L0_ffn_down_w': _L0_ffn_in['down_w'], 'L1_attn_a_W_q': _L1_attn_a_in['W_q'], 'L1_attn_a_W_k': _L1_attn_a_in['W_k'], 'L1_attn_a_W_v': _L1_attn_a_in['W_v'], 'L1_attn_a_W_o': _L1_attn_a_in['W_o'], 'L1_attn_b_W_act': _L1_attn_b_in['W_act'], 'L1_attn_b_W_val': _L1_attn_b_in['W_val'], 'L1_attn_b_W_rec': _L1_attn_b_in['W_rec'], 'L1_ffn_w_gate': _L1_ffn_in['w_gate'], 'L1_ffn_w_up': _L1_ffn_in['w_up'], 'L1_ffn_w_down': _L1_ffn_in['w_down']}
    _x0 = _d['L0_attn_a_x']
    _d['L0_attn_a_x'] = jax.random.normal(jax.random.fold_in(jax.random.key(seed), 1), (4, 512, 256), dtype=_x0.dtype)
    del _x0
    return _d

def reference(L0_attn_a_x, L0_attn_a_Wqkv, L0_attn_a_b_qkv, L0_attn_a_Wout, L0_attn_a_b_out, L0_ffn_W_q, L0_ffn_keys, L0_ffn_down_embed, L0_ffn_up_embed, L0_ffn_gate_w, L0_ffn_up_w, L0_ffn_down_w, L1_attn_a_W_q, L1_attn_a_W_k, L1_attn_a_W_v, L1_attn_a_W_o, L1_attn_b_W_act, L1_attn_b_W_val, L1_attn_b_W_rec, L1_ffn_w_gate, L1_ffn_w_up, L1_ffn_w_down):

    def _L0_attn_a_ref(x, Wqkv, b_qkv, Wout, b_out):
        import jax, jax.numpy as jnp
        import numpy as np
        D_MODEL = 256
        N_HEADS = 16
        SEQ_LEN = 256
        BATCH = 2
        BIAS_MAX = 8.0

        def alibi_bias(n_heads, seq_len, dtype):
            pos = jnp.arange(1 - seq_len, 1, dtype=dtype)
            m = jnp.arange(1, n_heads + 1, dtype=dtype) * (BIAS_MAX / n_heads)
            slopes = 1.0 / 2.0 ** m
            return pos[None, :] * slopes[:, None]
        B, S, D = x.shape
        H = N_HEADS
        hd = D // H
        scale = 1.0 / jnp.sqrt(jnp.asarray(hd, dtype=x.dtype))
        qkv = x @ Wqkv.T + b_qkv
        q, k, v = jnp.split(qkv, 3, axis=-1)
        q = q.reshape(B, S, H, hd)
        k = k.reshape(B, S, H, hd)
        v = v.reshape(B, S, H, hd)
        scores = jnp.einsum('bqhd,bkhd->bhqk', q, k) * scale
        bias = alibi_bias(H, S, x.dtype)
        scores = scores + bias[None, :, None, :]
        causal = jnp.tril(jnp.ones((S, S), dtype=bool))
        scores = jnp.where(causal[None, None, :, :], scores, jnp.asarray(-1000000000.0, dtype=x.dtype))
        p = jax.nn.softmax(scores, axis=-1)
        ctx = jnp.einsum('bhqk,bkhd->bqhd', p, v).reshape(B, S, D)
        return ctx @ Wout.T + b_out

    def _L0_attn_b_ref(x):
        import jax, jax.numpy as jnp
        import numpy as np
        energy = jnp.einsum('bci,bcj->bij', x, x)
        attention = jax.nn.softmax(energy, axis=-1)
        out = jnp.einsum('bcj,bij->bci', x, attention)
        return out

    def _L0_ffn_ref(hidden_states, W_q, keys, down_embed, up_embed, gate_w, up_w, down_w):
        import jax, jax.numpy as jnp
        import numpy as np
        HIDDEN = 256
        INTER = 1024
        RETRIEVAL = 128
        NUM_EXPERTS = 512
        NUM_KEYS = 64
        TOP_K = 8
        B, S = (4, 256)
        b, s, h = hidden_states.shape
        n = b * s
        queries = (hidden_states @ W_q).reshape(2, n, RETRIEVAL // 2)
        routing = jnp.einsum('tnd,tdk->tnk', queries, keys)
        scores2, idx2 = jax.lax.top_k(routing, TOP_K)
        sx, sy = (scores2[0], scores2[1])
        ix, iy = (idx2[0], idx2[1])
        all_scores = (sx[:, :, None] + sy[:, None, :]).reshape(n, TOP_K * TOP_K)
        all_idx = (ix[:, :, None] * NUM_KEYS + iy[:, None, :]).reshape(n, TOP_K * TOP_K)
        scores, pk = jax.lax.top_k(all_scores, TOP_K)
        indices = jnp.take_along_axis(all_idx, pk, axis=-1)
        de = down_embed[indices]
        ue = up_embed[indices]
        x = hidden_states.reshape(n, h)
        ew = jnp.einsum('nh,nkh->nk', x, de)
        ew = jax.nn.silu(ew) * jax.nn.softmax(scores, axis=-1)
        experts_states = jnp.einsum('nk,nkh->nh', ew, ue).reshape(b, s, h)
        mlp = jax.nn.silu(x @ gate_w) * (x @ up_w) @ down_w
        return mlp.reshape(b, s, h) + experts_states

    def _L1_attn_a_ref(x, W_q, W_k, W_v, W_o):
        import jax, jax.numpy as jnp
        import numpy as np
        B, S, D = (2, 256, 256)
        N_HEADS, N_KV_HEADS = (16, 4)
        HEAD_DIM = D // N_HEADS

        def _apply_rope(xh, positions):
            Dh = xh.shape[-1]
            half = Dh // 2
            freqs = 1.0 / 10000.0 ** (jnp.arange(half, dtype=jnp.float32) / half)
            angles = positions[:, None].astype(jnp.float32) * freqs[None, :]
            cos, sin = (jnp.cos(angles), jnp.sin(angles))
            xp = xh.reshape(*xh.shape[:-1], half, 2)
            x0, x1 = (xp[..., 0], xp[..., 1])
            r0 = x0 * cos - x1 * sin
            r1 = x0 * sin + x1 * cos
            return jnp.stack([r0, r1], axis=-1).reshape(xh.shape)
        b, s, d = x.shape
        positions = jnp.arange(s)
        rep = N_HEADS // N_KV_HEADS
        Q = (x @ W_q).reshape(b, s, N_HEADS, HEAD_DIM).transpose(0, 2, 1, 3)
        K = (x @ W_k).reshape(b, s, N_KV_HEADS, HEAD_DIM).transpose(0, 2, 1, 3)
        V = (x @ W_v).reshape(b, s, N_KV_HEADS, HEAD_DIM).transpose(0, 2, 1, 3)
        Qr = _apply_rope(Q, positions)
        K_rep = jnp.tile(K, (1, rep, 1, 1))
        V_rep = jnp.tile(V, (1, rep, 1, 1))
        Kr = _apply_rope(K_rep, positions)
        scores = jnp.einsum('bhqd,bhkd->bhqk', Qr, Kr) / HEAD_DIM ** 0.5
        weights = jax.nn.softmax(scores, axis=-1)
        out = jnp.einsum('bhqk,bhkd->bhqd', weights, V_rep)
        out = out.transpose(0, 2, 1, 3).reshape(b, s, d)
        return out @ W_o

    def _L1_attn_b_ref(x, W_act, W_val, W_rec):
        import jax, jax.numpy as jnp
        import numpy as np
        B, T, C = (4, 512, 256)
        Bx, Tx, Cx = x.shape
        shifted = jnp.concatenate([jnp.zeros_like(x[:, :1]), x[:, :-1]], axis=1)
        ct = jnp.concatenate([shifted, x], axis=-1)
        xv = jax.nn.sigmoid(jax.nn.relu(jnp.einsum('btk,ck->btc', ct, W_act)))
        z = xv.reshape(Bx, Tx, Cx // 2, 2)
        re, im = (z[..., 0], z[..., 1])
        mag = jnp.sqrt(re * re + im * im)
        m = jax.lax.cummax(mag, axis=1)
        re, im = (re / m, im / m)

        def cmul(a, b):
            ar, ai = a
            br, bi = b
            return (ar * br - ai * bi, ar * bi + ai * br)
        re_p, im_p = jax.lax.associative_scan(cmul, (re, im), axis=1)
        kv = jnp.stack([re_p, im_p], axis=-1).reshape(Bx, Tx, Cx)
        r = jax.nn.sigmoid(jax.nn.relu(jnp.einsum('btk,ck->btc', ct, W_rec)))
        return jnp.einsum('btk,ck->btc', kv, W_val) * r ** 4

    def _L1_ffn_ref(x, w_gate, w_up, w_down):
        import jax, jax.numpy as jnp
        import numpy as np

        def _sparsify_2to4(h):
            B, S, I = h.shape
            g = h.reshape(B, S, I // 4, 4)
            a = jnp.abs(g)
            _, idx = jax.lax.top_k(a, 2)
            pos = jnp.arange(4)
            mask = (pos == idx[..., 0:1]) | (pos == idx[..., 1:2])
            return (g * mask.astype(g.dtype)).reshape(B, S, I)
        h = jax.nn.silu(jnp.einsum('bsh,hi->bsi', x, w_gate)) * jnp.einsum('bsh,hi->bsi', x, w_up)
        h_sparse = _sparsify_2to4(h)
        return jnp.einsum('bsi,ih->bsh', h_sparse, w_down)
    x = L0_attn_a_x
    x = x + _L0_attn_a_ref(_layernorm(x, axis=-1), L0_attn_a_Wqkv, L0_attn_a_b_qkv, L0_attn_a_Wout, L0_attn_a_b_out)
    x = x + _L0_ffn_ref(_layernorm(x, axis=-1), L0_ffn_W_q, L0_ffn_keys, L0_ffn_down_embed, L0_ffn_up_embed, L0_ffn_gate_w, L0_ffn_up_w, L0_ffn_down_w)
    x = x + _L0_attn_b_ref(_layernorm(x, axis=-1))
    x = x + _L0_ffn_ref(_layernorm(x, axis=-1), L0_ffn_W_q, L0_ffn_keys, L0_ffn_down_embed, L0_ffn_up_embed, L0_ffn_gate_w, L0_ffn_up_w, L0_ffn_down_w)
    x = x + _L1_attn_a_ref(_layernorm(x, axis=-1), L1_attn_a_W_q, L1_attn_a_W_k, L1_attn_a_W_v, L1_attn_a_W_o)
    x = x + _L1_ffn_ref(_layernorm(x, axis=-1), L1_ffn_w_gate, L1_ffn_w_up, L1_ffn_w_down)
    x = x + _L1_attn_b_ref(_layernorm(x, axis=-1), L1_attn_b_W_act, L1_attn_b_W_val, L1_attn_b_W_rec)
    x = x + _L1_ffn_ref(_layernorm(x, axis=-1), L1_ffn_w_gate, L1_ffn_w_up, L1_ffn_w_down)
    return x

_drawn_inputs = setup_inputs


def setup_inputs(seed=0):
    import zlib

    import numpy as np

    out = dict(_drawn_inputs(seed))
    spreads = {'L0_attn_a_b_qkv': (0.0, 0.1), 'L0_attn_a_b_out': (0.0, 0.1)}
    factors = {'L0_ffn_W_q': 8.0,
     'L0_ffn_keys': 8.0,
     'L0_ffn_down_embed': 6.869,
     'L0_ffn_up_embed': 6.757,
     'L1_attn_a_W_q': 8.0,
     'L1_attn_a_W_k': 8.0,
     'L1_attn_a_W_v': 4.299,
     'L1_attn_a_W_o': 4.552,
     'L1_attn_b_W_act': 32.512,
     'L1_attn_b_W_val': 8.0,
     'L1_attn_b_W_rec': 22.344}
    for name, (base, spread) in spreads.items():
        noise = np.random.default_rng([zlib.crc32(name.encode()), seed]).standard_normal(out[name].shape)
        drawn = base * np.exp(spread * noise) if base else spread * noise
        out[name] = jnp.asarray(drawn.astype(out[name].dtype))
    for name, factor in factors.items():
        out[name] = (out[name] * factor).astype(out[name].dtype)
    return out
```

```python
from contextlib import ExitStack

import concourse.bass as bass
import numpy as np
from concourse import mybir

F32 = mybir.dt.float32
BF16 = mybir.dt.bfloat16
I32 = mybir.dt.int32
U32 = mybir.dt.uint32
ALU = mybir.AluOpType
ACT = mybir.ActivationFunctionType
AX = mybir.AxisListType.X

P = 128
B = 4
T = 512
NT = T // P
D = 256
DC = D // P
HEADS = 16
HD = D // HEADS
EPS = 1e-5
INTER = 1024
FC = INTER // P
EXPERTS = 512
EC = EXPERTS // P
NKEYS = 64
TOPK = 8
LOWKEYS = EXPERTS // NKEYS
BIG = 1e30
RSQRT_SEED = float(0x5F3759DF)


class Chain:

    def __init__(self, eng, sem, per):
        self.eng, self.sem, self.per = eng, sem, per

    def start(self, rnd):
        self.base, self.n = rnd * self.per, 0

    def do(self, ins):
        self.n += 1
        return ins.then_inc(self.sem, 1)

    def sync(self):
        self.eng.wait_ge(self.sem, self.base + self.n)

    def hold(self):
        self.sync()
        self.eng.sem_inc(self.sem, 1)
        self.n += 1

    def step(self, ins):
        self.do(ins)
        self.sync()

    def end(self):
        assert self.n == self.per, (self.n, self.per)


class Scope:

    def __init__(self, nc, name, stack):
        self.nc, self.name, self.stack = nc, name, stack

    def sb(self, name, shape, dt=F32):
        return self.stack.enter_context(self.nc.sbuf_tensor(f"{self.name}_{name}", shape, dt))

    def sem(self, name):
        return self.stack.enter_context(self.nc.semaphore(f"{self.name}_{name}"))


class NormBuffers:
    STEPS = 2 * NT + 1 + 3 + 9

    def __init__(self, s):
        self.stats = s.sb("stats", [P, NT, 6])
        self.mv = s.sb("mv", [P, NT, 2])
        self.var = s.sb("var", [P, NT])
        self.half = s.sb("half", [P, NT], I32)
        self.y = s.sb("rstd", [P, NT])
        self.t = s.sb("newton", [P, NT])


def norm_stats(dve, c, g, b, nb):
    x = g["x"]
    for t in range(NT):
        c.do(dve.bn_stats(nb.stats[:, t, :], x[:, 4 * b + t, :]))
    c.hold()
    for t in range(NT):
        c.do(dve.bn_aggr(nb.mv[:, t, :], nb.stats[:, t, :]))
    c.sync()
    c.step(dve.tensor_scalar(nb.var[:, :], nb.mv[:, :, 1], EPS, None, ALU.add))
    c.step(dve.tensor_scalar(nb.half[:, :], nb.var[:, :].bitcast(I32), 1, None, ALU.logical_shift_right))
    c.step(dve.tensor_scalar(nb.y[:, :].bitcast(I32), nb.half[:, :], -1.0, RSQRT_SEED, ALU.mult, ALU.add))
    for _ in range(3):
        c.step(dve.tensor_tensor(nb.t[:, :], nb.y[:, :], nb.y[:, :], ALU.mult))
        c.step(dve.scalar_tensor_tensor(nb.t[:, :], nb.t[:, :], -0.5, nb.var[:, :], ALU.mult, ALU.mult))
        c.step(dve.scalar_tensor_tensor(nb.y[:, :], nb.t[:, :], 1.5, nb.y[:, :], ALU.add, ALU.mult))


def norm_apply(dve, x, b, nb, xn):
    for t in range(NT):
        last = dve.tensor_scalar(xn[:, t, :], x[:, 4 * b + t, :], nb.mv[:, t, 0:1], nb.y[:, t:t + 1],
                                 ALU.subtract, ALU.mult)
    return last


def transpose_row(pe, ps, bank, xn, ident):
    for c in range(DC):
        for t in range(NT):
            last = pe.transpose(ps[:, bank + c, t * P:(t + 1) * P], xn[:, t, c * P:(c + 1) * P], ident[:, :])
    return last



def normalise_rows(nc, name, g, xT, queries=None):
    x, ps, ident = g["x"], g["ps"], g["ident"]
    with ExitStack() as stack:
        s = Scope(nc, name, stack)
        nb = NormBuffers(s)
        xn = s.sb("xn", [P, NT, D])
        dve_steps = s.sem("dve_steps")
        xn_ready, transposed, xt_ready = s.sem("xn_ready"), s.sem("transposed"), s.sem("xt_ready")
        if queries:
            wq, kb, scores = queries
            qT = s.sb("qT", [P, T])
            q_ready, qt_ready, r_ready, r_free = s.sem("q_ready"), s.sem("qt_ready"), s.sem("r_ready"), s.sem("r_free")
        block = stack.enter_context(nc.Block())

        @block.vector
        def _(dve):
            if queries:
                dve.sem_inc(r_free, 1)
            c = Chain(dve, dve_steps, NormBuffers.STEPS)
            with dve.Fori(0, B) as b:
                c.start(b)
                norm_stats(dve, c, g, b, nb)
                c.end()
                dve.wait_ge(transposed, b + 1)
                norm_apply(dve, x, b, nb, xn).then_inc(xn_ready, 1)
                if queries:
                    dve.wait_ge(r_ready, b + 1)
                    dve.tensor_copy(scores[:, bass.ds(4 * b, NT), :],
                                    ps[:, 3, :].rearrange("p (t k) -> p t k", t=NT)).then_inc(r_free, 1)

        @block.tensor
        def _(pe):
            pe.sem_inc(transposed, 1)
            pe.wait_ge(g["loaded"], g["loads"]["ident"])
            if queries:
                pe.wait_ge(g["loaded"], g["loads"]["router"])
            with pe.Fori(0, B) as b:
                pe.wait_ge(xn_ready, b + 1)
                pe.wait_ge(xt_ready, b + 1)
                transpose_row(pe, ps, 0, xn, ident).then_inc(transposed, 1)
                if queries:
                    pe.wait_ge(xt_ready, b + 2)
                    for c in range(DC):
                        last = pe.matmul(ps[:, 2, :], wq[:, c, :], xT[:, c, b, :], start=c == 0, stop=c == DC - 1)
                    last.then_inc(q_ready, 1)
                    pe.wait_ge(qt_ready, b + 1)
                    pe.wait_ge(r_free, b + 1)
                    for t in range(NT):
                        last = pe.matmul(ps[:, 3, t * P:(t + 1) * P], qT[:, t * P:(t + 1) * P], kb[:, b, :],
                                         start=True, stop=True)
                    last.then_inc(r_ready, 1)

        @block.scalar
        def _(act):
            act.sem_inc(xt_ready, 1)
            with act.Fori(0, B) as b:
                act.wait_ge(transposed, b + 2)
                act.activation(xT[:, :, b, :], ps[:, 0:DC, :], ACT.Copy).then_inc(xt_ready, 1)
                if queries:
                    act.wait_ge(q_ready, b + 1)
                    act.activation(qT[:, :], ps[:, 2, :], ACT.Copy).then_inc(qt_ready, 1)


def sparse_feed_forward(nc, name, g, w_gate, w_up, w_down):
    x, ps = g["x"], g["ps"]
    with ExitStack() as outer:
        so = Scope(nc, name, outer)
        xT = so.sb("xT", [P, DC, B, T])
        normalise_rows(nc, name + "n", g, xT)
        stack = outer.enter_context(ExitStack())
        s = Scope(nc, name + "m", stack)
        sg = s.sb("silu", [P, 2, T])
        h = s.sb("h", [P, FC, T])
        mag = s.sb("mag", [P, 2, 4, T])
        cmp_ = {ab: s.sb(f"ge{ab[0]}{ab[1]}", [P, T], BF16) for ab in
                [(0, 1), (0, 2), (0, 3), (1, 2), (1, 3), (2, 3)]}
        cnt = s.sb("count", [P, 4, T], BF16)
        gate_ready, up_ready = s.sem("gate_ready"), s.sem("up_ready")
        silu_done, prod_done, mag_done = s.sem("silu_done"), s.sem("prod_done"), s.sem("mag_done")
        sel_done, down_done, x_done = s.sem("sel_done"), s.sem("down_done"), s.sem("x_done")
        sel_steps = s.sem("sel_steps")
        block = stack.enter_context(nc.Block())


        @block.tensor
        def _(pe):
            pe.sem_inc(down_done, 2)
            pe.wait_ge(g["loaded"], g["loads"][g["w_key"]])

            def gate_up(b, half):
                for r in range(4):
                    j = 4 * half + r
                    n = FC * b + j
                    bank = 2 * (r % 2)
                    pe.wait_ge(silu_done, n + 1)
                    for c in range(DC):
                        last = pe.matmul(ps[:, bank, :], w_gate[:, c, j * P:(j + 1) * P], xT[:, c, b, :],
                                         start=c == 0, stop=c == DC - 1)
                    last.then_inc(gate_ready, 1)
                    pe.wait_ge(prod_done, n + 1)
                    for c in range(DC):
                        last = pe.matmul(ps[:, bank + 1, :], w_up[:, c, j * P:(j + 1) * P], xT[:, c, b, :],
                                         start=c == 0, stop=c == DC - 1)
                    last.then_inc(up_ready, 1)

            def down(b, half):
                pe.wait_ge(sel_done, 2 * b + half + 3)
                if half == 0:
                    pe.wait_ge(x_done, b + 1)
                for r in range(4):
                    j = 4 * half + r
                    for t in range(NT):
                        last = pe.matmul(ps[:, 4 + t // 2, (t % 2) * D:(t % 2 + 1) * D], h[:, j, t * P:(t + 1) * P],
                                         w_down[:, j, :], start=j == 0 and t % 2 == 0, stop=j == FC - 1,
                                         skip_group_check=True)
                last.then_inc(down_done, 1)

            gate_up(0, 0)
            with pe.Fori(0, B - 1) as b:
                gate_up(b, 1)
                down(b, 0)
                gate_up(b + 1, 0)
                down(b, 1)
            gate_up(B - 1, 1)
            down(B - 1, 0)
            down(B - 1, 1)

        @block.scalar
        def _(act):
            act.sem_inc(silu_done, 2)

            def half_chunks(b, half):
                m = 2 * b + half
                for r in range(4):
                    n = 4 * m + r
                    act.wait_ge(gate_ready, n + 1)
                    act.wait_ge(prod_done, n + 1)
                    act.activation(sg[:, r % 2, :], ps[:, 2 * (r % 2), :], ACT.Silu).then_inc(silu_done, 1)
                    act.wait_ge(prod_done, n + 3)
                    if r == 0:
                        act.wait_ge(sel_done, m + 1)
                    act.activation(mag[:, half, r, :], h[:, 4 * half + r, :], ACT.Abs).then_inc(mag_done, 1)

            with act.Fori(0, B) as b:
                half_chunks(b, 0)
                half_chunks(b, 1)

        @block.vector
        def _(dve):
            dve.sem_inc(prod_done, 2)
            dve.sem_inc(sel_done, 2)
            dve.sem_inc(x_done, 1)
            c = Chain(dve, sel_steps, 18)

            def product(b, half, r):
                m = 2 * b + half
                n = 4 * m + r
                dve.wait_ge(silu_done, n + 3)
                dve.wait_ge(up_ready, n + 1)
                if r == 0:
                    dve.wait_ge(down_done, m + 1)
                dve.tensor_tensor(h[:, 4 * half + r, :], sg[:, r % 2, :], ps[:, 2 * (r % 2) + 1, :],
                                  ALU.mult).then_inc(prod_done, 1)

            def select(b, half, part):
                m = 2 * b + half
                if part == 0:
                    c.start(m)
                    dve.wait_ge(mag_done, 4 * m + 4)
                    for (lo, hi), out in cmp_.items():
                        c.do(dve.tensor_tensor(out[:, :], mag[:, half, lo, :], mag[:, half, hi, :], ALU.is_ge))
                    c.sync()
                if part == 1:
                    g01, g02, g03, g12, g13, g23 = (cmp_[k][:, :] for k in cmp_)
                    for r, (a, e) in enumerate([(g01, g02), (g12, g13), (g02, g12), (g13, g23)]):
                        c.do(dve.tensor_tensor(cnt[:, r, :], a, e, ALU.add))
                    c.sync()
                    for r, (a, e, op) in enumerate([(cnt[:, 0, :], g03, ALU.add), (cnt[:, 1, :], g01, ALU.subtract),
                                                    (g23, cnt[:, 2, :], ALU.subtract), (cnt[:, 3, :], g03, ALU.add)]):
                        c.do(dve.tensor_tensor(cnt[:, r, :], a, e, op))
                    c.sync()
                if part == 2:
                    for r, (level, op) in enumerate([(1.5, ALU.is_ge), (0.5, ALU.is_ge), (-0.5, ALU.is_ge), (1.5, ALU.is_le)]):
                        hr = h[:, 4 * half + r, :]
                        c.do(dve.scalar_tensor_tensor(hr, cnt[:, r, :], level, hr, op, ALU.mult))
                    c.sync()
                    c.end()
                    dve.sem_inc(sel_done, 1)

            def add_to_x(b):
                dve.wait_ge(down_done, 2 * b + 4)
                for k in range(2):
                    xk = x[:, bass.ds(4 * b + 2 * k, 2), :]
                    last = dve.tensor_tensor(xk, xk, ps[:, 4 + k, :].rearrange("p (t d) -> p t d", t=2), ALU.add)
                last.then_inc(x_done, 1)

            for r in range(4):
                product(0, 0, r)
            with dve.Fori(0, B - 1) as b:
                for r in range(4):
                    product(b, 1, r)
                    if r < 3:
                        select(b, 0, r)
                for r in range(4):
                    product(b + 1, 0, r)
                    if r < 3:
                        select(b, 1, r)
                add_to_x(b)
            for r in range(4):
                product(B - 1, 1, r)
                if r < 3:
                    select(B - 1, 0, r)
            for r in range(3):
                select(B - 1, 1, r)
            add_to_x(B - 1)


def expert_feed_forward(nc, name, g, w_gate, w_up, w_down, wq, kb, w_de, w_ue):
    x, ps, ident = g["x"], g["ps"], g["ident"]
    with ExitStack() as outer:
        so = Scope(nc, name, outer)
        xT = so.sb("xT", [P, DC, B, T])
        scores = so.sb("scores", [P, B * NT, P])
        normalise_rows(nc, name + "n", g, xT, queries=(wq, kb, scores))
        stack = outer.enter_context(ExitStack())
        s = Scope(nc, name + "m", stack)
        NCH = FC + EC
        U = NT
        K8 = TOPK
        sg = s.sb("silu", [P, 2, T])
        h = s.sb("h", [P, NCH, T])
        sx, sy = s.sb("sx", [P, U, NKEYS]), s.sb("sy", [P, U, NKEYS])
        tx, ty, ts = s.sb("tx", [P, U, K8]), s.sb("ty", [P, U, K8]), s.sb("ts", [P, U, K8])
        ix, iy = s.sb("ix", [P, U, K8], U32), s.sb("iy", [P, U, K8], U32)
        ixf, iyf = s.sb("ixf", [P, U, K8]), s.sb("iyf", [P, U, K8])
        pair, rest = s.sb("pair", [P, U, K8, K8]), s.sb("rest", [P, U, K8, K8])
        pick = s.sb("pick", [P, U, K8, K8])
        arg = s.sb("arg", [P, U, LOWKEYS + NKEYS + K8 * K8])
        ex = s.sb("ex", [P, U, LOWKEYS + NKEYS + K8 * K8])
        picks, mass = s.sb("picks", [P, U, K8]), s.sb("mass", [P, U, K8])
        zsum, rz, hi = s.sb("zsum", [P, U]), s.sb("rz", [P, U]), s.sb("hi", [P, U])
        hot_x = s.sb("hot_x", [P, U, LOWKEYS, K8])
        need = s.sb("need", [P, U, LOWKEYS])
        hot_y = s.sb("hot_y", [P, U, NKEYS, K8])
        rank = s.sb("rank", [P, U, NKEYS])
        dense, wts = s.sb("dense", [P, U, LOWKEYS, NKEYS]), s.sb("wts", [P, U, LOWKEYS, NKEYS])
        iota, rankw = g["iota"], g["rankw"]
        gate_ready, up_ready = s.sem("gate_ready"), s.sem("up_ready")
        silu_done, prod_done = s.sem("silu_done"), s.sem("prod_done")
        down_done, x_done = s.sem("down_done"), s.sem("x_done")
        arg_ready, exp_done, w_ready = s.sem("arg_ready"), s.sem("exp_done"), s.sem("w_ready")
        route_steps = s.sem("route_steps")
        block = stack.enter_context(nc.Block())
        LO, HI = slice(0, LOWKEYS), slice(LOWKEYS, LOWKEYS + NKEYS)
        PR = slice(LOWKEYS + NKEYS, LOWKEYS + NKEYS + K8 * K8)


        @block.tensor
        def _(pe):
            pe.sem_inc(down_done, 2)
            pe.wait_ge(g["loaded"], g["loads"][g["w_key"]])

            def chunk(b, j):
                n = NCH * b + j
                bank = 2 * (j % 2)
                pe.wait_ge(silu_done, n + 1)
                for c in range(DC):
                    lhsT = w_gate[:, c, j * P:(j + 1) * P] if j < FC else w_de[:, c, (j - FC) * P:(j - FC + 1) * P]
                    last = pe.matmul(ps[:, bank, :], lhsT, xT[:, c, b, :], start=c == 0, stop=c == DC - 1)
                last.then_inc(gate_ready, 1)
                pe.wait_ge(prod_done, n + 1)
                if j < FC:
                    for c in range(DC):
                        last = pe.matmul(ps[:, bank + 1, :], w_up[:, c, j * P:(j + 1) * P], xT[:, c, b, :],
                                         start=c == 0, stop=c == DC - 1)
                else:
                    wt = wts[:, :, :, :].rearrange("p u i j -> p u (i j)")
                    for u in range(U):
                        last = pe.transpose(ps[:, bank + 1, u * P:(u + 1) * P], wt[:, u, (j - FC) * P:(j - FC + 1) * P],
                                            ident[:, :])
                last.then_inc(up_ready, 1)

            def down(b, group):
                js = range(FC) if group == 0 else range(FC, NCH)
                if group == 0:
                    pe.wait_ge(x_done, b + 1)
                for j in js:
                    pe.wait_ge(prod_done, NCH * b + j + 3)
                    for t in range(NT):
                        last = pe.matmul(ps[:, 4 + t // 2, (t % 2) * D:(t % 2 + 1) * D], h[:, j, t * P:(t + 1) * P],
                                         w_down[:, j, :] if j < FC else w_ue[:, j - FC, :],
                                         start=j == 0 and t % 2 == 0, stop=j == NCH - 1, skip_group_check=True)
                last.then_inc(down_done, 1)

            with pe.Fori(0, B) as b:
                for j in range(FC):
                    chunk(b, j)
                down(b, 0)
                pe.wait_ge(w_ready, b + 1)
                for j in range(FC, NCH):
                    chunk(b, j)
                down(b, 1)

        @block.scalar
        def _(act):
            act.sem_inc(silu_done, 2)
            with act.Fori(0, B) as b:
                for j in range(NCH):
                    n = NCH * b + j
                    act.wait_ge(gate_ready, n + 1)
                    act.wait_ge(prod_done, n + 1)
                    act.activation(sg[:, j % 2, :], ps[:, 2 * (j % 2), :], ACT.Silu).then_inc(silu_done, 1)
                    if j == 4:
                        act.wait_ge(arg_ready, b + 1)
                        act.activation(ex[:, :, :], arg[:, :, :], ACT.Exp).then_inc(exp_done, 1)

        @block.vector
        def _(dve):
            dve.sem_inc(prod_done, 2)
            dve.sem_inc(x_done, 1)
            c = Chain(dve, route_steps, 54)

            def product(b, j):
                n = NCH * b + j
                dve.wait_ge(silu_done, n + 3)
                dve.wait_ge(up_ready, n + 1)
                if j in (0, FC):
                    dve.wait_ge(down_done, 2 * b + j // FC + 1)
                if j < FC:
                    dve.tensor_tensor(h[:, j, :], sg[:, j % 2, :], ps[:, 2 * (j % 2) + 1, :],
                                      ALU.mult).then_inc(prod_done, 1)
                else:
                    ins = dve.tensor_tensor(h[:, j, :].rearrange("f (s p r) -> f s r p", s=2, r=2),
                                            sg[:, j % 2, :].rearrange("f (s p r) -> f s r p", s=2, r=2),
                                            ps[:, 2 * (j % 2) + 1, :].rearrange("f (s r p) -> f s r p", s=2, r=2),
                                            ALU.mult)
                    ins.then_inc(prod_done, 1)

            def wide(ap, shape, axis):
                return ap.unsqueeze(axis).broadcast_to(shape)

            def route(b, part):
                if part == 0:
                    c.start(b)
                    c.do(dve.tensor_copy(sx[:, :, :], scores[:, bass.ds(2 * b, 2), :].rearrange("p s (r k) -> p s r k", r=2)))
                    c.do(dve.tensor_copy(sy[:, :, :], scores[:, bass.ds(2 * b + 2 * NT, 2), :].rearrange("p s (r k) -> p s r k", r=2)))
                    c.hold()
                    for u in range(U):
                        c.do(dve.max(tx[:, u, :], sx[:, u, :]))
                        c.do(dve.max(ty[:, u, :], sy[:, u, :]))
                    c.sync()
                    c.do(dve.tensor_tensor(pair[:, :, :, :], wide(tx[:, :, :], [P, U, K8, K8], 3),
                                           wide(ty[:, :, :], [P, U, K8, K8], 2), ALU.add))
                if part == 1:
                    c.hold()
                    for u in range(U):
                        c.do(dve.max_index(ix[:, u, :], tx[:, u, :], sx[:, u, :]))
                        c.do(dve.max_index(iy[:, u, :], ty[:, u, :], sy[:, u, :]))
                    for u in range(U):
                        c.do(dve.max(ts[:, u, :], pair[:, u, :, :].rearrange("p a b -> p (a b)")))
                    c.hold()
                if part == 2:
                    for u in range(U):
                        c.do(dve.match_replace(rest[:, u, :, :].rearrange("p a b -> p (a b)"), ts[:, u, :],
                                               pair[:, u, :, :].rearrange("p a b -> p (a b)"), -3e38))
                    c.do(dve.tensor_tensor(arg[:, :, LO], sx[:, :, LO], tx[:, :, 0:1].broadcast_to([P, U, LOWKEYS]), ALU.subtract))
                    c.do(dve.tensor_tensor(arg[:, :, HI], sy[:, :, :], ty[:, :, 0:1].broadcast_to([P, U, NKEYS]), ALU.subtract))
                    c.do(dve.tensor_tensor(arg[:, :, PR], pair[:, :, :, :].rearrange("p u a b -> p u (a b)"),
                                           ts[:, :, 0:1].broadcast_to([P, U, K8 * K8]), ALU.subtract))
                    c.sync()
                    dve.sem_inc(arg_ready, 1)
                if part == 3:
                    c.do(dve.tensor_tensor(pick[:, :, :, :], rest[:, :, :, :], pair[:, :, :, :], ALU.is_lt))
                    c.do(dve.tensor_copy(ixf[:, :, :], ix[:, :, :]))
                    c.do(dve.tensor_copy(iyf[:, :, :], iy[:, :, :]))
                    c.sync()
                    c.do(dve.reduce_sum(picks[:, :, :], pick[:, :, :, :], AX))
                    c.do(dve.tensor_tensor(hot_x[:, :, :, :], wide(ixf[:, :, :], [P, U, LOWKEYS, K8], 2),
                                           iota[:, 0:LOWKEYS].unsqueeze(1).unsqueeze(3).broadcast_to([P, U, LOWKEYS, K8]),
                                           ALU.is_equal))
                    c.do(dve.tensor_tensor(hot_y[:, :, :, :], wide(iyf[:, :, :], [P, U, NKEYS, K8], 2),
                                           iota[:, :].unsqueeze(1).unsqueeze(3).broadcast_to([P, U, NKEYS, K8]),
                                           ALU.is_equal))
                    c.sync()
                if part == 4:
                    c.do(dve.tensor_tensor(hot_y[:, :, :, :].rearrange("p u j b -> p (u j) b"),
                                           hot_y[:, :, :, :].rearrange("p u j b -> p (u j) b"),
                                           rankw[:, :].unsqueeze(1).broadcast_to([P, U * NKEYS, K8]), ALU.mult))
                    c.do(dve.tensor_tensor(hot_x[:, :, :, :], hot_x[:, :, :, :], wide(picks[:, :, :], [P, U, LOWKEYS, K8], 2),
                                           ALU.mult))
                    c.sync()
                    c.do(dve.reduce_sum(rank[:, :, :], hot_y[:, :, :, :], AX))
                    c.do(dve.reduce_sum(need[:, :, :], hot_x[:, :, :, :], AX))
                    c.sync()
                if part == 5:
                    dve.wait_ge(exp_done, b + 1)
                    c.step(dve.tensor_tensor(rest[:, :, :, :].rearrange("p u a b -> p u (a b)"), ex[:, :, PR],
                                             pick[:, :, :, :].rearrange("p u a b -> p u (a b)"), ALU.mult))
                    c.step(dve.reduce_sum(mass[:, :, :], rest[:, :, :, :], AX))
                    c.step(dve.reduce_sum(zsum[:, :], mass[:, :, :], AX))
                    c.do(dve.reciprocal(rz[:, :], zsum[:, :]))
                    c.step(dve.scalar_tensor_tensor(mass[:, :, :], ixf[:, :, :], LOWKEYS - 0.5, mass[:, :, :], ALU.is_ge, ALU.mult))
                    c.do(dve.reduce_sum(hi[:, :], mass[:, :, :], AX))
                    c.step(dve.tensor_tensor(arg[:, :, LO], ex[:, :, LO], rz[:, :].unsqueeze(2).broadcast_to([P, U, LOWKEYS]), ALU.mult))
                    c.step(dve.tensor_tensor(hi[:, :], hi[:, :], rz[:, :], ALU.mult))
                if part == 6:
                    c.do(dve.tensor_tensor(dense[:, :, :, :], wide(rank[:, :, :], [P, U, LOWKEYS, NKEYS], 2),
                                           wide(need[:, :, :], [P, U, LOWKEYS, NKEYS], 3), ALU.add))
                    c.do(dve.tensor_tensor(wts[:, :, :, :], wide(ex[:, :, HI], [P, U, LOWKEYS, NKEYS], 2),
                                           wide(arg[:, :, LO], [P, U, LOWKEYS, NKEYS], 3), ALU.mult))
                    c.sync()
                if part == 7:
                    c.step(dve.scalar_tensor_tensor(wts[:, :, :, :], dense[:, :, :, :], K8 + 0.5, wts[:, :, :, :],
                                                    ALU.is_gt, ALU.mult))
                    lastw = wts[:, :, LOWKEYS - 1, NKEYS - 1]
                    dve.tensor_tensor(lastw, lastw, hi[:, :], ALU.add).then_inc(w_ready, 1)
                    c.end()

            with dve.Fori(0, B) as b:
                for j in range(NCH):
                    product(b, j)
                    if j < FC:
                        route(b, j)
                dve.wait_ge(down_done, 2 * b + 4)
                for k in range(2):
                    xk = x[:, bass.ds(4 * b + 2 * k, 2), :]
                    last = dve.tensor_tensor(xk, xk, ps[:, 4 + k, :].rearrange("p (t d) -> p t d", t=2), ALU.add)
                last.then_inc(x_done, 1)



PARTS = [0, 0, 1, 0, 1, 2]
K_PARTS = [0, 1, 0, 2, 1, 0]
STACK = 16 * len(PARTS)
SLOT = 32


def attention(nc, name, g, w, causal):
    x, ps, ident, identb = g["x"], g["ps"], g["ident"], g["identb"]
    KH = HEADS if causal else 4
    BIAS = 3 if causal else 0
    R1, R2 = STACK + BIAS, STACK + BIAS + 3
    NQ, NK = 2, KH * HD // P if causal else 1
    KP = min(P, KH * HD)
    NCH = NQ + NK
    HPC = P // HD
    with ExitStack() as stack:
        s = Scope(nc, name, stack)
        nb = NormBuffers(s)
        xn = s.sb("xn", [P, NT, D])
        xT = s.sb("xT", [P, DC, T])
        qk = s.sb("qk", [P, NCH, T])
        rot = s.sb("rot", [P, T]) if not causal else None
        part = s.sb("part", [P, 3, NCH, T], BF16)
        part_dram = nc.dram_tensor(name + "_parts", [NCH, P, 3, T], BF16).ap()
        qs = s.sb("qs", [P, 2, HEADS, T], BF16)
        ks = s.sb("ks", [P, 2, KH, T], BF16)
        negm = s.sb("negm", [P, NT, HEADS])
        mrest = s.sb("mrest", [HEADS, T])
        mpart = s.sb("mpart", [HEADS, 3, T], BF16)
        mpart_dram = nc.dram_tensor(name + "_maxima", [HEADS, 3, T], BF16).ap()
        va = s.sb("va", [P, NT, KH, SLOT])
        pr = s.sb("probs", [P, 8, T])
        ctxs = s.sb("ctxs", [P, T])
        rden = s.sb("rden", [P, T])
        ctxn = s.sb("ctxn", [P, 4, T])

        norm_steps, rot_steps, den_steps = s.sem("norm_steps"), s.sem("rot_steps"), s.sem("den_steps")
        m_steps, pool_steps = s.sem("m_steps"), s.sem("pool_steps")
        va_init, pool_free = s.sem("va_init"), s.sem("pool_free")
        xn_ready, xn_free, xt_ready = s.sem("xn_ready"), s.sem("xn_free"), s.sem("xt_ready")
        r1_ready, r1_free = s.sem("r1_ready"), s.sem("r1_free")
        qk_ready, parts_ready, consts_loaded = s.sem("qk_ready"), s.sem("parts_ready"), s.sem("consts_loaded")
        parts_stored, m_stored, sp_waits = s.sem("parts_stored"), s.sem("m_stored"), s.sem("sp_waits")
        stack_loaded, mpart_ready, m_loaded = s.sem("stack_loaded"), s.sem("mpart_ready"), s.sem("m_loaded")
        s_ready, exp_done, pv_done = s.sem("s_ready"), s.sem("exp_done"), s.sem("pv_done")
        ctx_out, den_ready, ctxn_done = s.sem("ctx_out"), s.sem("den_ready"), s.sem("ctxn_done")
        out_ready, x_done = s.sem("out_ready"), s.sem("x_done")
        block = stack.enter_context(nc.Block())

        PROJ = 2 if causal else 3
        ITEMS = 1 + PROJ + 32 + 2
        PAD = ITEMS % 2
        PER1 = ITEMS + PAD
        AT_SCORES, AT_MAX, AT_V = 1 + PROJ, ITEMS - 2, ITEMS - 1
        NDMA = 6 * (NQ + NK)
        CREDIT = 1
        STEPS2 = 4 * NT
        T_AT, PROJ_AT, SCORE_AT = 1, 2, 5

        def score_items(k):
            span = STEPS2 - SCORE_AT
            if k < SCORE_AT:
                return range(0)
            return range(32 * (k - SCORE_AT) // span, 32 * (k - SCORE_AT + 1) // span)

        def rounds(eng, body):
            body(0, None)
            with eng.Fori(1, B) as i:
                body(i, i - 1)
            body(None, B - 1)

        def bank1(pos):
            return 2 * (pos % 2)

        def width1(qt):
            return (qt + 1) * P if causal else T

        def width2(kt):
            return T - kt * P if causal else T

        @block.sync
        def _(sp):
            sp.sem_inc(stack_loaded, CREDIT)
            sp.sem_inc(m_loaded, CREDIT)
            for par in range(2):
                if causal:
                    sp.dma_start(ks[STACK:STACK + 3, par, :, :], w["bias_rows"]).then_inc(consts_loaded, 16)
                    sp.dma_start(qs[STACK:STACK + 3, par, :, :], w["one_rows"]).then_inc(consts_loaded, 16)
                sp.dma_start(ks[R1:R2, par, :, :], w["one_rows"][:, 0:KH, :]).then_inc(consts_loaded, 16)

            def hold(sem, value):
                sp.wait_ge(sem, value)
                sp.sem_inc(sp_waits, 1)

            def body(b1, b2):
                if b1 is None:
                    return
                hold(out_ready, b1 + 1)
                for ch in range(NCH):
                    is_q = ch < NQ
                    dst, c = (qs, ch) if is_q else (ks, ch - NQ)
                    hn = HPC if is_q or causal else KH
                    hold(parts_ready, NCH * b1 + ch + 1)
                    rows = hn * HD
                    sp.dma_start(part_dram[ch, 0:rows, :, :], part[0:rows, :, ch, :]).then_inc(parts_stored, 16)
                for ch in range(NCH):
                    is_q = ch < NQ
                    dst, c = (qs, ch) if is_q else (ks, ch - NQ)
                    hn = HPC if is_q or causal else KH
                    hold(parts_stored, 16 * (NCH * b1 + NCH))
                    for i, p in enumerate(PARTS if is_q else K_PARTS):
                        sp.dma_start(dst[16 * i:16 * i + 16, b1 % 2, HPC * c:HPC * c + hn, :],
                                     part_dram[ch, 0:hn * HD, p, :].rearrange("(h p) n -> p h n", p=HD)
                                     ).then_inc(stack_loaded, 16)
                hold(mpart_ready, b1 + 1)
                sp.dma_start(mpart_dram, mpart[:, :, :]).then_inc(m_stored, 16)
                hold(m_stored, 16 * (b1 + 1))
                sp.dma_start(qs[R1:R2, b1 % 2, :, :], mpart_dram.rearrange("h i n -> i h n")).then_inc(m_loaded, 16)

            rounds(sp, body)
            sp.wait_ge(m_loaded, 16 * B + CREDIT)

        @block.gpsimd
        def _(pool):
            pool.sem_inc(pool_free, 1)
            c = Chain(pool, pool_steps, 6 * NCH)
            with pool.Fori(0, B) as b:
                c.start(b)
                for ch in range(NCH):
                    p = P if ch < NQ else KP
                    f, hi_, mid, lo = qk[0:p, ch, :], *(part[0:p, i, ch, :] for i in range(3))
                    pool.wait_ge(qk_ready, NCH * b + ch + 1)
                    pool.wait_ge(stack_loaded, 16 * NDMA * b + CREDIT)
                    c.hold()
                    c.step(pool.tensor_copy(hi_, f))
                    c.do(pool.tensor_tensor(f, f, hi_, ALU.subtract))
                    c.hold()
                    c.step(pool.tensor_copy(mid, f))
                    c.step(pool.tensor_tensor(lo, f, mid, ALU.subtract))
                    pool.sem_inc(parts_ready, 1)
                c.end()
                pool.sem_inc(pool_free, 1)

        @block.tensor
        def _(pe):
            pe.sem_inc(xn_free, 1)
            pe.sem_inc(out_ready, 2)
            pe.sem_inc(pv_done, 2)
            pe.wait_ge(g["loaded"], g["loads"][w["key"]])

            def item(b1, pos):
                pe.wait_ge(r1_free, PER1 * b1 + pos + 1)

            def transposes(b1):
                pe.wait_ge(xn_ready, b1 + 1)
                item(b1, 0)
                last = transpose_row(pe, ps, bank1(0), xn, ident)
                last.then_inc(xn_free, 1)
                pe.wait_ge(xn_free, b1 + 2)
                pe.sem_inc(r1_ready, 1)

            def projections(b1):
                pe.wait_ge(xt_ready, b1 + 1)
                if causal:
                    groups = [[(w["wq"], 0, P), (w["wq"], P, P)], [(w["wk"], 0, P), (w["wk"], P, P)]]
                else:
                    groups = [[(w["wq"], 0, P), (w["wq2"], 0, P)], [(w["wq"], P, P), (w["wq2"], P, P)],
                              [(w["wk"], 0, KP), (w["wk2"], 0, KP)]]
                for n, group in enumerate(groups):
                    item(b1, 1 + n)
                    for k, (wt, f0, fn) in enumerate(group):
                        for c in range(DC):
                            last = pe.matmul(ps[0:fn, bank1(1 + n) + k, :], wt[:, c, f0:f0 + fn], xT[:, c, :],
                                             start=c == 0, stop=c == DC - 1)
                    last.then_inc(r1_ready, 1)

            def score_pair(b1, n):
                hp, qt = n // NT, n % NT
                pos = AT_SCORES + n
                item(b1, pos)
                for k in range(2):
                    hd = 2 * hp + k
                    out = ps[:, bank1(pos) + k, 0:width1(qt)]
                    last = pe.matmul(out, qs[0:R1, b1 % 2, hd, qt * P:(qt + 1) * P],
                                     ks[0:R1, b1 % 2, hd % KH, 0:width1(qt)], start=True, stop=True)
                    if causal:
                        last = pe.matmul(ps[:, bank1(pos) + k, qt * P:(qt + 1) * P], identb[:, :], w["mask_qk"][:, :],
                                         start=False, stop=True, skip_group_check=True)
                last.then_inc(r1_ready, 1)

            def maxima(b1):
                pe.wait_ge(r1_free, PER1 * b1 + AT_MAX + 2)
                for qt in range(NT):
                    last = pe.transpose(ps[0:HEADS, bank1(AT_MAX), qt * P:(qt + 1) * P], negm[:, qt, :], ident[:, :])
                last.then_inc(r1_ready, 1)

            def values(b1):
                item(b1, AT_V)
                n = KH * HD
                for t in range(NT):
                    col = t * n
                    for c in range(DC):
                        last = pe.matmul(ps[:, bank1(AT_V) + col // T, col % T:col % T + n], xT[:, c, t * P:(t + 1) * P],
                                         w["wv"][:, c, :], start=c == 0, stop=c == DC - 1)
                last.then_inc(r1_ready, 1 + PAD)

            def scores_t(b2, k):
                grp, kt = k // NT, k % NT
                for j in range(4):
                    hd, m = 4 * grp + j, 4 * k + j
                    pe.wait_ge(exp_done, 4 * STEPS2 * b2 + m + 1)
                    last = pe.matmul(ps[:, 4 + j % 2, 0:width2(kt)], ks[0:R2, b2 % 2, hd % KH, kt * P:(kt + 1) * P],
                                     qs[0:R2, b2 % 2, hd, T - width2(kt):T], start=True, stop=True)
                    if causal:
                        last = pe.matmul(ps[:, 4 + j % 2, 0:P], identb[:, :], w["mask_kq"][:, :],
                                         start=False, stop=True, skip_group_check=True)
                    last.then_inc(s_ready, 1)

            def context(b2, k):
                grp, kt = k // NT, k % NT
                pe.wait_ge(exp_done, 4 * STEPS2 * b2 + 4 * k + 4 + 2)
                if kt == 0:
                    pe.wait_ge(ctx_out, 4 * b2 + grp + 1)
                if k == 0:
                    pe.wait_ge(x_done, b2 + 1)
                    pe.wait_ge(r1_free, PER1 * (b2 + 1) + 2)
                for j in range(4):
                    hd = 4 * grp + j
                    last = pe.matmul(ps[SLOT * j:SLOT * (j + 1), 6, T - width2(kt):T], va[:, kt, hd % KH, :],
                                     pr[:, 4 * (k % 2) + j, 0:width2(kt)], start=kt == 0, stop=kt == NT - 1,
                                     skip_group_check=True)
                last.then_inc(pv_done, 1)

            def denominators(b2, grp):
                pe.wait_ge(ctx_out, 4 * b2 + grp + 2)
                pe.wait_ge(ctxn_done, 4 * b2 + grp + 1)
                pe.matmul(ps[:, 7, :], w["spread"][:, :], ctxs[:, :], start=True, stop=True).then_inc(den_ready, 1)

            def project_out(b2):
                pe.wait_ge(ctxn_done, 4 * b2 + 5)
                for t in range(NT):
                    for grp in range(4):
                        last = pe.matmul(ps[:, 7 - t // 2, (t % 2) * D:(t % 2 + 1) * D], ctxn[:, grp, t * P:(t + 1) * P],
                                         w["wo"][:, grp, :], start=grp == 0, stop=grp == 3)
                last.then_inc(out_ready, 1)

            def body(b1, b2):
                if b2 is not None:
                    pe.wait_ge(m_loaded, 16 * (b2 + 1) + CREDIT)
                for k in range(STEPS2):
                    if b1 is not None and k == T_AT:
                        transposes(b1)
                    if b1 is not None and k == PROJ_AT:
                        projections(b1)
                    if b2 is not None:
                        scores_t(b2, k)
                        if k >= 1:
                            context(b2, k - 1)
                        if k >= NT and k % NT == 1:
                            denominators(b2, k // NT - 1)
                    if b1 is not None:
                        if k == SCORE_AT:
                            pe.wait_ge(stack_loaded, 16 * NDMA * (b1 + 1) + CREDIT)
                        for n in score_items(k):
                            score_pair(b1, n)
                if b1 is not None:
                    maxima(b1)
                if b2 is not None:
                    context(b2, STEPS2 - 1)
                    denominators(b2, 3)
                    project_out(b2)
                if b1 is not None:
                    values(b1)

            pe.wait_ge(consts_loaded, (96 if causal else 32))
            rounds(pe, body)

        @block.scalar
        def _(act):
            act.sem_inc(exp_done, 2)
            act.sem_inc(ctx_out, 1)

            def copy_context(b2, grp):
                act.wait_ge(pv_done, 4 * (4 * b2 + grp) + 4 + 2)
                act.wait_ge(ctxn_done, 4 * b2 + grp + 1)
                act.activation(ctxs[:, :], ps[:, 6, :], ACT.Copy).then_inc(ctx_out, 1)

            with act.Fori(0, B) as b2:
                for k in range(STEPS2):
                    act.wait_ge(pv_done, STEPS2 * b2 + k + 1)
                    for j in range(4):
                        act.wait_ge(s_ready, 4 * (STEPS2 * b2 + k) + j + 1)
                        act.activation(pr[:, 4 * (k % 2) + j, 0:width2(k % NT)], ps[:, 4 + j % 2, 0:width2(k % NT)],
                                       ACT.Exp, scale=HD ** -0.5).then_inc(exp_done, 1)
                    if k >= NT and k % NT == 0:
                        copy_context(b2, k // NT - 1)
                copy_context(b2, 3)

        @block.vector
        def _(dve):
            dve.sem_inc(r1_free, 2)
            dve.sem_inc(ctxn_done, 1)
            dve.sem_inc(x_done, 1)
            dve.memset(va[:, :, :, HD:SLOT], 0.0).then_inc(va_init, 1)
            dve.wait_ge(va_init, 1)
            dve.memset(va[:, :, :, HD:HD + 1], 1.0).then_inc(va_init, 1)
            dve.wait_ge(va_init, 2)
            dve.wait_ge(g["loaded"], g["loads"][w["key"]])
            cn = Chain(dve, norm_steps, NormBuffers.STEPS)
            cr = Chain(dve, rot_steps, 9)
            cden = Chain(dve, den_steps, 1)
            cm = Chain(dve, m_steps, 4)

            def take(b1, pos):
                dve.wait_ge(r1_ready, PER1 * b1 + pos + 1)

            def transposed(b1):
                take(b1, 0)
                dve.tensor_copy(xT[:, :, :], ps[:, bank1(0):bank1(0) + 2, :]).then_inc(xt_ready, 1)
                dve.wait_ge(xt_ready, b1 + 1)
                dve.sem_inc(r1_free, 1)

            def projected(b1):
                dve.wait_ge(pool_free, b1 + 1)
                if causal:
                    for n in range(2):
                        take(b1, 1 + n)
                        for k in range(2):
                            last = dve.tensor_scalar(qk[:, 2 * n + k, :], ps[:, bank1(1 + n) + k, :],
                                                     w["bqk"][:, 2 * n + k:2 * n + k + 1], None, ALU.add)
                            last.then_inc(qk_ready, 1)
                        dve.wait_ge(qk_ready, NCH * b1 + 2 * n + 2)
                        dve.sem_inc(r1_free, 1)
                else:
                    cr.start(b1)
                    for n in range(3):
                        take(b1, 1 + n)
                        p = P if n < NQ else KP
                        q = qk[0:p, n, :]
                        cr.do(dve.tensor_tensor(q, ps[0:p, bank1(1 + n), :], w["cos"][0:p, :], ALU.mult))
                        cr.step(dve.tensor_tensor(rot[0:p, :], ps[0:p, bank1(1 + n) + 1, :], w["sin"][0:p, :], ALU.mult))
                        dve.sem_inc(r1_free, 1)
                        cr.step(dve.tensor_tensor(q, q, rot[0:p, :], ALU.add))
                        dve.sem_inc(qk_ready, 1)
                    cr.end()

            def row_max(b1, n):
                hp, qt = n // NT, n % NT
                pos = AT_SCORES + n
                take(b1, pos)
                dve.tensor_reduce(negm[:, qt, 2 * hp:2 * hp + 2], ps[:, bank1(pos):bank1(pos) + 2, 0:width1(qt)],
                                  AX, ALU.max, negate=True).then_inc(r1_free, 1)

            def max_rows(b1):
                take(b1, AT_MAX)
                dve.wait_ge(m_loaded, 16 * b1 + CREDIT)
                cm.start(b1)
                m = ps[0:HEADS, bank1(AT_MAX), :]
                cm.step(dve.tensor_copy(mpart[:, 0, :], m))
                cm.step(dve.tensor_tensor(mrest[:, :], m, mpart[:, 0, :], ALU.subtract))
                dve.sem_inc(r1_free, 1)
                cm.step(dve.tensor_copy(mpart[:, 1, :], mrest[:, :]))
                cm.step(dve.tensor_tensor(mpart[:, 2, :], mrest[:, :], mpart[:, 1, :], ALU.subtract))
                cm.end()
                dve.sem_inc(mpart_ready, 1)

            def values(b1):
                take(b1, AT_V)
                n = KH * HD
                src = ps[:, bank1(AT_V):bank1(AT_V) + (2 if causal else 1), :].rearrange("p b n -> p (b n)")[:, 0:NT * n] \
                    .rearrange("p (t h d) -> p t h d", t=NT, h=KH)
                if causal:
                    for t in range(NT):
                        last = dve.tensor_tensor(va[:, t, :, 0:HD], src[:, t, :, :],
                                                 w["bv"][:, :].rearrange("p (h d) -> p h d", h=KH), ALU.add)
                else:
                    last = dve.tensor_copy(va[:, :, :, 0:HD], src)
                last.then_inc(r1_free, 1 + PAD)

            def normalised(b2, grp):
                dve.wait_ge(den_ready, 4 * b2 + grp + 1)
                cden.start(4 * b2 + grp)
                cden.step(dve.reciprocal(rden[:, :], ps[:, 7, :]))
                dve.tensor_tensor(ctxn[:, grp, :], ctxs[:, :], rden[:, :], ALU.mult).then_inc(ctxn_done, 1)

            def add_to_x(b2):
                dve.wait_ge(out_ready, b2 + 3)
                for k in range(2):
                    xk = x[:, bass.ds(4 * b2 + 2 * k, 2), :]
                    last = dve.tensor_tensor(xk, xk, ps[:, 7 - k, :].rearrange("p (t d) -> p t d", t=2), ALU.add)
                last.then_inc(x_done, 1)

            def body(b1, b2):
                if b1 is not None:
                    cn.start(b1)
                    norm_stats(dve, cn, g, b1, nb)
                    cn.end()
                    dve.wait_ge(xn_free, b1 + 1)
                    norm_apply(dve, x, b1, nb, xn).then_inc(xn_ready, 1)
                for k in range(STEPS2):
                    if b1 is not None and k == T_AT:
                        transposed(b1)
                    if b1 is not None and k == PROJ_AT:
                        projected(b1)
                    if b2 is not None and k >= NT and k % NT == 1:
                        normalised(b2, k // NT - 1)
                    if b1 is not None:
                        for n in score_items(k):
                            row_max(b1, n)
                if b1 is not None:
                    max_rows(b1)
                if b2 is not None:
                    normalised(b2, 3)
                    add_to_x(b2)
                if b1 is not None:
                    values(b1)

            rounds(dve, body)



def feature_attention(nc, name, g):
    x, ps, ident = g["x"], g["ps"], g["ident"]
    with ExitStack() as stack:
        s = Scope(nc, name, stack)
        nb = NormBuffers(s)
        xn = s.sb("xn", [P, NT, D])
        xT = s.sb("xT", [P, DC, T])
        negm = s.sb("negm", [P, DC])
        pr = s.sb("probs", [P, DC, D])
        den, rden = s.sb("den", [P, DC]), s.sb("rden", [P, DC])
        attT = s.sb("attT", [P, DC, D])
        norm_steps, soft_steps = s.sem("norm_steps"), s.sem("soft_steps")
        xn_ready, e_ready, tr_ready, xt_ready = s.sem("xn_ready"), s.sem("e_ready"), s.sem("tr_ready"), s.sem("xt_ready")
        max_ready, exp_done, att_ready, at_ready = s.sem("max_ready"), s.sem("exp_done"), s.sem("att_ready"), s.sem("at_ready")
        attt_ready, out_ready, x_done = s.sem("attt_ready"), s.sem("out_ready"), s.sem("x_done")
        block = stack.enter_context(nc.Block())


        @block.tensor
        def _(pe):
            pe.wait_ge(g["loaded"], g["loads"]["ident"])
            with pe.Fori(0, B) as b:
                pe.wait_ge(xn_ready, b + 1)
                for i in range(DC):
                    for t in range(NT):
                        last = pe.matmul(ps[:, 0, i * D:(i + 1) * D], xn[:, t, i * P:(i + 1) * P], xn[:, t, :],
                                         start=t == 0, stop=t == NT - 1)
                last.then_inc(e_ready, 1)
                transpose_row(pe, ps, 1, xn, ident).then_inc(tr_ready, 1)
                pe.wait_ge(att_ready, b + 1)
                for j in range(DC):
                    for i in range(DC):
                        last = pe.transpose(ps[:, 3, j * D + i * P:j * D + (i + 1) * P], pr[:, i, j * P:(j + 1) * P],
                                            ident[:, :])
                last.then_inc(at_ready, 1)
                pe.wait_ge(xt_ready, b + 1)
                pe.wait_ge(attt_ready, b + 1)
                pe.wait_ge(x_done, b + 1)
                for t in range(NT):
                    for j in range(DC):
                        last = pe.matmul(ps[:, 4 + t // 2, (t % 2) * D:(t % 2 + 1) * D], xT[:, j, t * P:(t + 1) * P],
                                         attT[:, j, :], start=j == 0, stop=j == DC - 1)
                last.then_inc(out_ready, 1)

        @block.scalar
        def _(act):
            with act.Fori(0, B) as b:
                act.wait_ge(tr_ready, b + 1)
                act.activation(xT[:, :, :], ps[:, 1:3, :], ACT.Copy).then_inc(xt_ready, 1)
                act.wait_ge(max_ready, b + 1)
                for i in range(DC):
                    act.activation(pr[:, i, :], ps[:, 0, i * D:(i + 1) * D], ACT.Exp, bias=negm[:, i:i + 1],
                                   accum_out=den[:, i:i + 1]).then_inc(exp_done, 1)
                act.wait_ge(at_ready, b + 1)
                act.activation(attT[:, :, :], ps[:, 3, :].rearrange("p (j i) -> p j i", j=DC), ACT.Copy).then_inc(attt_ready, 1)

        @block.vector
        def _(dve):
            dve.sem_inc(x_done, 1)
            cn = Chain(dve, norm_steps, NormBuffers.STEPS)
            cs = Chain(dve, soft_steps, 1)
            with dve.Fori(0, B) as b:
                cn.start(b)
                norm_stats(dve, cn, g, b, nb)
                cn.end()
                norm_apply(dve, x, b, nb, xn).then_inc(xn_ready, 1)
                dve.wait_ge(e_ready, b + 1)
                dve.tensor_reduce(negm[:, :], ps[:, 0, :].rearrange("p (i j) -> p i j", i=DC), AX, ALU.max,
                                  negate=True).then_inc(max_ready, 1)
                dve.wait_ge(exp_done, 2 * b + 2)
                cs.start(b)
                cs.step(dve.reciprocal(rden[:, :], den[:, :]))
                for i in range(DC):
                    last = dve.tensor_scalar(pr[:, i, :], pr[:, i, :], rden[:, i:i + 1], None, ALU.mult)
                last.then_inc(att_ready, 1)
                dve.wait_ge(out_ready, b + 1)
                for k in range(2):
                    xk = x[:, bass.ds(4 * b + 2 * k, 2), :]
                    last = dve.tensor_tensor(xk, xk, ps[:, 4 + k, :].rearrange("p (t d) -> p t d", t=2), ALU.add)
                last.then_inc(x_done, 1)



def gated_scan(nc, name, g, w_act, w_val, w_rec, key):
    x, ps, ident = g["x"], g["ps"], g["ident"]
    with ExitStack() as outer:
        so = Scope(nc, name, outer)
        zz = so.sb("z", [P, 2, B, T])
        r4 = so.sb("r4", [P, B, NT * D])
        kv = so.sb("kv", [P, 2, T])
        with ExitStack() as stack:
            s = Scope(nc, name + "g", stack)
            nb = NormBuffers(s)
            xn = s.sb("xn", [P, NT, D])
            xT = s.sb("xT", [P, DC, T + 1])
            z = s.sb("zrow", [P, 2, T])
            sq = s.sb("sq", [P, 2, T])
            mag, peak, rpeak = s.sb("mag", [P, T]), s.sb("peak", [P, T]), s.sb("rpeak", [P, T])
            rr = s.sb("rr", [P, NT * D])
            norm_steps, z_steps = s.sem("norm_steps"), s.sem("z_steps")
            zero_done = s.sem("zero_done")
            xn_ready, transposed, xt_ready = s.sem("xn_ready"), s.sem("transposed"), s.sem("xt_ready")
            act_ready, rec_ready, sig_done = s.sem("act_ready"), s.sem("rec_ready"), s.sem("sig_done")
            sq_ready, mag_done, z_done = s.sem("sq_ready"), s.sem("mag_done"), s.sem("z_done")
            block = stack.enter_context(nc.Block())


            @block.tensor
            def _(pe):
                pe.wait_ge(g["loaded"], g["loads"][key])
                pe.wait_ge(zero_done, 1)
                with pe.Fori(0, B) as b:
                    pe.wait_ge(xn_ready, b + 1)
                    transpose_row(pe, ps, 0, xn, ident).then_inc(transposed, 1)
                    pe.wait_ge(xt_ready, b + 1)
                    for part in range(2):
                        for k in range(2 * DC):
                            shift = k // DC
                            last = pe.matmul(ps[:, 2 + part, :], w_act[:, k, part * P:(part + 1) * P],
                                             xT[:, k % DC, shift:shift + T], start=k == 0, stop=k == 2 * DC - 1)
                    last.then_inc(act_ready, 1)
                    for t in range(NT):
                        for k in range(2 * DC):
                            c0 = t * P + k // DC
                            last = pe.matmul(ps[:, 4 + t // 2, (t % 2) * D:(t % 2 + 1) * D], xT[:, k % DC, c0:c0 + P],
                                             w_rec[:, k, :], start=k == 0, stop=k == 2 * DC - 1)
                    last.then_inc(rec_ready, 1)

            @block.scalar
            def _(act):
                with act.Fori(0, B) as b:
                    act.wait_ge(transposed, b + 1)
                    act.activation(xT[:, :, 1:T + 1], ps[:, 0:DC, :], ACT.Copy).then_inc(xt_ready, 1)
                    act.wait_ge(act_ready, b + 1)
                    act.activation(z[:, :, :], ps[:, 2:4, :], ACT.Sigmoid).then_inc(sig_done, 1)
                    act.wait_ge(rec_ready, b + 1)
                    act.activation(rr[:, :], ps[:, 4:6, :].rearrange("p b n -> p (b n)"), ACT.Sigmoid).then_inc(sig_done, 1)
                    act.wait_ge(sq_ready, b + 1)
                    act.activation(mag[:, :], sq[:, 0, :], ACT.Sqrt).then_inc(mag_done, 1)

            @block.vector
            def _(dve):
                dve.memset(xT[:, :, 0:1], 0.0).then_inc(zero_done, 1)
                cn = Chain(dve, norm_steps, NormBuffers.STEPS)
                cz = Chain(dve, z_steps, 7)
                with dve.Fori(0, B) as b:
                    cn.start(b)
                    norm_stats(dve, cn, g, b, nb)
                    cn.end()
                    norm_apply(dve, x, b, nb, xn).then_inc(xn_ready, 1)
                    dve.wait_ge(sig_done, 2 * b + 1)
                    cz.start(b)
                    cz.step(dve.tensor_scalar(z[:, :, :], z[:, :, :], 0.5, None, ALU.max))
                    cz.step(dve.tensor_tensor(sq[:, :, :], z[:, :, :], z[:, :, :], ALU.mult))
                    dve.tensor_tensor(sq[:, 0, :], sq[:, 0, :], sq[:, 1, :], ALU.add).then_inc(sq_ready, 1)
                    dve.wait_ge(sig_done, 2 * b + 2)
                    cz.step(dve.tensor_scalar(rr[:, :], rr[:, :], 0.5, None, ALU.max))
                    cz.step(dve.tensor_tensor(rr[:, :], rr[:, :], rr[:, :], ALU.mult))
                    cz.do(dve.tensor_tensor(r4[:, b, :], rr[:, :], rr[:, :], ALU.mult))
                    dve.wait_ge(mag_done, b + 1)
                    cz.step(dve.tensor_tensor_scan(peak[:, :], mag[:, :], mag[:, :], 0.0, ALU.max, ALU.max))
                    cz.step(dve.reciprocal(rpeak[:, :], peak[:, :]))
                    cz.end()
                    dve.tensor_tensor(zz[:, :, b, :], z[:, :, :], rpeak[:, :].unsqueeze(1).broadcast_to([P, 2, T]),
                                      ALU.mult).then_inc(z_done, 1)
                    dve.wait_ge(z_done, b + 1)

        with ExitStack() as stack:
            s = Scope(nc, name + "s", stack)
            S1, S2 = 8, 8
            S3 = T // (S1 * S2)
            tmp = [s.sb(f"t{i}", [P, B * T]) for i in range(4)]
            scan_steps = s.sem("scan_steps")
            prefix_done, kv_ready, out_ready, x_done = s.sem("prefix_done"), s.sem("kv_ready"), s.sem("out_ready"), s.sem("x_done")
            out_steps = s.sem("out_steps")
            prod = s.sb("prod", [P, NT * D])
            block = stack.enter_context(nc.Block())

            @block.vector
            def _(dve):
                c = Chain(dve, scan_steps, 0)
                c.start(0)

                def multiply(part, carry, shape):
                    n = int(np.prod(shape))
                    t = [a[:, 0:n] for a in tmp]
                    if len(shape) == 2:
                        t = [a.rearrange("p (a b) -> p a b", a=shape[0]) for a in t]
                    if len(shape) == 3:
                        t = [a.rearrange("p (a b c) -> p a b c", a=shape[0], b=shape[1]) for a in t]
                    for k, (i, j) in enumerate([(0, 0), (1, 1), (0, 1), (1, 0)]):
                        c.do(dve.tensor_tensor(t[k], carry(i), part(j), ALU.mult))
                    c.sync()
                    c.do(dve.tensor_tensor(part(0), t[0], t[1], ALU.subtract))
                    c.do(dve.tensor_tensor(part(1), t[2], t[3], ALU.add))
                    c.sync()

                seg = [zz[:, k, :, :].rearrange("p b (n s) -> p (b n) s", s=S1) for k in range(2)]
                for i in range(1, S1):
                    multiply(lambda k: seg[k][:, :, i], lambda k: seg[k][:, :, i - 1], (B * T // S1,))
                tot = [zz[:, k, :, :].rearrange("p b (m q s) -> p (b m) q s", s=S1, q=S2)[:, :, :, S1 - 1] for k in range(2)]
                for i in range(1, S2):
                    multiply(lambda k: tot[k][:, :, i], lambda k: tot[k][:, :, i - 1], (B * S3,))
                grp = [zz[:, k, :, :].rearrange("p b (m r) -> p b m r", m=S3)[:, :, :, S1 * S2 - 1] for k in range(2)]
                for i in range(1, S3):
                    multiply(lambda k: grp[k][:, :, i], lambda k: grp[k][:, :, i - 1], (B,))
                tot4 = [zz[:, k, :, :].rearrange("p b (m q s) -> p b m q s", s=S1, q=S2)[:, :, :, :, S1 - 1] for k in range(2)]
                multiply(lambda k: tot4[k][:, :, 1:S3, 0:S2 - 1],
                         lambda k: grp[k][:, :, 0:S3 - 1].unsqueeze(3).broadcast_to([P, B, S3 - 1, S2 - 1]),
                         (B, S3 - 1, S2 - 1))
                seg4 = [zz[:, k, :, :].rearrange("p b (n s) -> p b n s", s=S1) for k in range(2)]
                NS = T // S1
                multiply(lambda k: seg4[k][:, :, 1:NS, 0:S1 - 1],
                         lambda k: seg4[k][:, :, 0:NS - 1, S1 - 1:S1].broadcast_to([P, B, NS - 1, S1 - 1]),
                         (B, NS - 1, S1 - 1))
                dve.sem_inc(prefix_done, 1)
                dve.sem_inc(x_done, 1)
                co = Chain(dve, out_steps, 1)
                with dve.Fori(0, B) as b:
                    dve.wait_ge(out_ready, b + 1)
                    co.start(b)
                    co.step(dve.tensor_tensor(prod[:, :], ps[:, 0:2, :].rearrange("p b n -> p (b n)"), r4[:, b, :], ALU.mult))
                    xb = x[:, bass.ds(4 * b, NT), :]
                    dve.tensor_tensor(xb, xb, prod[:, :].rearrange("p (t d) -> p t d", t=NT), ALU.add).then_inc(x_done, 1)

            @block.scalar
            def _(act):
                act.wait_ge(prefix_done, 1)
                with act.Fori(0, B) as b:
                    act.wait_ge(x_done, b + 1)
                    act.activation(kv[:, :, :], zz[:, :, b, :], ACT.Copy).then_inc(kv_ready, 1)

            @block.tensor
            def _(pe):
                with pe.Fori(0, B) as b:
                    pe.wait_ge(kv_ready, b + 1)
                    for t in range(NT):
                        for k in range(2):
                            last = pe.matmul(ps[:, t // 2, (t % 2) * D:(t % 2 + 1) * D], kv[:, k, t * P:(t + 1) * P],
                                             w_val[:, k, :], start=k == 0, stop=k == 1)
                    last.then_inc(out_ready, 1)



def stages(nc, a, out):
    with ExitStack() as stack:
        def place(names, into):
            return {n: into.enter_context(nc.sbuf_tensor("sb_" + n, list(a[n].shape), a[n].dtype)) for n in names}

        x = stack.enter_context(nc.sbuf_tensor("x", [P, B * NT, D], F32))
        ps = stack.enter_context(nc.psum_tensor("ps", [P, 8, T], F32))
        loaded = stack.enter_context(nc.semaphore("loaded"))
        stored = stack.enter_context(nc.semaphore("stored"))
        common = ["ident", "identb", "spread", "iota", "rankw"]
        att0 = ["a0_wq", "a0_wk", "a0_bqk", "a0_wv", "a0_bv", "a0_wo", "mask_qk", "mask_kq"]
        router = ["f0_wq", "f0_kb"]
        ffn0 = ["f0_gate", "f0_up", "f0_down", "f0_de", "f0_ue"]
        att1 = ["a1_wq", "a1_wq2", "a1_wk", "a1_wk2", "a1_wv", "a1_wo", "cos", "sin"]
        ffn1 = ["f1_gate", "f1_up", "f1_down"]
        scan = ["s_act", "s_rec", "s_val"]

        sb, loads, issued = {}, {}, [0]
        sb.update(place(common, stack))

        def load(sp, names, key):
            for n in names:
                sp.dma_start(sb[n][:], a[n]).then_inc(loaded, 16)
            issued[0] += 16 * len(names)
            loads[key] = issued[0]

        g = dict(x=x, ps=ps, loaded=loaded, loads=loads, ident=sb["ident"], identb=sb["identb"],
                 iota=sb["iota"], rankw=sb["rankw"])
        early = stack.enter_context(ExitStack())
        sb.update(place(router + ffn0, early))
        with ExitStack() as first:
            sb.update(place(att0, first))
            with nc.Block() as block:
                @block.sync
                def _(sp):
                    sp.dma_start(x[:, :, :], a["x"]).then_inc(loaded, 16)
                    issued[0] += 16
                    loads["x"] = issued[0]
                    load(sp, common + att0, "att0")
                    loads["ident"] = issued[0]
                    sp.wait_ge(loaded, issued[0])
                    load(sp, router + ffn0, "ffn0")
                    loads["router"] = issued[0]
            w = {n[3:]: sb[n] for n in att0 if n.startswith("a0_")}
            w.update(spread=sb["spread"], mask_qk=sb["mask_qk"], mask_kq=sb["mask_kq"],
                     bias_rows=a["bias_rows"], one_rows=a["one_rows"], key="att0")
            attention(nc, "attn0", g, w, causal=True)

        g["w_key"] = "ffn0"
        experts = [sb[n] for n in ("f0_gate", "f0_up", "f0_down", "f0_wq", "f0_kb", "f0_de", "f0_ue")]
        expert_feed_forward(nc, "moe0", g, *experts)
        feature_attention(nc, "feat", g)
        expert_feed_forward(nc, "moe1", g, *experts)
        early.close()

        late = stack.enter_context(ExitStack())
        sb.update(place(att1 + ffn1 + scan, late))
        with nc.Block() as block:
            @block.sync
            def _(sp):
                load(sp, att1, "att1")
                sp.wait_ge(loaded, issued[0])
                load(sp, ffn1, "ffn1")
                load(sp, scan, "scan")
        w = {n[3:]: sb[n] for n in att1 if n.startswith("a1_")}
        w.update(spread=sb["spread"], cos=sb["cos"], sin=sb["sin"], one_rows=a["one_rows"], key="att1")
        attention(nc, "attn1", g, w, causal=False)
        g["w_key"] = "ffn1"
        loads["ffn1"] = loads["scan"]
        sparse_feed_forward(nc, "mlp0", g, sb["f1_gate"], sb["f1_up"], sb["f1_down"])
        gated_scan(nc, "scan", g, sb["s_act"], sb["s_val"], sb["s_rec"], "scan")
        sparse_feed_forward(nc, "mlp1", g, sb["f1_gate"], sb["f1_up"], sb["f1_down"])
        with nc.Block() as block:
            @block.sync
            def _(sp):
                sp.dma_start(out, x[:, :, :]).then_inc(stored, 16)
                sp.wait_ge(stored, 16)


def bf16_bits(v):
    bits = v.astype(np.float32).view(np.uint32)
    bits = (bits + 0x7FFF + ((bits >> 16) & 1)) & np.uint32(0xFFFF0000)
    return (bits >> 16).astype(np.uint16), v - bits.view(np.float32)


def bf16_parts(v):
    got = []
    for _ in range(3):
        bits, v = bf16_bits(v)
        got.append(bits)
    return np.stack(got)


def shape_constants():
    slopes = 1.0 / 2.0 ** (np.arange(1, HEADS + 1, dtype=np.float32) * np.float32(8.0 / HEADS))
    bias = (np.arange(1 - T, 1, dtype=np.float32)[None, :] * slopes[:, None]).astype(np.float32)
    upper = np.triu(np.full((P, P), -BIG, np.float32), 1)
    spread = np.zeros((P, P), np.float32)
    for j in range(P // SLOT):
        spread[SLOT * j + HD, SLOT * j:SLOT * (j + 1)] = 1
    freqs = (1.0 / 10000.0 ** (np.arange(HD // 2, dtype=np.float32) / (HD // 2))).astype(np.float32)
    angles = (np.arange(T, dtype=np.float32)[:, None] * freqs).astype(np.float64)
    i = (np.arange(P) % HD) // 2
    sign = np.where(np.arange(P) % 2 == 0, -1.0, 1.0)
    return {
        "ident": np.eye(P, dtype=np.float32), "identb": bf16_bits(np.eye(P, dtype=np.float32))[0],
        "mask_qk": bf16_bits(upper)[0], "mask_kq": bf16_bits(np.ascontiguousarray(upper.T))[0],
        "bias_rows": bf16_parts(np.float32(HD ** 0.5) * bias), "one_rows": bf16_bits(np.ones((3, HEADS, T), np.float32))[0],
        "spread": spread,
        "iota": np.tile(np.arange(NKEYS, dtype=np.float32), (P, 1)),
        "rankw": np.tile(TOPK - np.arange(TOPK, dtype=np.float32), (P, 1)),
        "cos": np.cos(angles).T[i].astype(np.float32),
        "sin": (np.sin(angles).T[i] * sign[:, None]).astype(np.float32),
    }


def rows(w):
    return np.ascontiguousarray(w.reshape(w.shape[0] // P, P, w.shape[1]).transpose(1, 0, 2))


def swapped(w):
    return w.reshape(w.shape[0], -1, 2)[:, :, ::-1].reshape(w.shape)


def slots(w, bias=None):
    o = np.zeros((P, 4, D), w.dtype)
    for hd in range(HEADS):
        o[SLOT * (hd % 4):SLOT * (hd % 4) + HD, hd // 4] = w[HD * hd:HD * (hd + 1)]
    if bias is not None:
        o[HD, 0] = bias
    return o


def laid_out(v):
    half = INTER // 2
    member = np.array([4 * (P * hf + p) + r for hf in range(2) for r in range(4) for p in range(P)])
    paired = np.array([2 * p + part for part in range(2) for p in range(P)])
    kb = np.zeros((P, B, P), np.float32)
    for b in range(B):
        for r in range(2):
            kb[NKEYS * r:NKEYS * (r + 1), b, NKEYS * r:NKEYS * (r + 1)] = v["L0_ffn_keys"][b // 2]
    wqkv, bqkv = v["L0_attn_a_Wqkv"].T, v["L0_attn_a_b_qkv"]
    return {
        "x": np.ascontiguousarray(v["L0_attn_a_x"].reshape(B * NT, P, D).transpose(1, 0, 2)),
        "a0_wq": rows(wqkv[:, 0:D]), "a0_wk": rows(wqkv[:, D:2 * D]), "a0_wv": rows(wqkv[:, 2 * D:]),
        "a0_bqk": np.ascontiguousarray(bqkv[:2 * D].reshape(4, P).T), "a0_bv": np.tile(bqkv[2 * D:], (P, 1)),
        "a0_wo": slots(v["L0_attn_a_Wout"].T, v["L0_attn_a_b_out"]),
        "f0_wq": rows(v["L0_ffn_W_q"]), "f0_kb": kb,
        "f0_gate": rows(v["L0_ffn_gate_w"]), "f0_up": rows(v["L0_ffn_up_w"]), "f0_down": rows(v["L0_ffn_down_w"]),
        "f0_de": rows(v["L0_ffn_down_embed"].T), "f0_ue": rows(v["L0_ffn_up_embed"]),
        "a1_wq": rows(v["L1_attn_a_W_q"]), "a1_wq2": rows(swapped(v["L1_attn_a_W_q"])),
        "a1_wk": rows(v["L1_attn_a_W_k"]), "a1_wk2": rows(swapped(v["L1_attn_a_W_k"])),
        "a1_wv": rows(v["L1_attn_a_W_v"]), "a1_wo": slots(v["L1_attn_a_W_o"]),
        "f1_gate": rows(v["L1_ffn_w_gate"][:, member]), "f1_up": rows(v["L1_ffn_w_up"][:, member]),
        "f1_down": rows(v["L1_ffn_w_down"][member]),
        "s_act": rows(v["L1_attn_b_W_act"].T[:, paired]), "s_rec": rows(v["L1_attn_b_W_rec"].T),
        "s_val": rows(v["L1_attn_b_W_val"].T[paired]),
    }


def kernel(**inputs):
    import concourse.bacc as _bacc
    from concourse.bass_utils import run_bass_kernel_spmd as _run

    nc = _bacc.Bacc("TRN2", target_bir_lowering=False, num_devices=1)
    arrays = laid_out({k: np.asarray(v) for k, v in inputs.items()})
    arrays.update(shape_constants())
    a = {}
    for name, v in arrays.items():
        ap = nc.dram_tensor(f"in_{name}", v.shape, mybir.dt.from_np(v.dtype), kind="ExternalInput").ap()
        a[name] = ap.bitcast(BF16) if v.dtype == np.uint16 else ap
    out = nc.dram_tensor("out_x", (P, B * NT, D), F32, kind="ExternalOutput").ap()
    stages(nc, a, out)
    r = _run(nc, [{f"in_{name}": v for name, v in arrays.items()}], core_ids=[0])
    got = r.results[0]["out_x"]
    return np.ascontiguousarray(got.transpose(1, 0, 2)).reshape(B, T, D)
```

```python
from contextlib import ExitStack

import concourse.bass as bass
import numpy as np
from concourse import mybir

F32 = mybir.dt.float32
BF16 = mybir.dt.bfloat16
I32 = mybir.dt.int32
U32 = mybir.dt.uint32
ALU = mybir.AluOpType
ACT = mybir.ActivationFunctionType
AX = mybir.AxisListType.X

P = 128
B = 4
T = 512
NT = T // P
D = 256
DC = D // P
HEADS = 16
HD = D // HEADS
EPS = 1e-5
INTER = 1024
FC = INTER // P
EXPERTS = 512
EC = EXPERTS // P
NKEYS = 64
TOPK = 8
LOWKEYS = EXPERTS // NKEYS
BIG = 1e30
RSQRT_SEED = float(0x5F3759DF)


class Chain:

    def __init__(self, eng, sem, per):
        self.eng, self.sem, self.per = eng, sem, per

    def start(self, rnd):
        self.base, self.n = rnd * self.per, 0

    def do(self, ins):
        self.n += 1
        return ins.then_inc(self.sem, 1)

    def sync(self):
        self.eng.wait_ge(self.sem, self.base + self.n)

    def hold(self):
        self.sync()
        self.eng.sem_inc(self.sem, 1)
        self.n += 1

    def step(self, ins):
        self.do(ins)
        self.sync()

    def end(self):
        assert self.n == self.per, (self.n, self.per)


class Scope:

    def __init__(self, nc, name, stack, pool=None):
        self.nc, self.name, self.stack, self.pool = nc, name, stack, pool

    def sb(self, name, shape, dt=F32):
        return self.stack.enter_context(self.nc.sbuf_tensor(f"{self.name}_{name}", shape, dt))

    def sem(self, name):
        if self.pool is None:
            return self.stack.enter_context(self.nc.semaphore(f"{self.name}_{name}"))
        self.pool.append(self.nc.alloc_semaphore(name=f"{self.name}_{name}"))
        return self.pool[-1]


class NormBuffers:
    STEPS = 2 * NT + 1 + 3 + 9

    def __init__(self, s):
        self.stats = s.sb("stats", [P, NT, 6])
        self.mv = s.sb("mv", [P, NT, 2])
        self.var = s.sb("var", [P, NT])
        self.half = s.sb("half", [P, NT], I32)
        self.y = s.sb("rstd", [P, NT])
        self.t = s.sb("newton", [P, NT])


def norm_stats(dve, c, g, b, nb):
    x = g["x"]
    for t in range(NT):
        c.do(dve.bn_stats(nb.stats[:, t, :], x[:, 4 * b + t, :]))
    c.hold()
    for t in range(NT):
        c.do(dve.bn_aggr(nb.mv[:, t, :], nb.stats[:, t, :]))
    c.sync()
    c.step(dve.tensor_scalar(nb.var[:, :], nb.mv[:, :, 1], EPS, None, ALU.add))
    c.step(dve.tensor_scalar(nb.half[:, :], nb.var[:, :].bitcast(I32), 1, None, ALU.logical_shift_right))
    c.step(dve.tensor_scalar(nb.y[:, :].bitcast(I32), nb.half[:, :], -1.0, RSQRT_SEED, ALU.mult, ALU.add))
    for _ in range(3):
        c.step(dve.tensor_tensor(nb.t[:, :], nb.y[:, :], nb.y[:, :], ALU.mult))
        c.step(dve.scalar_tensor_tensor(nb.t[:, :], nb.t[:, :], -0.5, nb.var[:, :], ALU.mult, ALU.mult))
        c.step(dve.scalar_tensor_tensor(nb.y[:, :], nb.t[:, :], 1.5, nb.y[:, :], ALU.add, ALU.mult))


def norm_apply(dve, x, b, nb, xn):
    for t in range(NT):
        last = dve.tensor_scalar(xn[:, t, :], x[:, 4 * b + t, :], nb.mv[:, t, 0:1], nb.y[:, t:t + 1],
                                 ALU.subtract, ALU.mult)
    return last


def transpose_row(pe, ps, bank, xn, ident):
    for c in range(DC):
        for t in range(NT):
            last = pe.transpose(ps[:, bank + c, t * P:(t + 1) * P], xn[:, t, c * P:(c + 1) * P], ident[:, :])
    return last



def normalise_rows(nc, name, g, xT, queries=None):
    x, ps, ident = g["x"], g["ps"], g["ident"]
    with ExitStack() as stack:
        s = Scope(nc, name, stack)
        nb = NormBuffers(s)
        xn = s.sb("xn", [P, NT, D])
        dve_steps = s.sem("dve_steps")
        xn_ready, transposed, xt_ready = s.sem("xn_ready"), s.sem("transposed"), s.sem("xt_ready")
        if queries:
            wq, kb, scores = queries
            qT = s.sb("qT", [P, T])
            q_ready, qt_ready, r_ready, r_free = s.sem("q_ready"), s.sem("qt_ready"), s.sem("r_ready"), s.sem("r_free")
        block = stack.enter_context(nc.Block())

        @block.vector
        def _(dve):
            if queries:
                dve.sem_inc(r_free, 1)
            c = Chain(dve, dve_steps, NormBuffers.STEPS)
            with dve.Fori(0, B) as b:
                c.start(b)
                norm_stats(dve, c, g, b, nb)
                c.end()
                dve.wait_ge(transposed, b + 1)
                norm_apply(dve, x, b, nb, xn).then_inc(xn_ready, 1)
                if queries:
                    dve.wait_ge(r_ready, b + 1)
                    dve.tensor_copy(scores[:, bass.ds(4 * b, NT), :],
                                    ps[:, 3, :].rearrange("p (t k) -> p t k", t=NT)).then_inc(r_free, 1)

        @block.tensor
        def _(pe):
            pe.sem_inc(transposed, 1)
            pe.wait_ge(g["loaded"], g["loads"]["ident"])
            if queries:
                pe.wait_ge(g["loaded"], g["loads"]["router"])
            with pe.Fori(0, B) as b:
                pe.wait_ge(xn_ready, b + 1)
                pe.wait_ge(xt_ready, b + 1)
                transpose_row(pe, ps, 0, xn, ident).then_inc(transposed, 1)
                if queries:
                    pe.wait_ge(xt_ready, b + 2)
                    for c in range(DC):
                        last = pe.matmul(ps[:, 2, :], wq[:, c, :], xT[:, c, b, :], start=c == 0, stop=c == DC - 1)
                    last.then_inc(q_ready, 1)
                    pe.wait_ge(qt_ready, b + 1)
                    pe.wait_ge(r_free, b + 1)
                    for t in range(NT):
                        last = pe.matmul(ps[:, 3, t * P:(t + 1) * P], qT[:, t * P:(t + 1) * P], kb[:, b, :],
                                         start=True, stop=True)
                    last.then_inc(r_ready, 1)

        @block.scalar
        def _(act):
            act.sem_inc(xt_ready, 1)
            with act.Fori(0, B) as b:
                act.wait_ge(transposed, b + 2)
                act.activation(xT[:, :, b, :], ps[:, 0:DC, :], ACT.Copy).then_inc(xt_ready, 1)
                if queries:
                    act.wait_ge(q_ready, b + 1)
                    act.activation(qT[:, :], ps[:, 2, :], ACT.Copy).then_inc(qt_ready, 1)


def sparse_feed_forward(nc, name, g, w_gate, w_up, w_down):
    x, ps = g["x"], g["ps"]
    with ExitStack() as outer:
        so = Scope(nc, name, outer)
        xT = so.sb("xT", [P, DC, B, T])
        normalise_rows(nc, name + "n", g, xT)
        stack = outer.enter_context(ExitStack())
        s = Scope(nc, name + "m", stack)
        sg = s.sb("silu", [P, 2, T])
        h = s.sb("h", [P, FC, T])
        mag = s.sb("mag", [P, 2, 4, T])
        cmp_ = {ab: s.sb(f"ge{ab[0]}{ab[1]}", [P, T], BF16) for ab in
                [(0, 1), (0, 2), (0, 3), (1, 2), (1, 3), (2, 3)]}
        cnt = s.sb("count", [P, 4, T], BF16)
        gate_ready, up_ready = s.sem("gate_ready"), s.sem("up_ready")
        silu_done, prod_done, mag_done = s.sem("silu_done"), s.sem("prod_done"), s.sem("mag_done")
        sel_done, down_done, x_done = s.sem("sel_done"), s.sem("down_done"), s.sem("x_done")
        sel_steps = s.sem("sel_steps")
        block = stack.enter_context(nc.Block())


        @block.tensor
        def _(pe):
            pe.sem_inc(down_done, 2)
            pe.wait_ge(g["loaded"], g["loads"][g["w_key"]])

            def gate_up(b, half):
                for r in range(4):
                    j = 4 * half + r
                    n = FC * b + j
                    bank = 2 * (r % 2)
                    pe.wait_ge(silu_done, n + 1)
                    for c in range(DC):
                        last = pe.matmul(ps[:, bank, :], w_gate[:, c, j * P:(j + 1) * P], xT[:, c, b, :],
                                         start=c == 0, stop=c == DC - 1)
                    last.then_inc(gate_ready, 1)
                    pe.wait_ge(prod_done, n + 1)
                    for c in range(DC):
                        last = pe.matmul(ps[:, bank + 1, :], w_up[:, c, j * P:(j + 1) * P], xT[:, c, b, :],
                                         start=c == 0, stop=c == DC - 1)
                    last.then_inc(up_ready, 1)

            def down(b, half):
                pe.wait_ge(sel_done, 2 * b + half + 3)
                if half == 0:
                    pe.wait_ge(x_done, b + 1)
                for r in range(4):
                    j = 4 * half + r
                    for t in range(NT):
                        last = pe.matmul(ps[:, 4 + t // 2, (t % 2) * D:(t % 2 + 1) * D], h[:, j, t * P:(t + 1) * P],
                                         w_down[:, j, :], start=j == 0 and t % 2 == 0, stop=j == FC - 1,
                                         skip_group_check=True)
                last.then_inc(down_done, 1)

            gate_up(0, 0)
            with pe.Fori(0, B - 1) as b:
                gate_up(b, 1)
                down(b, 0)
                gate_up(b + 1, 0)
                down(b, 1)
            gate_up(B - 1, 1)
            down(B - 1, 0)
            down(B - 1, 1)

        @block.scalar
        def _(act):
            act.sem_inc(silu_done, 2)

            def half_chunks(b, half):
                m = 2 * b + half
                for r in range(4):
                    n = 4 * m + r
                    act.wait_ge(gate_ready, n + 1)
                    act.wait_ge(prod_done, n + 1)
                    act.activation(sg[:, r % 2, :], ps[:, 2 * (r % 2), :], ACT.Silu).then_inc(silu_done, 1)
                    act.wait_ge(prod_done, n + 3)
                    if r == 0:
                        act.wait_ge(sel_done, m + 1)
                    act.activation(mag[:, half, r, :], h[:, 4 * half + r, :], ACT.Abs).then_inc(mag_done, 1)

            with act.Fori(0, B) as b:
                half_chunks(b, 0)
                half_chunks(b, 1)

        @block.vector
        def _(dve):
            dve.sem_inc(prod_done, 2)
            dve.sem_inc(sel_done, 2)
            dve.sem_inc(x_done, 1)
            c = Chain(dve, sel_steps, 18)

            def product(b, half, r):
                m = 2 * b + half
                n = 4 * m + r
                dve.wait_ge(silu_done, n + 3)
                dve.wait_ge(up_ready, n + 1)
                if r == 0:
                    dve.wait_ge(down_done, m + 1)
                dve.tensor_tensor(h[:, 4 * half + r, :], sg[:, r % 2, :], ps[:, 2 * (r % 2) + 1, :],
                                  ALU.mult).then_inc(prod_done, 1)

            def select(b, half, part):
                m = 2 * b + half
                if part == 0:
                    c.start(m)
                    dve.wait_ge(mag_done, 4 * m + 4)
                    for (lo, hi), out in cmp_.items():
                        c.do(dve.tensor_tensor(out[:, :], mag[:, half, lo, :], mag[:, half, hi, :], ALU.is_ge))
                    c.sync()
                if part == 1:
                    g01, g02, g03, g12, g13, g23 = (cmp_[k][:, :] for k in cmp_)
                    for r, (a, e) in enumerate([(g01, g02), (g12, g13), (g02, g12), (g13, g23)]):
                        c.do(dve.tensor_tensor(cnt[:, r, :], a, e, ALU.add))
                    c.sync()
                    for r, (a, e, op) in enumerate([(cnt[:, 0, :], g03, ALU.add), (cnt[:, 1, :], g01, ALU.subtract),
                                                    (g23, cnt[:, 2, :], ALU.subtract), (cnt[:, 3, :], g03, ALU.add)]):
                        c.do(dve.tensor_tensor(cnt[:, r, :], a, e, op))
                    c.sync()
                if part == 2:
                    for r, (level, op) in enumerate([(1.5, ALU.is_ge), (0.5, ALU.is_ge), (-0.5, ALU.is_ge), (1.5, ALU.is_le)]):
                        hr = h[:, 4 * half + r, :]
                        c.do(dve.scalar_tensor_tensor(hr, cnt[:, r, :], level, hr, op, ALU.mult))
                    c.sync()
                    c.end()
                    dve.sem_inc(sel_done, 1)

            def add_to_x(b):
                dve.wait_ge(down_done, 2 * b + 4)
                for k in range(2):
                    xk = x[:, bass.ds(4 * b + 2 * k, 2), :]
                    last = dve.tensor_tensor(xk, xk, ps[:, 4 + k, :].rearrange("p (t d) -> p t d", t=2), ALU.add)
                last.then_inc(x_done, 1)

            for r in range(4):
                product(0, 0, r)
            with dve.Fori(0, B - 1) as b:
                for r in range(4):
                    product(b, 1, r)
                    if r < 3:
                        select(b, 0, r)
                for r in range(4):
                    product(b + 1, 0, r)
                    if r < 3:
                        select(b, 1, r)
                add_to_x(b)
            for r in range(4):
                product(B - 1, 1, r)
                if r < 3:
                    select(B - 1, 0, r)
            for r in range(3):
                select(B - 1, 1, r)
            add_to_x(B - 1)


def expert_feed_forward(nc, name, g, w_gate, w_up, w_down, wq, kb, w_de, w_ue):
    x, ps, ident = g["x"], g["ps"], g["ident"]
    with ExitStack() as outer:
        so = Scope(nc, name, outer)
        xT = so.sb("xT", [P, DC, B, T])
        scores = so.sb("scores", [P, B * NT, P])
        normalise_rows(nc, name + "n", g, xT, queries=(wq, kb, scores))
        stack = outer.enter_context(ExitStack())
        s = Scope(nc, name + "m", stack)
        NCH = FC + EC
        U = NT
        K8 = TOPK
        sg = s.sb("silu", [P, 2, T])
        h = s.sb("h", [P, NCH, T])
        sx, sy = s.sb("sx", [P, U, NKEYS]), s.sb("sy", [P, U, NKEYS])
        tx, ty, ts = s.sb("tx", [P, U, K8]), s.sb("ty", [P, U, K8]), s.sb("ts", [P, U, K8])
        ix, iy = s.sb("ix", [P, U, K8], U32), s.sb("iy", [P, U, K8], U32)
        ixf, iyf = s.sb("ixf", [P, U, K8]), s.sb("iyf", [P, U, K8])
        pair, rest = s.sb("pair", [P, U, K8, K8]), s.sb("rest", [P, U, K8, K8])
        pick = s.sb("pick", [P, U, K8, K8])
        arg = s.sb("arg", [P, U, LOWKEYS + NKEYS + K8 * K8])
        ex = s.sb("ex", [P, U, LOWKEYS + NKEYS + K8 * K8])
        picks, mass = s.sb("picks", [P, U, K8]), s.sb("mass", [P, U, K8])
        zsum, rz, hi = s.sb("zsum", [P, U]), s.sb("rz", [P, U]), s.sb("hi", [P, U])
        hot_x = s.sb("hot_x", [P, U, LOWKEYS, K8])
        need = s.sb("need", [P, U, LOWKEYS])
        hot_y = s.sb("hot_y", [P, U, NKEYS, K8])
        rank = s.sb("rank", [P, U, NKEYS])
        dense, wts = s.sb("dense", [P, U, LOWKEYS, NKEYS]), s.sb("wts", [P, U, LOWKEYS, NKEYS])
        iota, rankw = g["iota"], g["rankw"]
        gate_ready, up_ready = s.sem("gate_ready"), s.sem("up_ready")
        silu_done, prod_done = s.sem("silu_done"), s.sem("prod_done")
        down_done, x_done = s.sem("down_done"), s.sem("x_done")
        arg_ready, exp_done, w_ready = s.sem("arg_ready"), s.sem("exp_done"), s.sem("w_ready")
        route_steps = s.sem("route_steps")
        block = stack.enter_context(nc.Block())
        LO, HI = slice(0, LOWKEYS), slice(LOWKEYS, LOWKEYS + NKEYS)
        PR = slice(LOWKEYS + NKEYS, LOWKEYS + NKEYS + K8 * K8)


        @block.tensor
        def _(pe):
            pe.sem_inc(down_done, 2)
            pe.wait_ge(g["loaded"], g["loads"][g["w_key"]])

            def chunk(b, j):
                n = NCH * b + j
                bank = 2 * (j % 2)
                pe.wait_ge(silu_done, n + 1)
                for c in range(DC):
                    lhsT = w_gate[:, c, j * P:(j + 1) * P] if j < FC else w_de[:, c, (j - FC) * P:(j - FC + 1) * P]
                    last = pe.matmul(ps[:, bank, :], lhsT, xT[:, c, b, :], start=c == 0, stop=c == DC - 1)
                last.then_inc(gate_ready, 1)
                pe.wait_ge(prod_done, n + 1)
                if j < FC:
                    for c in range(DC):
                        last = pe.matmul(ps[:, bank + 1, :], w_up[:, c, j * P:(j + 1) * P], xT[:, c, b, :],
                                         start=c == 0, stop=c == DC - 1)
                else:
                    wt = wts[:, :, :, :].rearrange("p u i j -> p u (i j)")
                    for u in range(U):
                        last = pe.transpose(ps[:, bank + 1, u * P:(u + 1) * P], wt[:, u, (j - FC) * P:(j - FC + 1) * P],
                                            ident[:, :])
                last.then_inc(up_ready, 1)

            def down(b, group):
                js = range(FC) if group == 0 else range(FC, NCH)
                if group == 0:
                    pe.wait_ge(x_done, b + 1)
                for j in js:
                    pe.wait_ge(prod_done, NCH * b + j + 3)
                    for t in range(NT):
                        last = pe.matmul(ps[:, 4 + t // 2, (t % 2) * D:(t % 2 + 1) * D], h[:, j, t * P:(t + 1) * P],
                                         w_down[:, j, :] if j < FC else w_ue[:, j - FC, :],
                                         start=j == 0 and t % 2 == 0, stop=j == NCH - 1, skip_group_check=True)
                last.then_inc(down_done, 1)

            with pe.Fori(0, B) as b:
                for j in range(FC):
                    chunk(b, j)
                down(b, 0)
                pe.wait_ge(w_ready, b + 1)
                for j in range(FC, NCH):
                    chunk(b, j)
                down(b, 1)

        @block.scalar
        def _(act):
            act.sem_inc(silu_done, 2)
            with act.Fori(0, B) as b:
                for j in range(NCH):
                    n = NCH * b + j
                    act.wait_ge(gate_ready, n + 1)
                    act.wait_ge(prod_done, n + 1)
                    act.activation(sg[:, j % 2, :], ps[:, 2 * (j % 2), :], ACT.Silu).then_inc(silu_done, 1)
                    if j == 4:
                        act.wait_ge(arg_ready, b + 1)
                        act.activation(ex[:, :, :], arg[:, :, :], ACT.Exp).then_inc(exp_done, 1)

        @block.vector
        def _(dve):
            dve.sem_inc(prod_done, 2)
            dve.sem_inc(x_done, 1)
            c = Chain(dve, route_steps, 54)

            def product(b, j):
                n = NCH * b + j
                dve.wait_ge(silu_done, n + 3)
                dve.wait_ge(up_ready, n + 1)
                if j in (0, FC):
                    dve.wait_ge(down_done, 2 * b + j // FC + 1)
                if j < FC:
                    dve.tensor_tensor(h[:, j, :], sg[:, j % 2, :], ps[:, 2 * (j % 2) + 1, :],
                                      ALU.mult).then_inc(prod_done, 1)
                else:
                    ins = dve.tensor_tensor(h[:, j, :].rearrange("f (s p r) -> f s r p", s=2, r=2),
                                            sg[:, j % 2, :].rearrange("f (s p r) -> f s r p", s=2, r=2),
                                            ps[:, 2 * (j % 2) + 1, :].rearrange("f (s r p) -> f s r p", s=2, r=2),
                                            ALU.mult)
                    ins.then_inc(prod_done, 1)

            def wide(ap, shape, axis):
                return ap.unsqueeze(axis).broadcast_to(shape)

            def route(b, part):
                if part == 0:
                    c.start(b)
                    c.do(dve.tensor_copy(sx[:, :, :], scores[:, bass.ds(2 * b, 2), :].rearrange("p s (r k) -> p s r k", r=2)))
                    c.do(dve.tensor_copy(sy[:, :, :], scores[:, bass.ds(2 * b + 2 * NT, 2), :].rearrange("p s (r k) -> p s r k", r=2)))
                    c.hold()
                    for u in range(U):
                        c.do(dve.max(tx[:, u, :], sx[:, u, :]))
                        c.do(dve.max(ty[:, u, :], sy[:, u, :]))
                    c.sync()
                    c.do(dve.tensor_tensor(pair[:, :, :, :], wide(tx[:, :, :], [P, U, K8, K8], 3),
                                           wide(ty[:, :, :], [P, U, K8, K8], 2), ALU.add))
                if part == 1:
                    c.hold()
                    for u in range(U):
                        c.do(dve.max_index(ix[:, u, :], tx[:, u, :], sx[:, u, :]))
                        c.do(dve.max_index(iy[:, u, :], ty[:, u, :], sy[:, u, :]))
                    for u in range(U):
                        c.do(dve.max(ts[:, u, :], pair[:, u, :, :].rearrange("p a b -> p (a b)")))
                    c.hold()
                if part == 2:
                    for u in range(U):
                        c.do(dve.match_replace(rest[:, u, :, :].rearrange("p a b -> p (a b)"), ts[:, u, :],
                                               pair[:, u, :, :].rearrange("p a b -> p (a b)"), -3e38))
                    c.do(dve.tensor_tensor(arg[:, :, LO], sx[:, :, LO], tx[:, :, 0:1].broadcast_to([P, U, LOWKEYS]), ALU.subtract))
                    c.do(dve.tensor_tensor(arg[:, :, HI], sy[:, :, :], ty[:, :, 0:1].broadcast_to([P, U, NKEYS]), ALU.subtract))
                    c.do(dve.tensor_tensor(arg[:, :, PR], pair[:, :, :, :].rearrange("p u a b -> p u (a b)"),
                                           ts[:, :, 0:1].broadcast_to([P, U, K8 * K8]), ALU.subtract))
                    c.sync()
                    dve.sem_inc(arg_ready, 1)
                if part == 3:
                    c.do(dve.tensor_tensor(pick[:, :, :, :], rest[:, :, :, :], pair[:, :, :, :], ALU.is_lt))
                    c.do(dve.tensor_copy(ixf[:, :, :], ix[:, :, :]))
                    c.do(dve.tensor_copy(iyf[:, :, :], iy[:, :, :]))
                    c.sync()
                    c.do(dve.reduce_sum(picks[:, :, :], pick[:, :, :, :], AX))
                    c.do(dve.tensor_tensor(hot_x[:, :, :, :], wide(ixf[:, :, :], [P, U, LOWKEYS, K8], 2),
                                           iota[:, 0:LOWKEYS].unsqueeze(1).unsqueeze(3).broadcast_to([P, U, LOWKEYS, K8]),
                                           ALU.is_equal))
                    c.do(dve.tensor_tensor(hot_y[:, :, :, :], wide(iyf[:, :, :], [P, U, NKEYS, K8], 2),
                                           iota[:, :].unsqueeze(1).unsqueeze(3).broadcast_to([P, U, NKEYS, K8]),
                                           ALU.is_equal))
                    c.sync()
                if part == 4:
                    c.do(dve.tensor_tensor(hot_y[:, :, :, :].rearrange("p u j b -> p (u j) b"),
                                           hot_y[:, :, :, :].rearrange("p u j b -> p (u j) b"),
                                           rankw[:, :].unsqueeze(1).broadcast_to([P, U * NKEYS, K8]), ALU.mult))
                    c.do(dve.tensor_tensor(hot_x[:, :, :, :], hot_x[:, :, :, :], wide(picks[:, :, :], [P, U, LOWKEYS, K8], 2),
                                           ALU.mult))
                    c.sync()
                    c.do(dve.reduce_sum(rank[:, :, :], hot_y[:, :, :, :], AX))
                    c.do(dve.reduce_sum(need[:, :, :], hot_x[:, :, :, :], AX))
                    c.sync()
                if part == 5:
                    dve.wait_ge(exp_done, b + 1)
                    c.step(dve.tensor_tensor(rest[:, :, :, :].rearrange("p u a b -> p u (a b)"), ex[:, :, PR],
                                             pick[:, :, :, :].rearrange("p u a b -> p u (a b)"), ALU.mult))
                    c.step(dve.reduce_sum(mass[:, :, :], rest[:, :, :, :], AX))
                    c.step(dve.reduce_sum(zsum[:, :], mass[:, :, :], AX))
                    c.do(dve.reciprocal(rz[:, :], zsum[:, :]))
                    c.step(dve.scalar_tensor_tensor(mass[:, :, :], ixf[:, :, :], LOWKEYS - 0.5, mass[:, :, :], ALU.is_ge, ALU.mult))
                    c.do(dve.reduce_sum(hi[:, :], mass[:, :, :], AX))
                    c.step(dve.tensor_tensor(arg[:, :, LO], ex[:, :, LO], rz[:, :].unsqueeze(2).broadcast_to([P, U, LOWKEYS]), ALU.mult))
                    c.step(dve.tensor_tensor(hi[:, :], hi[:, :], rz[:, :], ALU.mult))
                if part == 6:
                    c.do(dve.tensor_tensor(dense[:, :, :, :], wide(rank[:, :, :], [P, U, LOWKEYS, NKEYS], 2),
                                           wide(need[:, :, :], [P, U, LOWKEYS, NKEYS], 3), ALU.add))
                    c.do(dve.tensor_tensor(wts[:, :, :, :], wide(ex[:, :, HI], [P, U, LOWKEYS, NKEYS], 2),
                                           wide(arg[:, :, LO], [P, U, LOWKEYS, NKEYS], 3), ALU.mult))
                    c.sync()
                if part == 7:
                    c.step(dve.scalar_tensor_tensor(wts[:, :, :, :], dense[:, :, :, :], K8 + 0.5, wts[:, :, :, :],
                                                    ALU.is_gt, ALU.mult))
                    lastw = wts[:, :, LOWKEYS - 1, NKEYS - 1]
                    dve.tensor_tensor(lastw, lastw, hi[:, :], ALU.add).then_inc(w_ready, 1)
                    c.end()

            with dve.Fori(0, B) as b:
                for j in range(NCH):
                    product(b, j)
                    if j < FC:
                        route(b, j)
                dve.wait_ge(down_done, 2 * b + 4)
                for k in range(2):
                    xk = x[:, bass.ds(4 * b + 2 * k, 2), :]
                    last = dve.tensor_tensor(xk, xk, ps[:, 4 + k, :].rearrange("p (t d) -> p t d", t=2), ALU.add)
                last.then_inc(x_done, 1)



PARTS = [0, 0, 1, 0, 1, 2]
K_PARTS = [0, 1, 0, 2, 1, 0]
STACK = 16 * len(PARTS)
SLOT = 32


def stack_rows(causal):
    first = STACK + (3 if causal else 0)
    return first, first + 3


def project_heads(nc, name, g, w, causal, qs, ks, vv):
    x, ps, ident = g["x"], g["ps"], g["ident"]
    KH = HEADS if causal else 4
    R1, R2 = stack_rows(causal)
    NQ, NK = 2, KH * HD // P if causal else 1
    KP = min(P, KH * HD)
    NCH = NQ + NK
    NG = 2 if causal else 3
    CREDIT = 1
    with ExitStack() as stack:
        s = Scope(nc, name, stack, g["to_clear"])
        nb = NormBuffers(s)
        xn = s.sb("xn", [P, NT, D])
        xT = s.sb("xT", [P, DC, T])
        qk = s.sb("qk", [P, NCH, T])
        rot = None if causal else s.sb("rot", [P, NCH, T])
        part = s.sb("part", [P, 3, NCH, T], BF16)
        q_dram = nc.dram_tensor(name + "_q_parts", [B, D, 3, T], BF16).ap()
        k_dram = nc.dram_tensor(name + "_k_parts", [B, KH * HD, 3, T], BF16).ap()
        norm_steps = s.sem("norm_steps")
        xn_ready, transposed, xt_ready = s.sem("xn_ready"), s.sem("transposed"), s.sem("xt_ready")
        proj_ready, proj_free = s.sem("proj_ready"), s.sem("proj_free")
        v_ready, v_free = s.sem("v_ready"), s.sem("v_free")
        qk_ready, rot_half, turned = s.sem("qk_ready"), s.sem("rot_half"), s.sem("turned")
        hi_ready, rest_ready, mid_ready, parts_ready = (s.sem("hi_ready"), s.sem("rest_ready"), s.sem("mid_ready"),
                                                        s.sem("parts_ready"))
        parts_stored, stack_loaded, sp_waits = s.sem("parts_stored"), s.sem("stack_loaded"), s.sem("sp_waits")
        block = stack.enter_context(nc.Block())


        @block.sync
        def _(sp):
            sp.sem_inc(parts_stored, CREDIT)
            for b in range(B):
                if causal:
                    sp.dma_start(ks[STACK:R1, b, :, :], w["bias_rows"]).then_inc(stack_loaded, 16)
                    sp.dma_start(qs[STACK:R1, b, :, :], w["one_rows"]).then_inc(stack_loaded, 16)
                sp.dma_start(ks[R1:R2, b, :, :], w["one_rows"][:, 0:KH, :]).then_inc(stack_loaded, 16)

            def hold(sem, value):
                sp.wait_ge(sem, value)
                sp.sem_inc(sp_waits, 1)

            with sp.Fori(0, B) as b:
                for ch in range(NCH):
                    dram, c, rows_ = (q_dram, ch, P) if ch < NQ else (k_dram, ch - NQ, KP)
                    hold(parts_ready, NCH * b + ch + 1 + NCH)
                    sp.dma_start(dram[b, c * P:c * P + rows_, :, :], part[0:rows_, :, ch, :]).then_inc(parts_stored, 16)
                hold(parts_stored, 16 * NCH * (b + 1) + CREDIT)
                for dst, dram, which in [(qs, q_dram, PARTS), (ks, k_dram, K_PARTS)]:
                    for i, p in enumerate(which):
                        sp.dma_start(dst[16 * i:16 * i + 16, b, :, :],
                                     dram[b, :, p, :].rearrange("(h p) n -> p h n", p=HD)).then_inc(stack_loaded, 16)
            sp.wait_ge(stack_loaded, 16 * (2 * len(PARTS) + (3 if causal else 1)) * B)

        @block.gpsimd
        def _(pool):
            pool.sem_inc(parts_ready, NCH)

            def chunk(ch):
                p = P if ch < NQ else KP
                return qk[0:p, ch, :], part[0:p, 0, ch, :], part[0:p, 1, ch, :], part[0:p, 2, ch, :], p

            with pool.Fori(0, B) as b:
                for ch in range(NCH + 2):
                    if not causal and ch < NCH:
                        f, _, _, _, p = chunk(ch)
                        pool.wait_ge(qk_ready, NCH * b + ch + 1)
                        pool.tensor_tensor(f, f, rot[0:p, ch, :], ALU.add).then_inc(turned, 1)
                    if 0 <= ch - 1 < NCH:
                        f, hi_, _, _, _ = chunk(ch - 1)
                        pool.wait_ge(hi_ready, NCH * b + ch)
                        pool.tensor_tensor(f, f, hi_, ALU.subtract).then_inc(rest_ready, 1)
                    if 0 <= ch - 2:
                        f, _, mid, lo, _ = chunk(ch - 2)
                        pool.wait_ge(mid_ready, NCH * b + ch - 1)
                        pool.tensor_tensor(lo, f, mid, ALU.subtract).then_inc(parts_ready, 1)

        @block.tensor
        def _(pe):
            pe.sem_inc(proj_free, NG)
            pe.sem_inc(v_free, 1)
            pe.wait_ge(g["loaded"], g["loads"][w["key"]])
            if causal:
                groups = [[(w["wq"], 0, P), (w["wq"], P, P)], [(w["wk"], 0, P), (w["wk"], P, P)]]
            else:
                groups = [[(w["wq"], 0, P), (w["wq2"], 0, P)], [(w["wq"], P, P), (w["wq2"], P, P)],
                          [(w["wk"], 0, KP), (w["wk2"], 0, KP)]]
            n_v = KH * HD
            with pe.Fori(0, B) as b:
                pe.wait_ge(xn_ready, b + 1)
                pe.wait_ge(v_free, b + 1)
                transpose_row(pe, ps, 0, xn, ident).then_inc(transposed, 1)
                pe.wait_ge(xt_ready, b + 1)
                for n, group in enumerate(groups):
                    pe.wait_ge(proj_free, NG * b + n + 1)
                    for k, (wt, f0, fn) in enumerate(group):
                        for c in range(DC):
                            last = pe.matmul(ps[0:fn, 2 + 2 * n + k, :], wt[:, c, f0:f0 + fn], xT[:, c, :],
                                             start=c == 0, stop=c == DC - 1)
                    last.then_inc(proj_ready, 1)
                for t in range(NT):
                    col = t * n_v
                    for c in range(DC):
                        last = pe.matmul(ps[:, col // T, col % T:col % T + n_v], xT[:, c, t * P:(t + 1) * P],
                                         w["wv"][:, c, :], start=c == 0, stop=c == DC - 1)
                last.then_inc(v_ready, 1)

        @block.scalar
        def _(act):
            def copy_transposed(b):
                act.wait_ge(transposed, b + 1)
                act.activation(xT[:, :, :], ps[:, 0:2, :], ACT.Copy).then_inc(xt_ready, 1)

            def cut(b):
                act.wait_ge(parts_stored, 16 * NCH * b + CREDIT)
                for ch in range(NCH + 1):
                    if ch < NCH:
                        p = P if ch < NQ else KP
                        act.wait_ge(qk_ready if causal else turned, NCH * b + ch + 1)
                        act.activation(part[0:p, 0, ch, :], qk[0:p, ch, :], ACT.Copy).then_inc(hi_ready, 1)
                    if ch >= 1:
                        p = P if ch - 1 < NQ else KP
                        act.wait_ge(rest_ready, NCH * b + ch)
                        act.activation(part[0:p, 1, ch - 1, :], qk[0:p, ch - 1, :], ACT.Copy).then_inc(mid_ready, 1)

            copy_transposed(0)
            with act.Fori(1, B) as b:
                copy_transposed(b)
                cut(b - 1)
            cut(B - 1)

        @block.vector
        def _(dve):
            c = Chain(dve, norm_steps, NormBuffers.STEPS)
            dve.wait_ge(g["loaded"], g["loads"][w["key"]])

            def normalise(b):
                c.start(b)
                norm_stats(dve, c, g, b, nb)
                c.end()

            def take(b):
                dve.wait_ge(parts_ready, NCH * (b + 1))
                if causal:
                    for ch in range(NCH):
                        if ch % 2 == 0:
                            dve.wait_ge(proj_ready, NG * b + ch // 2 + 1)
                        dve.tensor_scalar(qk[:, ch, :], ps[:, 2 + ch, :], w["bqk"][:, ch:ch + 1], None,
                                          ALU.add).then_inc(qk_ready, 1)
                        if ch % 2 == 1:
                            dve.wait_ge(qk_ready, NCH * b + ch + 1)
                            dve.sem_inc(proj_free, 1)
                else:
                    for n in range(NG):
                        p = P if n < NQ else KP
                        dve.wait_ge(proj_ready, NG * b + n + 1)
                        dve.tensor_tensor(qk[0:p, n, :], ps[0:p, 2 + 2 * n, :], w["cos"][0:p, :], ALU.mult).then_inc(rot_half, 1)
                        dve.tensor_tensor(rot[0:p, n, :], ps[0:p, 3 + 2 * n, :], w["sin"][0:p, :], ALU.mult).then_inc(rot_half, 1)
                        dve.wait_ge(rot_half, 2 * (NG * b + n + 1))
                        dve.sem_inc(qk_ready, 1)
                        dve.sem_inc(proj_free, 1)
                dve.wait_ge(v_ready, b + 1)
                src = ps[:, 0:2, :].rearrange("p b n -> p (b n)")[:, 0:NT * KH * HD].rearrange("p (t n) -> p t n", t=NT)
                if causal:
                    dve.tensor_tensor(vv[:, b, :, :], src, w["bv"][:, :].unsqueeze(1).broadcast_to([P, NT, KH * HD]),
                                      ALU.add).then_inc(v_free, 1)
                else:
                    dve.tensor_copy(vv[:, b, :, :], src).then_inc(v_free, 1)

            normalise(0)
            norm_apply(dve, x, 0, nb, xn).then_inc(xn_ready, 1)
            with dve.Fori(1, B) as b:
                normalise(b)
                dve.wait_ge(transposed, b)
                norm_apply(dve, x, b, nb, xn).then_inc(xn_ready, 1)
                take(b - 1)
            take(B - 1)


def attend(nc, name, g, w, causal, qs, ks, vv):
    x, ps, ident, identb = g["x"], g["ps"], g["ident"], g["identb"]
    KH = HEADS if causal else 4
    R1, R2 = stack_rows(causal)
    with ExitStack() as stack:
        s = Scope(nc, name, stack, g["to_clear"])
        negm = s.sb("negm", [P, NT, HEADS])
        mrest = s.sb("mrest", [HEADS, T])
        mpart = s.sb("mpart", [HEADS, 3, T], BF16)
        mpart_dram = nc.dram_tensor(name + "_maxima", [HEADS, 3, T], BF16).ap()
        va = s.sb("va", [P, NT, KH, SLOT])
        pr = s.sb("probs", [P, 8, T])
        ctxs = s.sb("ctxs", [P, T])
        rden = s.sb("rden", [P, NT, 4])
        ctx = s.sb("ctx", [P, NT, D])
        ctxT = s.sb("ctxT", [P, DC, T])

        den_steps, m_steps = s.sem("den_steps"), s.sem("m_steps")
        va_init, va_ready, biased = s.sem("va_init"), s.sem("va_ready"), s.sem("biased")
        r1_ready, r1_free = s.sem("r1_ready"), s.sem("r1_free")
        m_stored, sp_waits, mpart_ready, m_loaded = s.sem("m_stored"), s.sem("sp_waits"), s.sem("mpart_ready"), s.sem("m_loaded")
        s_ready, exp_done, pv_done = s.sem("s_ready"), s.sem("exp_done"), s.sem("pv_done")
        ctx_out, flipped, normalised = s.sem("ctx_out"), s.sem("flipped"), s.sem("normalised")
        merged, ctxt_ready, out_ready, x_done = s.sem("merged"), s.sem("ctxt_ready"), s.sem("out_ready"), s.sem("x_done")
        block = stack.enter_context(nc.Block())

        PAIRS = HEADS // 2 * NT
        PER1 = PAIRS + 2
        STEPS2 = 4 * NT
        CREDIT = 1
        LEAD, TAIL = 6, 3

        def pairs_at(k):
            if k < 0:
                return range(LEAD)
            if k >= STEPS2:
                return range(PAIRS - TAIL + k - STEPS2, PAIRS - TAIL + k - STEPS2 + 1)
            span = PAIRS - LEAD - TAIL
            return range(LEAD + span * k // STEPS2, LEAD + span * (k + 1) // STEPS2)

        def rounds(eng, body):
            body(0, None)
            with eng.Fori(1, B) as i:
                body(i, i - 1)
            body(None, B - 1)

        def bank1(pos):
            return 2 * (pos % 2)

        def width1(qt):
            return (qt + 1) * P if causal else T

        def width2(kt):
            return T - kt * P if causal else T

        @block.sync
        def _(sp):
            def hold(sem, value):
                sp.wait_ge(sem, value)
                sp.sem_inc(sp_waits, 1)

            sp.sem_inc(m_loaded, CREDIT)
            with sp.Fori(0, B) as b1:
                hold(mpart_ready, b1 + 1)
                sp.dma_start(mpart_dram, mpart[:, :, :]).then_inc(m_stored, 16)
                hold(m_stored, 16 * (b1 + 1))
                sp.dma_start(qs[R1:R2, b1, :, :], mpart_dram.rearrange("h i n -> i h n")).then_inc(m_loaded, 16)
            sp.wait_ge(m_loaded, 16 * B + CREDIT)

        if causal:
            @block.gpsimd
            def _(pool):
                pool.wait_ge(g["loaded"], g["loads"][w["key"]])
                with pool.Fori(0, B) as b:
                    xb = x[:, bass.ds(4 * b, NT), :]
                    pool.tensor_tensor(xb, xb, w["bo"][:, :].unsqueeze(1).broadcast_to([P, NT, D]),
                                       ALU.add).then_inc(biased, 1)

        @block.tensor
        def _(pe):
            pe.sem_inc(pv_done, 2)
            pe.wait_ge(g["loaded"], g["loads"][w["key"]])

            def item(b1, pos):
                pe.wait_ge(r1_free, PER1 * b1 + pos + 1)

            def score_pair(b1, n):
                hp, qt = n // NT, n % NT
                item(b1, n)
                for k in range(2):
                    hd = 2 * hp + k
                    last = pe.matmul(ps[:, bank1(n) + k, 0:width1(qt)], qs[0:R1, b1, hd, qt * P:(qt + 1) * P],
                                     ks[0:R1, b1, hd % KH, 0:width1(qt)], start=True, stop=True)
                    if causal:
                        last = pe.matmul(ps[:, bank1(n) + k, qt * P:(qt + 1) * P], identb[:, :], w["mask_qk"][:, :],
                                         start=False, stop=True, skip_group_check=True)
                last.then_inc(r1_ready, 1)

            def maxima(b1):
                pe.wait_ge(r1_free, PER1 * b1 + PAIRS + 2)
                for qt in range(NT):
                    last = pe.transpose(ps[0:HEADS, bank1(PAIRS), qt * P:(qt + 1) * P], negm[:, qt, :], ident[:, :])
                last.then_inc(r1_ready, 2)

            def scores_t(b2, k):
                grp, kt = k // NT, k % NT
                for j in range(4):
                    hd, m = 4 * grp + j, 4 * k + j
                    pe.wait_ge(exp_done, 4 * STEPS2 * b2 + m + 1)
                    last = pe.matmul(ps[:, 4 + j % 2, 0:width2(kt)], ks[0:R2, b2, hd % KH, kt * P:(kt + 1) * P],
                                     qs[0:R2, b2, hd, T - width2(kt):T], start=True, stop=True)
                    if causal:
                        last = pe.matmul(ps[:, 4 + j % 2, 0:P], identb[:, :], w["mask_kq"][:, :],
                                         start=False, stop=True, skip_group_check=True)
                    last.then_inc(s_ready, 1)

            def context(b2, k):
                grp, kt = k // NT, k % NT
                pe.wait_ge(exp_done, 4 * STEPS2 * b2 + 4 * k + 4 + 2)
                if kt == 0:
                    pe.wait_ge(ctx_out, 4 * b2 + grp + 1)
                if k == 0:
                    pe.wait_ge(x_done, b2 + 1)
                    pe.wait_ge(va_ready, b2 + 1)
                for j in range(4):
                    hd = 4 * grp + j
                    last = pe.matmul(ps[SLOT * j:SLOT * (j + 1), 6, T - width2(kt):T], va[:, kt, hd % KH, :],
                                     pr[:, 4 * (k % 2) + j, 0:width2(kt)], start=kt == 0, stop=kt == NT - 1,
                                     skip_group_check=True)
                last.then_inc(pv_done, 1)

            def flip(b2, grp):
                pe.wait_ge(ctx_out, 4 * b2 + grp + 2)
                pe.wait_ge(normalised, 4 * b2 + grp + 1)
                for t in range(NT):
                    last = pe.transpose(ps[:, 7, t * P:(t + 1) * P], ctxs[:, t * P:(t + 1) * P], ident[:, :])
                last.then_inc(flipped, 1)

            def merge(b2):
                pe.wait_ge(normalised, 4 * b2 + 5)
                transpose_row(pe, ps, 6, ctx, ident).then_inc(merged, 1)

            def project_out(b2):
                pe.wait_ge(ctxt_ready, b2 + 1)
                for t in range(NT):
                    for c in range(DC):
                        last = pe.matmul(ps[:, 6 + t // 2, (t % 2) * D:(t % 2 + 1) * D], ctxT[:, c, t * P:(t + 1) * P],
                                         w["wo"][:, c, :], start=c == 0, stop=c == DC - 1)
                last.then_inc(out_ready, 1)

            def body(b1, b2):
                for k in range(-1, STEPS2 + TAIL):
                    if b2 is not None:
                        if k == 0:
                            pe.wait_ge(m_loaded, 16 * (b2 + 1) + CREDIT)
                        if 0 <= k < STEPS2:
                            scores_t(b2, k)
                        if 1 <= k <= STEPS2:
                            context(b2, k - 1)
                        if k >= NT and k % NT == 1:
                            flip(b2, k // NT - 1)
                        if k == STEPS2 + 2:
                            merge(b2)
                    if b1 is not None:
                        for n in pairs_at(k):
                            score_pair(b1, n)
                if b1 is not None:
                    maxima(b1)
                if b2 is not None:
                    project_out(b2)

            pe.wait_ge(va_init, 2)
            rounds(pe, body)

        @block.scalar
        def _(act):
            act.sem_inc(exp_done, 2)
            act.sem_inc(ctx_out, 1)
            act.sem_inc(flipped, 1)

            def copy_context(b2, grp):
                act.wait_ge(pv_done, 4 * (4 * b2 + grp) + 4 + 2)
                act.wait_ge(flipped, 4 * b2 + grp + 1)
                act.activation(ctxs[:, :], ps[:, 6, :], ACT.Copy).then_inc(ctx_out, 1)

            with act.Fori(0, B) as b2:
                act.wait_ge(pv_done, STEPS2 * b2 + 2)
                act.activation(va[:, :, :, 0:HD], vv[:, b2, :, :].rearrange("p t (h d) -> p t h d", h=KH),
                               ACT.Copy).then_inc(va_ready, 1)
                for k in range(STEPS2):
                    act.wait_ge(pv_done, STEPS2 * b2 + k + 1)
                    for j in range(4):
                        act.wait_ge(s_ready, 4 * (STEPS2 * b2 + k) + j + 1)
                        act.activation(pr[:, 4 * (k % 2) + j, 0:width2(k % NT)], ps[:, 4 + j % 2, 0:width2(k % NT)],
                                       ACT.Exp, scale=HD ** -0.5).then_inc(exp_done, 1)
                    if k >= NT and k % NT == 0:
                        copy_context(b2, k // NT - 1)
                copy_context(b2, 3)
                act.wait_ge(merged, b2 + 1)
                act.activation(ctxT[:, :, :], ps[:, 6:8, :], ACT.Copy).then_inc(ctxt_ready, 1)

        @block.vector
        def _(dve):
            dve.sem_inc(r1_free, 2)
            dve.sem_inc(normalised, 1)
            dve.sem_inc(x_done, 1)
            dve.memset(va[:, :, :, HD:SLOT], 0.0).then_inc(va_init, 1)
            dve.wait_ge(va_init, 1)
            dve.memset(va[:, :, :, HD:HD + 1], 1.0).then_inc(va_init, 1)
            cden = Chain(dve, den_steps, 1)
            cm = Chain(dve, m_steps, 4)

            def take(b1, pos):
                dve.wait_ge(r1_ready, PER1 * b1 + pos + 1)

            def row_max(b1, n):
                hp, qt = n // NT, n % NT
                take(b1, n)
                dve.tensor_reduce(negm[:, qt, 2 * hp:2 * hp + 2], ps[:, bank1(n):bank1(n) + 2, 0:width1(qt)],
                                  AX, ALU.max, negate=True).then_inc(r1_free, 1)

            def max_rows(b1):
                take(b1, PAIRS)
                dve.wait_ge(m_loaded, 16 * b1 + CREDIT)
                cm.start(b1)
                m = ps[0:HEADS, bank1(PAIRS), :]
                cm.step(dve.tensor_copy(mpart[:, 0, :], m))
                cm.step(dve.tensor_tensor(mrest[:, :], m, mpart[:, 0, :], ALU.subtract))
                dve.sem_inc(r1_free, 2)
                cm.step(dve.tensor_copy(mpart[:, 1, :], mrest[:, :]))
                cm.step(dve.tensor_tensor(mpart[:, 2, :], mrest[:, :], mpart[:, 1, :], ALU.subtract))
                cm.end()
                dve.sem_inc(mpart_ready, 1)

            def normalise(b2, grp):
                dve.wait_ge(flipped, 4 * b2 + grp + 2)
                cden.start(4 * b2 + grp)
                got = ps[:, 7, :].rearrange("p (t j s) -> p t j s", t=NT, j=4)
                cden.step(dve.reciprocal(rden[:, :, :], got[:, :, :, HD]))
                dve.tensor_tensor(ctx[:, :, 4 * HD * grp:4 * HD * (grp + 1)].rearrange("p t (j d) -> p t j d", j=4),
                                  got[:, :, :, 0:HD], rden[:, :, :].unsqueeze(3).broadcast_to([P, NT, 4, HD]),
                                  ALU.mult).then_inc(normalised, 1)

            def add_to_x(b2):
                dve.wait_ge(out_ready, b2 + 1)
                if causal:
                    dve.wait_ge(biased, B)
                xb = x[:, bass.ds(4 * b2, NT), :]
                dve.tensor_tensor(xb, xb, ps[:, 6:8, :].rearrange("p b (t d) -> p (b t) d", t=2),
                                  ALU.add).then_inc(x_done, 1)

            def body(b1, b2):
                for k in range(-1, STEPS2 + TAIL):
                    if b2 is not None and k >= NT and k % NT == 1:
                        normalise(b2, k // NT - 1)
                    if b1 is not None:
                        for n in pairs_at(k):
                            row_max(b1, n)
                if b1 is not None:
                    max_rows(b1)
                if b2 is not None:
                    add_to_x(b2)

            rounds(dve, body)



def feature_attention(nc, name, g):
    x, ps, ident = g["x"], g["ps"], g["ident"]
    with ExitStack() as stack:
        s = Scope(nc, name, stack)
        nb = NormBuffers(s)
        xn = s.sb("xn", [P, NT, D])
        xT = s.sb("xT", [P, DC, T])
        negm = s.sb("negm", [P, DC])
        pr = s.sb("probs", [P, DC, D])
        den, rden = s.sb("den", [P, DC]), s.sb("rden", [P, DC])
        attT = s.sb("attT", [P, DC, D])
        norm_steps, soft_steps = s.sem("norm_steps"), s.sem("soft_steps")
        xn_ready, e_ready, tr_ready, xt_ready = s.sem("xn_ready"), s.sem("e_ready"), s.sem("tr_ready"), s.sem("xt_ready")
        max_ready, exp_done, att_ready, at_ready = s.sem("max_ready"), s.sem("exp_done"), s.sem("att_ready"), s.sem("at_ready")
        attt_ready, out_ready, x_done = s.sem("attt_ready"), s.sem("out_ready"), s.sem("x_done")
        block = stack.enter_context(nc.Block())


        @block.tensor
        def _(pe):
            pe.wait_ge(g["loaded"], g["loads"]["ident"])
            with pe.Fori(0, B) as b:
                pe.wait_ge(xn_ready, b + 1)
                for i in range(DC):
                    for t in range(NT):
                        last = pe.matmul(ps[:, 0, i * D:(i + 1) * D], xn[:, t, i * P:(i + 1) * P], xn[:, t, :],
                                         start=t == 0, stop=t == NT - 1)
                last.then_inc(e_ready, 1)
                transpose_row(pe, ps, 1, xn, ident).then_inc(tr_ready, 1)
                pe.wait_ge(att_ready, b + 1)
                for j in range(DC):
                    for i in range(DC):
                        last = pe.transpose(ps[:, 3, j * D + i * P:j * D + (i + 1) * P], pr[:, i, j * P:(j + 1) * P],
                                            ident[:, :])
                last.then_inc(at_ready, 1)
                pe.wait_ge(xt_ready, b + 1)
                pe.wait_ge(attt_ready, b + 1)
                pe.wait_ge(x_done, b + 1)
                for t in range(NT):
                    for j in range(DC):
                        last = pe.matmul(ps[:, 4 + t // 2, (t % 2) * D:(t % 2 + 1) * D], xT[:, j, t * P:(t + 1) * P],
                                         attT[:, j, :], start=j == 0, stop=j == DC - 1)
                last.then_inc(out_ready, 1)

        @block.scalar
        def _(act):
            with act.Fori(0, B) as b:
                act.wait_ge(tr_ready, b + 1)
                act.activation(xT[:, :, :], ps[:, 1:3, :], ACT.Copy).then_inc(xt_ready, 1)
                act.wait_ge(max_ready, b + 1)
                for i in range(DC):
                    act.activation(pr[:, i, :], ps[:, 0, i * D:(i + 1) * D], ACT.Exp, bias=negm[:, i:i + 1],
                                   accum_out=den[:, i:i + 1]).then_inc(exp_done, 1)
                act.wait_ge(at_ready, b + 1)
                act.activation(attT[:, :, :], ps[:, 3, :].rearrange("p (j i) -> p j i", j=DC), ACT.Copy).then_inc(attt_ready, 1)

        @block.vector
        def _(dve):
            dve.sem_inc(x_done, 1)
            cn = Chain(dve, norm_steps, NormBuffers.STEPS)
            cs = Chain(dve, soft_steps, 1)
            with dve.Fori(0, B) as b:
                cn.start(b)
                norm_stats(dve, cn, g, b, nb)
                cn.end()
                norm_apply(dve, x, b, nb, xn).then_inc(xn_ready, 1)
                dve.wait_ge(e_ready, b + 1)
                dve.tensor_reduce(negm[:, :], ps[:, 0, :].rearrange("p (i j) -> p i j", i=DC), AX, ALU.max,
                                  negate=True).then_inc(max_ready, 1)
                dve.wait_ge(exp_done, 2 * b + 2)
                cs.start(b)
                cs.step(dve.reciprocal(rden[:, :], den[:, :]))
                for i in range(DC):
                    last = dve.tensor_scalar(pr[:, i, :], pr[:, i, :], rden[:, i:i + 1], None, ALU.mult)
                last.then_inc(att_ready, 1)
                dve.wait_ge(out_ready, b + 1)
                for k in range(2):
                    xk = x[:, bass.ds(4 * b + 2 * k, 2), :]
                    last = dve.tensor_tensor(xk, xk, ps[:, 4 + k, :].rearrange("p (t d) -> p t d", t=2), ALU.add)
                last.then_inc(x_done, 1)



def gated_scan(nc, name, g, w_act, w_val, w_rec, key):
    x, ps, ident = g["x"], g["ps"], g["ident"]
    with ExitStack() as outer:
        so = Scope(nc, name, outer)
        zz = so.sb("z", [P, 2, B, T])
        r4 = so.sb("r4", [P, B, NT * D])
        kv = so.sb("kv", [P, 2, T])
        with ExitStack() as stack:
            s = Scope(nc, name + "g", stack)
            nb = NormBuffers(s)
            xn = s.sb("xn", [P, NT, D])
            xT = s.sb("xT", [P, DC, T + 1])
            z = s.sb("zrow", [P, 2, T])
            sq = s.sb("sq", [P, 2, T])
            mag, peak, rpeak = s.sb("mag", [P, T]), s.sb("peak", [P, T]), s.sb("rpeak", [P, T])
            rr = s.sb("rr", [P, NT * D])
            norm_steps, z_steps = s.sem("norm_steps"), s.sem("z_steps")
            zero_done = s.sem("zero_done")
            xn_ready, transposed, xt_ready = s.sem("xn_ready"), s.sem("transposed"), s.sem("xt_ready")
            act_ready, rec_ready, sig_done = s.sem("act_ready"), s.sem("rec_ready"), s.sem("sig_done")
            sq_ready, mag_done, z_done = s.sem("sq_ready"), s.sem("mag_done"), s.sem("z_done")
            block = stack.enter_context(nc.Block())


            @block.tensor
            def _(pe):
                pe.wait_ge(g["loaded"], g["loads"][key])
                pe.wait_ge(zero_done, 1)
                with pe.Fori(0, B) as b:
                    pe.wait_ge(xn_ready, b + 1)
                    transpose_row(pe, ps, 0, xn, ident).then_inc(transposed, 1)
                    pe.wait_ge(xt_ready, b + 1)
                    for part in range(2):
                        for k in range(2 * DC):
                            shift = k // DC
                            last = pe.matmul(ps[:, 2 + part, :], w_act[:, k, part * P:(part + 1) * P],
                                             xT[:, k % DC, shift:shift + T], start=k == 0, stop=k == 2 * DC - 1)
                    last.then_inc(act_ready, 1)
                    for t in range(NT):
                        for k in range(2 * DC):
                            c0 = t * P + k // DC
                            last = pe.matmul(ps[:, 4 + t // 2, (t % 2) * D:(t % 2 + 1) * D], xT[:, k % DC, c0:c0 + P],
                                             w_rec[:, k, :], start=k == 0, stop=k == 2 * DC - 1)
                    last.then_inc(rec_ready, 1)

            @block.scalar
            def _(act):
                with act.Fori(0, B) as b:
                    act.wait_ge(transposed, b + 1)
                    act.activation(xT[:, :, 1:T + 1], ps[:, 0:DC, :], ACT.Copy).then_inc(xt_ready, 1)
                    act.wait_ge(act_ready, b + 1)
                    act.activation(z[:, :, :], ps[:, 2:4, :], ACT.Sigmoid).then_inc(sig_done, 1)
                    act.wait_ge(rec_ready, b + 1)
                    act.activation(rr[:, :], ps[:, 4:6, :].rearrange("p b n -> p (b n)"), ACT.Sigmoid).then_inc(sig_done, 1)
                    act.wait_ge(sq_ready, b + 1)
                    act.activation(mag[:, :], sq[:, 0, :], ACT.Sqrt).then_inc(mag_done, 1)

            @block.vector
            def _(dve):
                dve.memset(xT[:, :, 0:1], 0.0).then_inc(zero_done, 1)
                cn = Chain(dve, norm_steps, NormBuffers.STEPS)
                cz = Chain(dve, z_steps, 7)
                with dve.Fori(0, B) as b:
                    cn.start(b)
                    norm_stats(dve, cn, g, b, nb)
                    cn.end()
                    norm_apply(dve, x, b, nb, xn).then_inc(xn_ready, 1)
                    dve.wait_ge(sig_done, 2 * b + 1)
                    cz.start(b)
                    cz.step(dve.tensor_scalar(z[:, :, :], z[:, :, :], 0.5, None, ALU.max))
                    cz.step(dve.tensor_tensor(sq[:, :, :], z[:, :, :], z[:, :, :], ALU.mult))
                    dve.tensor_tensor(sq[:, 0, :], sq[:, 0, :], sq[:, 1, :], ALU.add).then_inc(sq_ready, 1)
                    dve.wait_ge(sig_done, 2 * b + 2)
                    cz.step(dve.tensor_scalar(rr[:, :], rr[:, :], 0.5, None, ALU.max))
                    cz.step(dve.tensor_tensor(rr[:, :], rr[:, :], rr[:, :], ALU.mult))
                    cz.do(dve.tensor_tensor(r4[:, b, :], rr[:, :], rr[:, :], ALU.mult))
                    dve.wait_ge(mag_done, b + 1)
                    cz.step(dve.tensor_tensor_scan(peak[:, :], mag[:, :], mag[:, :], 0.0, ALU.max, ALU.max))
                    cz.step(dve.reciprocal(rpeak[:, :], peak[:, :]))
                    cz.end()
                    dve.tensor_tensor(zz[:, :, b, :], z[:, :, :], rpeak[:, :].unsqueeze(1).broadcast_to([P, 2, T]),
                                      ALU.mult).then_inc(z_done, 1)
                    dve.wait_ge(z_done, b + 1)

        with ExitStack() as stack:
            s = Scope(nc, name + "s", stack)
            S1, S2 = 8, 8
            S3 = T // (S1 * S2)
            tmp = [s.sb(f"t{i}", [P, B * T]) for i in range(4)]
            scan_steps = s.sem("scan_steps")
            prefix_done, kv_ready, out_ready, x_done = s.sem("prefix_done"), s.sem("kv_ready"), s.sem("out_ready"), s.sem("x_done")
            out_steps = s.sem("out_steps")
            prod = s.sb("prod", [P, NT * D])
            block = stack.enter_context(nc.Block())

            @block.vector
            def _(dve):
                c = Chain(dve, scan_steps, 0)
                c.start(0)

                def multiply(part, carry, shape):
                    n = int(np.prod(shape))
                    t = [a[:, 0:n] for a in tmp]
                    if len(shape) == 2:
                        t = [a.rearrange("p (a b) -> p a b", a=shape[0]) for a in t]
                    if len(shape) == 3:
                        t = [a.rearrange("p (a b c) -> p a b c", a=shape[0], b=shape[1]) for a in t]
                    for k, (i, j) in enumerate([(0, 0), (1, 1), (0, 1), (1, 0)]):
                        c.do(dve.tensor_tensor(t[k], carry(i), part(j), ALU.mult))
                    c.sync()
                    c.do(dve.tensor_tensor(part(0), t[0], t[1], ALU.subtract))
                    c.do(dve.tensor_tensor(part(1), t[2], t[3], ALU.add))
                    c.sync()

                seg = [zz[:, k, :, :].rearrange("p b (n s) -> p (b n) s", s=S1) for k in range(2)]
                for i in range(1, S1):
                    multiply(lambda k: seg[k][:, :, i], lambda k: seg[k][:, :, i - 1], (B * T // S1,))
                tot = [zz[:, k, :, :].rearrange("p b (m q s) -> p (b m) q s", s=S1, q=S2)[:, :, :, S1 - 1] for k in range(2)]
                for i in range(1, S2):
                    multiply(lambda k: tot[k][:, :, i], lambda k: tot[k][:, :, i - 1], (B * S3,))
                grp = [zz[:, k, :, :].rearrange("p b (m r) -> p b m r", m=S3)[:, :, :, S1 * S2 - 1] for k in range(2)]
                for i in range(1, S3):
                    multiply(lambda k: grp[k][:, :, i], lambda k: grp[k][:, :, i - 1], (B,))
                tot4 = [zz[:, k, :, :].rearrange("p b (m q s) -> p b m q s", s=S1, q=S2)[:, :, :, :, S1 - 1] for k in range(2)]
                multiply(lambda k: tot4[k][:, :, 1:S3, 0:S2 - 1],
                         lambda k: grp[k][:, :, 0:S3 - 1].unsqueeze(3).broadcast_to([P, B, S3 - 1, S2 - 1]),
                         (B, S3 - 1, S2 - 1))
                seg4 = [zz[:, k, :, :].rearrange("p b (n s) -> p b n s", s=S1) for k in range(2)]
                NS = T // S1
                multiply(lambda k: seg4[k][:, :, 1:NS, 0:S1 - 1],
                         lambda k: seg4[k][:, :, 0:NS - 1, S1 - 1:S1].broadcast_to([P, B, NS - 1, S1 - 1]),
                         (B, NS - 1, S1 - 1))
                dve.sem_inc(prefix_done, 1)
                dve.sem_inc(x_done, 1)
                co = Chain(dve, out_steps, 1)
                with dve.Fori(0, B) as b:
                    dve.wait_ge(out_ready, b + 1)
                    co.start(b)
                    co.step(dve.tensor_tensor(prod[:, :], ps[:, 0:2, :].rearrange("p b n -> p (b n)"), r4[:, b, :], ALU.mult))
                    xb = x[:, bass.ds(4 * b, NT), :]
                    dve.tensor_tensor(xb, xb, prod[:, :].rearrange("p (t d) -> p t d", t=NT), ALU.add).then_inc(x_done, 1)

            @block.scalar
            def _(act):
                act.wait_ge(prefix_done, 1)
                with act.Fori(0, B) as b:
                    act.wait_ge(x_done, b + 1)
                    act.activation(kv[:, :, :], zz[:, :, b, :], ACT.Copy).then_inc(kv_ready, 1)

            @block.tensor
            def _(pe):
                with pe.Fori(0, B) as b:
                    pe.wait_ge(kv_ready, b + 1)
                    for t in range(NT):
                        for k in range(2):
                            last = pe.matmul(ps[:, t // 2, (t % 2) * D:(t % 2 + 1) * D], kv[:, k, t * P:(t + 1) * P],
                                             w_val[:, k, :], start=k == 0, stop=k == 1)
                    last.then_inc(out_ready, 1)



def stages(nc, a, out):
    with ExitStack() as stack:
        def place(names, into):
            return {n: into.enter_context(nc.sbuf_tensor("sb_" + n, list(a[n].shape), a[n].dtype)) for n in names}

        x = stack.enter_context(nc.sbuf_tensor("x", [P, B * NT, D], F32))
        ps = stack.enter_context(nc.psum_tensor("ps", [P, 8, T], F32))
        loaded = stack.enter_context(nc.semaphore("loaded"))
        stored = stack.enter_context(nc.semaphore("stored"))
        common = ["ident", "identb", "iota", "rankw"]
        heads0 = ["a0_wq", "a0_wk", "a0_bqk", "a0_wv", "a0_bv"]
        att0 = ["a0_wo", "a0_bo", "mask_qk", "mask_kq"]
        router = ["f0_wq", "f0_kb"]
        ffn0 = ["f0_gate", "f0_up", "f0_down", "f0_de", "f0_ue"]
        att1 = ["a1_wq", "a1_wq2", "a1_wk", "a1_wk2", "a1_wv", "a1_wo", "cos", "sin"]
        ffn1 = ["f1_gate", "f1_up", "f1_down"]
        scan = ["s_act", "s_rec", "s_val"]

        sb, loads, issued = {}, {}, [0]
        sb.update(place(common, stack))

        def w_of(prefix, names):
            return {n[len(prefix):]: sb[n] for n in names if n.startswith(prefix)}

        def load(sp, names, key):
            for n in names:
                sp.dma_start(sb[n][:], a[n]).then_inc(loaded, 16)
            issued[0] += 16 * len(names)
            loads[key] = issued[0]

        g = dict(x=x, to_clear=[], ps=ps, loaded=loaded, loads=loads, ident=sb["ident"], identb=sb["identb"],
                 iota=sb["iota"], rankw=sb["rankw"])

        def stacks(name, key_heads, into):
            s = Scope(nc, name, into)
            return dict(qs=s.sb("qs", [P, B, HEADS, T], BF16), ks=s.sb("ks", [P, B, key_heads, T], BF16),
                        vv=s.sb("v", [P, B, NT, key_heads * HD]))

        with ExitStack() as first:
            sb.update(place(att0, first))
            qkv = stacks("attn0", HEADS, first)
            with ExitStack() as heads:
                sb.update(place(heads0, heads))
                with nc.Block() as block:
                    @block.sync
                    def _(sp):
                        sp.dma_start(x[:, :, :], a["x"]).then_inc(loaded, 16)
                        issued[0] += 16
                        loads["x"] = issued[0]
                        load(sp, common + heads0 + att0, "att0")
                        loads["ident"] = issued[0]
                w = dict(w_of("a0_", heads0 + att0), bias_rows=a["bias_rows"], one_rows=a["one_rows"],
                         mask_qk=sb["mask_qk"], mask_kq=sb["mask_kq"], key="att0")
                project_heads(nc, "heads0", g, w, True, **qkv)
            attend(nc, "attn0", g, w, True, **qkv)
        nc.clear_and_free_semaphores(g["to_clear"])
        g["to_clear"].clear()

        early = stack.enter_context(ExitStack())
        sb.update(place(router + ffn0, early))
        with nc.Block() as block:
            @block.sync
            def _(sp):
                load(sp, router + ffn0, "ffn0")
                loads["router"] = issued[0]
        g["w_key"] = "ffn0"
        experts = [sb[n] for n in ("f0_gate", "f0_up", "f0_down", "f0_wq", "f0_kb", "f0_de", "f0_ue")]
        expert_feed_forward(nc, "moe0", g, *experts)
        feature_attention(nc, "feat", g)
        expert_feed_forward(nc, "moe1", g, *experts)
        early.close()

        late = stack.enter_context(ExitStack())
        sb.update(place(att1 + ffn1 + scan, late))
        with nc.Block() as block:
            @block.sync
            def _(sp):
                load(sp, att1, "att1")
                sp.wait_ge(loaded, issued[0])
                load(sp, ffn1, "ffn1")
                load(sp, scan, "scan")
        with ExitStack() as second:
            qkv = stacks("attn1", 4, second)
            w = dict(w_of("a1_", att1), cos=sb["cos"], sin=sb["sin"], one_rows=a["one_rows"], key="att1")
            project_heads(nc, "heads1", g, w, False, **qkv)
            attend(nc, "attn1", g, w, False, **qkv)
        g["w_key"] = "ffn1"
        loads["ffn1"] = loads["scan"]
        sparse_feed_forward(nc, "mlp0", g, sb["f1_gate"], sb["f1_up"], sb["f1_down"])
        gated_scan(nc, "scan", g, sb["s_act"], sb["s_val"], sb["s_rec"], "scan")
        sparse_feed_forward(nc, "mlp1", g, sb["f1_gate"], sb["f1_up"], sb["f1_down"])
        with nc.Block() as block:
            @block.sync
            def _(sp):
                sp.dma_start(out, x[:, :, :]).then_inc(stored, 16)
                sp.wait_ge(stored, 16)


def bf16_bits(v):
    bits = v.astype(np.float32).view(np.uint32)
    bits = (bits + 0x7FFF + ((bits >> 16) & 1)) & np.uint32(0xFFFF0000)
    return (bits >> 16).astype(np.uint16), v - bits.view(np.float32)


def bf16_parts(v):
    got = []
    for _ in range(3):
        bits, v = bf16_bits(v)
        got.append(bits)
    return np.stack(got)


def shape_constants():
    slopes = 1.0 / 2.0 ** (np.arange(1, HEADS + 1, dtype=np.float32) * np.float32(8.0 / HEADS))
    bias = (np.arange(1 - T, 1, dtype=np.float32)[None, :] * slopes[:, None]).astype(np.float32)
    upper = np.triu(np.full((P, P), -BIG, np.float32), 1)
    freqs = (1.0 / 10000.0 ** (np.arange(HD // 2, dtype=np.float32) / (HD // 2))).astype(np.float32)
    angles = (np.arange(T, dtype=np.float32)[:, None] * freqs).astype(np.float64)
    i = (np.arange(P) % HD) // 2
    sign = np.where(np.arange(P) % 2 == 0, -1.0, 1.0)
    return {
        "ident": np.eye(P, dtype=np.float32), "identb": bf16_bits(np.eye(P, dtype=np.float32))[0],
        "mask_qk": bf16_bits(upper)[0], "mask_kq": bf16_bits(np.ascontiguousarray(upper.T))[0],
        "bias_rows": bf16_parts(np.float32(HD ** 0.5) * bias), "one_rows": bf16_bits(np.ones((3, HEADS, T), np.float32))[0],
        "iota": np.tile(np.arange(NKEYS, dtype=np.float32), (P, 1)),
        "rankw": np.tile(TOPK - np.arange(TOPK, dtype=np.float32), (P, 1)),
        "cos": np.cos(angles).T[i].astype(np.float32),
        "sin": (np.sin(angles).T[i] * sign[:, None]).astype(np.float32),
    }


def rows(w):
    return np.ascontiguousarray(w.reshape(w.shape[0] // P, P, w.shape[1]).transpose(1, 0, 2))


def swapped(w):
    return w.reshape(w.shape[0], -1, 2)[:, :, ::-1].reshape(w.shape)


def laid_out(v):
    half = INTER // 2
    member = np.array([4 * (P * hf + p) + r for hf in range(2) for r in range(4) for p in range(P)])
    paired = np.array([2 * p + part for part in range(2) for p in range(P)])
    kb = np.zeros((P, B, P), np.float32)
    for b in range(B):
        for r in range(2):
            kb[NKEYS * r:NKEYS * (r + 1), b, NKEYS * r:NKEYS * (r + 1)] = v["L0_ffn_keys"][b // 2]
    wqkv, bqkv = v["L0_attn_a_Wqkv"].T, v["L0_attn_a_b_qkv"]
    return {
        "x": np.ascontiguousarray(v["L0_attn_a_x"].reshape(B * NT, P, D).transpose(1, 0, 2)),
        "a0_wq": rows(wqkv[:, 0:D]), "a0_wk": rows(wqkv[:, D:2 * D]), "a0_wv": rows(wqkv[:, 2 * D:]),
        "a0_bqk": np.ascontiguousarray(bqkv[:2 * D].reshape(4, P).T), "a0_bv": np.tile(bqkv[2 * D:], (P, 1)),
        "a0_wo": rows(v["L0_attn_a_Wout"].T), "a0_bo": np.tile(v["L0_attn_a_b_out"], (P, 1)),
        "f0_wq": rows(v["L0_ffn_W_q"]), "f0_kb": kb,
        "f0_gate": rows(v["L0_ffn_gate_w"]), "f0_up": rows(v["L0_ffn_up_w"]), "f0_down": rows(v["L0_ffn_down_w"]),
        "f0_de": rows(v["L0_ffn_down_embed"].T), "f0_ue": rows(v["L0_ffn_up_embed"]),
        "a1_wq": rows(v["L1_attn_a_W_q"]), "a1_wq2": rows(swapped(v["L1_attn_a_W_q"])),
        "a1_wk": rows(v["L1_attn_a_W_k"]), "a1_wk2": rows(swapped(v["L1_attn_a_W_k"])),
        "a1_wv": rows(v["L1_attn_a_W_v"]), "a1_wo": rows(v["L1_attn_a_W_o"]),
        "f1_gate": rows(v["L1_ffn_w_gate"][:, member]), "f1_up": rows(v["L1_ffn_w_up"][:, member]),
        "f1_down": rows(v["L1_ffn_w_down"][member]),
        "s_act": rows(v["L1_attn_b_W_act"].T[:, paired]), "s_rec": rows(v["L1_attn_b_W_rec"].T),
        "s_val": rows(v["L1_attn_b_W_val"].T[paired]),
    }


def kernel(**inputs):
    import concourse.bacc as _bacc
    from concourse.bass_utils import run_bass_kernel_spmd as _run

    nc = _bacc.Bacc("TRN2", target_bir_lowering=False, num_devices=1)
    arrays = laid_out({k: np.asarray(v) for k, v in inputs.items()})
    arrays.update(shape_constants())
    a = {}
    for name, v in arrays.items():
        ap = nc.dram_tensor(f"in_{name}", v.shape, mybir.dt.from_np(v.dtype), kind="ExternalInput").ap()
        a[name] = ap.bitcast(BF16) if v.dtype == np.uint16 else ap
    out = nc.dram_tensor("out_x", (P, B * NT, D), F32, kind="ExternalOutput").ap()
    stages(nc, a, out)
    r = _run(nc, [{f"in_{name}": v for name, v in arrays.items()}], core_ids=[0])
    got = r.results[0]["out_x"]
    return np.ascontiguousarray(got.transpose(1, 0, 2)).reshape(B, T, D)
```

```python
from contextlib import ExitStack

import concourse.bass as bass
import numpy as np
from concourse import mybir

F32 = mybir.dt.float32
F32R = mybir.dt.float32r
BF16 = mybir.dt.bfloat16
I32 = mybir.dt.int32
U32 = mybir.dt.uint32
ALU = mybir.AluOpType
ACT = mybir.ActivationFunctionType
AX = mybir.AxisListType.X

P = 128
B = 4
T = 512
NT = T // P
D = 256
DC = D // P
HEADS = 16
HD = D // HEADS
EPS = 1e-5
INTER = 1024
FC = INTER // P
EXPERTS = 512
EC = EXPERTS // P
NKEYS = 64
TOPK = 8
LOWKEYS = EXPERTS // NKEYS
BIG = 1e30
RSQRT_SEED = float(0x5F3759DF)


class Chain:

    def __init__(self, eng, sem, per):
        self.eng, self.sem, self.per = eng, sem, per

    def start(self, rnd):
        self.base, self.n = rnd * self.per, 0

    def resume(self, rnd):
        self.base = rnd * self.per

    def do(self, ins):
        self.n += 1
        return ins.then_inc(self.sem, 1)

    def sync(self):
        self.eng.wait_ge(self.sem, self.base + self.n)

    def hold(self):
        self.sync()
        self.eng.sem_inc(self.sem, 1)
        self.n += 1

    def step(self, ins):
        self.do(ins)
        self.sync()

    def end(self):
        assert self.n == self.per, (self.n, self.per)


class Scope:

    def __init__(self, nc, name, stack, pool=None):
        self.nc, self.name, self.stack, self.pool = nc, name, stack, pool

    def sb(self, name, shape, dt=F32):
        return self.stack.enter_context(self.nc.sbuf_tensor(f"{self.name}_{name}", shape, dt))

    def sem(self, name):
        if self.pool is None:
            return self.stack.enter_context(self.nc.semaphore(f"{self.name}_{name}"))
        self.pool.append(self.nc.alloc_semaphore(name=f"{self.name}_{name}"))
        return self.pool[-1]


class NormBuffers:
    STEPS = 2 * NT + 1 + 3 + 9

    @staticmethod
    def steps(tiles):
        return 2 * tiles + 1 + 3 + 9

    def __init__(self, s, tiles=NT):
        self.tiles = tiles
        self.stats = s.sb("stats", [P, tiles, 6])
        self.mv = s.sb("mv", [P, tiles, 2])
        self.var = s.sb("var", [P, tiles])
        self.half = s.sb("half", [P, tiles], I32)
        self.y = s.sb("rstd", [P, tiles])
        self.t = s.sb("newton", [P, tiles])


def norm_stats(dve, c, g, b, nb):
    x = g["x"]
    for t in range(nb.tiles):
        c.do(dve.bn_stats(nb.stats[:, t, :], x[:, 4 * b + t, :]))
    c.hold()
    for t in range(nb.tiles):
        c.do(dve.bn_aggr(nb.mv[:, t, :], nb.stats[:, t, :]))
    c.sync()
    c.step(dve.tensor_scalar(nb.var[:, :], nb.mv[:, :, 1], EPS, None, ALU.add))
    c.step(dve.tensor_scalar(nb.half[:, :], nb.var[:, :].bitcast(I32), 1, None, ALU.logical_shift_right))
    c.step(dve.tensor_scalar(nb.y[:, :].bitcast(I32), nb.half[:, :], -1.0, RSQRT_SEED, ALU.mult, ALU.add))
    for _ in range(3):
        c.step(dve.tensor_tensor(nb.t[:, :], nb.y[:, :], nb.y[:, :], ALU.mult))
        c.step(dve.scalar_tensor_tensor(nb.t[:, :], nb.t[:, :], -0.5, nb.var[:, :], ALU.mult, ALU.mult))
        c.step(dve.scalar_tensor_tensor(nb.y[:, :], nb.t[:, :], 1.5, nb.y[:, :], ALU.add, ALU.mult))


def norm_apply(dve, x, b, nb, xn, first=0):
    for t in range(NT):
        last = dve.tensor_scalar(xn[:, t, :], x[:, 4 * b + t, :], nb.mv[:, first + t, 0:1], nb.y[:, first + t:first + t + 1],
                                 ALU.subtract, ALU.mult)
    return last


def transpose_row(pe, ps, bank, xn, ident):
    for c in range(DC):
        for t in range(NT):
            last = pe.transpose(ps[:, bank + c, t * P:(t + 1) * P], xn[:, t, c * P:(c + 1) * P], ident[:, :])
    return last



class Halves:

    def __init__(self, high, low):
        self.high, self.low = high, low


def products(a, b):
    return [(a.high, b.high), (a.high, b.low), (a.low, b.high)]


def normalise_rows(nc, name, g, xT, cut, queries=None, cut_first=()):
    x, ps, ident = g["x"], g["ps"], g["ident"]
    with ExitStack() as stack:
        s = Scope(nc, name, stack, g["to_clear"])
        nb = NormBuffers(s, B * NT)
        xn = s.sb("xn", [P, 2, NT, D])
        dve_steps = s.sem("dve_steps")
        xn_ready, transposed, xh_ready, xl_ready = s.sem("xn_ready"), s.sem("transposed"), s.sem("xh_ready"), s.sem("xl_ready")
        high_ready, cut_done = s.sem("high_ready"), s.sem("cut_done")
        first_in, all_in = s.sem("first_in"), s.sem("all_in")
        whole = {id(w): s.sb(f"w{k}", w.shape) for k, (w, _) in enumerate([*cut_first, *cut])}
        if queries:
            wq, kb, scores = queries
            qT = s.sb("qT", [P, T])
            q_ready, qt_ready, r_ready, r_free = s.sem("q_ready"), s.sem("qt_ready"), s.sem("r_ready"), s.sem("r_free")
        block = stack.enter_context(nc.Block())

        if cut or cut_first:
            @block.sync
            def _(sp):
                for w, _ in cut_first:
                    sp.dma_start(whole[id(w)][:], w).then_inc(first_in, 16)
                for w, _ in cut:
                    sp.dma_start(whole[id(w)][:], w).then_inc(all_in, 16)

        if cut:
            @block.gpsimd
            def _(pool):
                for k, (w, parts) in enumerate(cut):
                    if k % 2 == 1:
                        pool.wait_ge(high_ready, len(cut_first) + k + 1)
                        pool.tensor_tensor(parts.low[:], whole[id(w)][:], parts.high[:], ALU.subtract).then_inc(cut_done, 1)

        @block.vector
        def _(dve):
            def low_parts(weights, n, every):
                for k, (w, parts) in enumerate(weights):
                    if k % every == 0:
                        dve.wait_ge(high_ready, n + k + 1)
                        dve.tensor_tensor(parts.low[:], whole[id(w)][:], parts.high[:], ALU.subtract).then_inc(cut_done, 1)

            dve.sem_inc(xl_ready, 2)
            low_parts(cut_first, 0, 1)
            c = Chain(dve, dve_steps, NormBuffers.steps(B * NT))

            def take(b):
                dve.wait_ge(xh_ready, b + 1)
                dve.tensor_tensor(xT.low[:, :, b, :], ps[:, 4 * (b % 2):4 * (b % 2) + DC, :], xT.high[:, :, b, :], ALU.subtract).then_inc(xl_ready, 1)

            c.start(0)
            norm_stats(dve, c, g, 0, nb)
            c.end()
            norm_apply(dve, x, 0, nb, xn[:, 0, :, :]).then_inc(xn_ready, 1)
            for b in range(1, B):
                if b > 1:
                    dve.wait_ge(transposed, b - 1)
                norm_apply(dve, x, b, nb, xn[:, b % 2, :, :], 4 * b).then_inc(xn_ready, 1)
                take(b - 1)
            take(B - 1)
            low_parts(cut, len(cut_first), 2)

        @block.tensor
        def _(pe):
            pe.wait_ge(g["loaded"], g["loads"]["ident"])
            if queries:
                pe.wait_ge(g["loaded"], g["loads"]["router"])
            if cut_first:
                pe.wait_ge(cut_done, len(cut_first))

            def transposes(b):
                pe.wait_ge(xn_ready, b + 1)
                pe.wait_ge(xl_ready, b + 1)
                transpose_row(pe, ps, 4 * (b % 2), xn[:, b % 2, :, :], ident).then_inc(transposed, 1)

            def scores_of(b):
                pe.wait_ge(xl_ready, b + 3)
                for c in range(DC):
                    for k, (wp, xp) in enumerate(products(wq, xT)):
                        last = pe.matmul(ps[:, 2, :], wp[:, c, :], xp[:, c, b, :], start=c == 0 and k == 0,
                                         stop=c == DC - 1 and k == 2)
                last.then_inc(q_ready, 1)
                pe.wait_ge(qt_ready, b + 1)
                pe.wait_ge(r_free, b + 1)
                for t in range(NT):
                    last = pe.matmul(ps[:, 3, t * P:(t + 1) * P], qT[:, t * P:(t + 1) * P], kb[:, b, :],
                                     start=True, stop=True)
                last.then_inc(r_ready, 1)

            transposes(0)
            for b in range(1, B):
                transposes(b)
                if queries:
                    scores_of(b - 1)
            if queries:
                scores_of(B - 1)

        @block.scalar
        def _(act):
            def high_parts(weights, loaded):
                if weights:
                    act.wait_ge(loaded, 16 * len(weights))
                for w, parts in weights:
                    act.activation(parts.high[:], whole[id(w)][:], ACT.Copy).then_inc(high_ready, 1)

            if queries:
                act.sem_inc(r_free, 1)
            high_parts(cut_first, first_in)

            def high_row(b):
                act.wait_ge(transposed, b + 1)
                act.activation(xT.high[:, :, b, :], ps[:, 4 * (b % 2):4 * (b % 2) + DC, :], ACT.Copy).then_inc(xh_ready, 1)

            def copy_scores(b):
                act.wait_ge(q_ready, b + 1)
                act.activation(qT[:, :], ps[:, 2, :], ACT.Copy).then_inc(qt_ready, 1)
                act.wait_ge(r_ready, b + 1)
                act.activation(scores[:, bass.ds(4 * b, NT), :], ps[:, 3, :].rearrange("p (t k) -> p t k", t=NT),
                               ACT.Copy).then_inc(r_free, 1)

            high_row(0)
            for b in range(1, B - 1):
                high_row(b)
                if queries:
                    copy_scores(b - 1)
            high_row(B - 1)
            if queries:
                copy_scores(B - 2)
            high_parts(cut, all_in)
            if queries:
                copy_scores(B - 1)


def sparse_feed_forward(nc, name, g, w_gate, w_up, w_down, cut, out=None):
    x, ps = g["x"], g["ps"]
    with ExitStack() as outer:
        so = Scope(nc, name, outer)
        xT = Halves(so.sb("xh", [P, DC, B, T], F32R), so.sb("xl", [P, DC, B, T], F32R))
        normalise_rows(nc, name + "n", g, xT, cut)
        stack = outer.enter_context(ExitStack())
        s = Scope(nc, name + "m", stack)
        sg = s.sb("silu", [P, 2, T])
        h = s.sb("h", [P, FC, T])
        kept = Halves(s.sb("kept_high", [P, FC, T], F32R), s.sb("kept_low", [P, FC, T], F32R))
        mag = s.sb("mag", [P, 2, 4, T])
        cmp_ = {ab: s.sb(f"ge{ab[0]}{ab[1]}", [P, T], BF16) for ab in
                [(0, 1), (0, 2), (0, 3), (1, 2), (1, 3), (2, 3)]}
        cnt = s.sb("count", [P, 4, T], BF16)
        gate_ready, up_ready = s.sem("gate_ready"), s.sem("up_ready")
        silu_done, prod_done, mag_done = s.sem("silu_done"), s.sem("prod_done"), s.sem("mag_done")
        sel_done, high_done, low_done = s.sem("sel_done"), s.sem("high_done"), s.sem("low_done")
        down_done, x_done = s.sem("down_done"), s.sem("x_done")
        sel_steps = s.sem("sel_steps")
        stored, sp_waits = s.sem("stored"), s.sem("sp_waits")
        block = stack.enter_context(nc.Block())

        if out is not None:
            @block.sync
            def _(sp):
                with sp.Fori(0, B) as b:
                    sp.wait_ge(x_done, b + 3)
                    sp.sem_inc(sp_waits, 1)
                    sp.dma_start(out[:, bass.ds(4 * b, NT), :], x[:, bass.ds(4 * b, NT), :]).then_inc(stored, 16)
                sp.wait_ge(stored, 16 * B)


        @block.tensor
        def _(pe):
            pe.sem_inc(down_done, 2)
            def gate_up(b, half):
                for r in range(4):
                    j = 4 * half + r
                    n = FC * b + j
                    bank = 2 * (r % 2)
                    pe.wait_ge(silu_done, n + 1)
                    for c in range(DC):
                        for k, (wp, xp) in enumerate(products(w_gate, xT)):
                            last = pe.matmul(ps[:, bank, :], wp[:, c, j * P:(j + 1) * P], xp[:, c, b, :],
                                             start=c == 0 and k == 0, stop=c == DC - 1 and k == 2)
                    last.then_inc(gate_ready, 1)
                    pe.wait_ge(prod_done, n + 1)
                    for c in range(DC):
                        for k, (wp, xp) in enumerate(products(w_up, xT)):
                            last = pe.matmul(ps[:, bank + 1, :], wp[:, c, j * P:(j + 1) * P], xp[:, c, b, :],
                                             start=c == 0 and k == 0, stop=c == DC - 1 and k == 2)
                    last.then_inc(up_ready, 1)

            def down(b, half):
                m = 2 * b + half
                if half == 0:
                    pe.wait_ge(x_done, b + 1)
                for r in range(4):
                    j = 4 * half + r
                    pe.wait_ge(low_done, 4 * m + r + 9)
                    for t in range(NT):
                        for k, (hp, wp) in enumerate(products(kept, w_down)):
                            last = pe.matmul(ps[:, 4 + 2 * (b % 2) + t // 2, (t % 2) * D:(t % 2 + 1) * D], hp[:, j, t * P:(t + 1) * P],
                                             wp[:, j, :], start=j == 0 and t % 2 == 0 and k == 0,
                                             stop=j == FC - 1 and k == 2, skip_group_check=True)
                last.then_inc(down_done, 1)

            gate_up(0, 0)
            gate_up(0, 1)
            with pe.Fori(0, B - 1) as b:
                gate_up(b + 1, 0)
                down(b, 0)
                gate_up(b + 1, 1)
                down(b, 1)
            down(B - 1, 0)
            down(B - 1, 1)

        @block.scalar
        def _(act):
            act.sem_inc(silu_done, 2)

            def high_parts(m, half):
                act.wait_ge(sel_done, m + 3)
                act.wait_ge(down_done, m + 1)
                for r in range(4):
                    act.activation(kept.high[:, 4 * half + r, :], h[:, 4 * half + r, :], ACT.Copy).then_inc(high_done, 1)

            def half_chunks(b, half):
                m = 2 * b + half
                for r in range(4):
                    n = 4 * m + r
                    act.wait_ge(gate_ready, n + 1)
                    act.wait_ge(prod_done, n + 1)
                    act.activation(sg[:, r % 2, :], ps[:, 2 * (r % 2), :], ACT.Silu).then_inc(silu_done, 1)
                    act.wait_ge(prod_done, n + 3)
                    if r == 0:
                        act.wait_ge(sel_done, m + 1)
                    act.activation(mag[:, half, r, :], h[:, 4 * half + r, :], ACT.Abs).then_inc(mag_done, 1)

            half_chunks(0, 0)
            half_chunks(0, 1)
            high_parts(0, 0)
            with act.Fori(0, B - 1) as b:
                half_chunks(b + 1, 0)
                high_parts(2 * b + 1, 1)
                half_chunks(b + 1, 1)
                high_parts(2 * b + 2, 0)
            high_parts(2 * B - 1, 1)

        @block.gpsimd
        def _(pool):
            pool.sem_inc(low_done, 8)
            with pool.Fori(0, B) as b:
                for j in range(FC):
                    pool.wait_ge(high_done, FC * b + j + 1)
                    pool.tensor_tensor(kept.low[:, j, :], h[:, j, :], kept.high[:, j, :], ALU.subtract).then_inc(low_done, 1)

        @block.vector
        def _(dve):
            dve.sem_inc(prod_done, 2)
            dve.sem_inc(sel_done, 2)
            dve.sem_inc(x_done, 2)
            c = Chain(dve, sel_steps, 18)

            def product(b, half, r):
                m = 2 * b + half
                n = 4 * m + r
                dve.wait_ge(silu_done, n + 3)
                dve.wait_ge(up_ready, n + 1)
                dve.wait_ge(low_done, n + 1)
                dve.tensor_tensor(h[:, 4 * half + r, :], sg[:, r % 2, :], ps[:, 2 * (r % 2) + 1, :],
                                  ALU.mult).then_inc(prod_done, 1)

            def select(b, half, part):
                m = 2 * b + half
                if part == 0:
                    c.start(m)
                    dve.wait_ge(mag_done, 4 * m + 4)
                    for (lo, hi), out in cmp_.items():
                        c.do(dve.tensor_tensor(out[:, :], mag[:, half, lo, :], mag[:, half, hi, :], ALU.is_ge))
                    c.sync()
                if part == 1:
                    g01, g02, g03, g12, g13, g23 = (cmp_[k][:, :] for k in cmp_)
                    for r, (a, e) in enumerate([(g01, g02), (g12, g13), (g02, g12), (g13, g23)]):
                        c.do(dve.tensor_tensor(cnt[:, r, :], a, e, ALU.add))
                    c.sync()
                    for r, (a, e, op) in enumerate([(cnt[:, 0, :], g03, ALU.add), (cnt[:, 1, :], g01, ALU.subtract),
                                                    (g23, cnt[:, 2, :], ALU.subtract), (cnt[:, 3, :], g03, ALU.add)]):
                        c.do(dve.tensor_tensor(cnt[:, r, :], a, e, op))
                    c.sync()
                if part == 2:
                    for r, (level, op) in enumerate([(1.5, ALU.is_ge), (0.5, ALU.is_ge), (-0.5, ALU.is_ge), (1.5, ALU.is_le)]):
                        hr = h[:, 4 * half + r, :]
                        c.do(dve.scalar_tensor_tensor(hr, cnt[:, r, :], level, hr, op, ALU.mult))
                    c.sync()
                    c.end()
                    dve.sem_inc(sel_done, 1)

            def add_to_x(b):
                dve.wait_ge(down_done, 2 * b + 4)
                for k in range(2):
                    xk = x[:, bass.ds(4 * b + 2 * k, 2), :]
                    last = dve.tensor_tensor(xk, xk, ps[:, 4 + 2 * (b % 2) + k, :].rearrange("p (t d) -> p t d", t=2), ALU.add)
                last.then_inc(x_done, 1)

            def half_chunks(b, half, selected, added=None):
                for r in range(4):
                    product(b, half, r)
                    if selected is not None and r < 3:
                        select(*selected, r)
                    if added is not None and r == 1:
                        add_to_x(added)

            half_chunks(0, 0, None)
            half_chunks(0, 1, (0, 0))
            half_chunks(1, 0, (0, 1))
            with dve.Fori(1, B - 1) as b:
                half_chunks(b, 1, (b, 0))
                half_chunks(b + 1, 0, (b, 1), b - 1)
            half_chunks(B - 1, 1, (B - 1, 0))
            select(B - 1, 1, 0)
            select(B - 1, 1, 1)
            add_to_x(B - 2)
            select(B - 1, 1, 2)
            add_to_x(B - 1)


def expert_feed_forward(nc, name, g, w, cut, cut_first):
    w_gate, w_up, w_down, w_de, w_ue = (w[n] for n in ("gate", "up", "down", "de", "ue"))
    x, ps, ident = g["x"], g["ps"], g["ident"]
    with ExitStack() as outer:
        so = Scope(nc, name, outer)
        xT = Halves(so.sb("xh", [P, DC, B, T], F32R), so.sb("xl", [P, DC, B, T], F32R))
        scores = so.sb("scores", [P, B * NT, P])
        normalise_rows(nc, name + "n", g, xT, cut, (w["wq"], w["kb"], scores), cut_first)
        stack = outer.enter_context(ExitStack())
        s = Scope(nc, name + "m", stack, g["to_clear"])
        NCH = FC + EC
        U = NT
        K8 = TOPK
        sg = s.sb("silu", [P, 2, T])
        RING, LAG = 4, 3
        h = s.sb("h", [P, RING, T])
        hc = Halves(s.sb("h_high", [P, RING, T], F32R), s.sb("h_low", [P, RING, T], F32R))
        sx, sy = s.sb("sx", [P, U, NKEYS]), s.sb("sy", [P, U, NKEYS])
        tx, ty, ts = s.sb("tx", [P, U, K8]), s.sb("ty", [P, U, K8]), s.sb("ts", [P, U, K8])
        ix, iy = s.sb("ix", [P, U, K8], U32), s.sb("iy", [P, U, K8], U32)
        ixf, iyf = s.sb("ixf", [P, U, K8]), s.sb("iyf", [P, U, K8])
        pair, rest = s.sb("pair", [P, U, K8, K8]), s.sb("rest", [P, U, K8, K8])
        pick = s.sb("pick", [P, U, K8, K8])
        arg = s.sb("arg", [P, U, LOWKEYS + NKEYS + K8 * K8])
        ex = s.sb("ex", [P, U, LOWKEYS + NKEYS + K8 * K8])
        picks, mass = s.sb("picks", [P, U, K8]), s.sb("mass", [P, U, K8])
        zsum, rz, hi = s.sb("zsum", [P, U]), s.sb("rz", [P, U]), s.sb("hi", [P, U])
        hot_x = s.sb("hot_x", [P, U, LOWKEYS, K8])
        need = s.sb("need", [P, U, LOWKEYS])
        hot_y = s.sb("hot_y", [P, U, NKEYS, K8])
        rank = s.sb("rank", [P, U, NKEYS])
        dense, wts = s.sb("dense", [P, U, LOWKEYS, NKEYS]), s.sb("wts", [P, U, LOWKEYS, NKEYS])
        iota, rankw = g["iota"], g["rankw"]
        gate_ready, up_ready = s.sem("gate_ready"), s.sem("up_ready")
        silu_done, prod_done = s.sem("silu_done"), s.sem("prod_done")
        high_done, low_done = s.sem("high_done"), s.sem("low_done")
        down_done, x_done = s.sem("down_done"), s.sem("x_done")
        arg_ready, exp_done, w_ready = s.sem("arg_ready"), s.sem("exp_done"), s.sem("w_ready")
        route_steps = s.sem("route_steps")
        block = stack.enter_context(nc.Block())
        LO, HI = slice(0, LOWKEYS), slice(LOWKEYS, LOWKEYS + NKEYS)
        PR = slice(LOWKEYS + NKEYS, LOWKEYS + NKEYS + K8 * K8)


        @block.tensor
        def _(pe):
            pe.sem_inc(down_done, RING)
            def chunk(b, j):
                n = NCH * b + j
                bank = 2 * (j % 2)
                pe.wait_ge(silu_done, n + 1)
                gate, f0 = (w_gate, j * P) if j < FC else (w_de, (j - FC) * P)
                for c in range(DC):
                    for k, (wp, xp) in enumerate(products(gate, xT)):
                        last = pe.matmul(ps[:, bank, :], wp[:, c, f0:f0 + P], xp[:, c, b, :],
                                         start=c == 0 and k == 0, stop=c == DC - 1 and k == 2)
                last.then_inc(gate_ready, 1)
                pe.wait_ge(prod_done, n + 1)
                if j < FC:
                    for c in range(DC):
                        for k, (wp, xp) in enumerate(products(w_up, xT)):
                            last = pe.matmul(ps[:, bank + 1, :], wp[:, c, f0:f0 + P], xp[:, c, b, :],
                                             start=c == 0 and k == 0, stop=c == DC - 1 and k == 2)
                else:
                    wt = wts[:, :, :, :].rearrange("p u i j -> p u (i j)")
                    for u in range(U):
                        last = pe.transpose(ps[:, bank + 1, u * P:(u + 1) * P], wt[:, u, (j - FC) * P:(j - FC + 1) * P],
                                            ident[:, :])
                last.then_inc(up_ready, 1)

            def down(b, j):
                if j == 0:
                    pe.wait_ge(x_done, b + 1)
                pe.wait_ge(low_done, NCH * b + j + 1 + RING)
                down_w, jw = (w_down, j) if j < FC else (w_ue, j - FC)
                for t in range(NT):
                    for k, (hp, wp) in enumerate(products(hc, down_w)):
                        last = pe.matmul(ps[:, 4 + t // 2, (t % 2) * D:(t % 2 + 1) * D], hp[:, j % RING, t * P:(t + 1) * P],
                                         wp[:, jw, :], start=j == 0 and t % 2 == 0 and k == 0,
                                         stop=j == NCH - 1 and k == 2, skip_group_check=True)
                last.then_inc(down_done, 1)

            def batch_row(b, before):
                for j in range(NCH):
                    if j == FC:
                        pe.wait_ge(w_ready, b + 1)
                    chunk(b, j)
                    if j >= LAG:
                        down(b, j - LAG)
                    elif before is not None:
                        down(before, NCH - LAG + j)

            batch_row(0, None)
            with pe.Fori(1, B) as b:
                batch_row(b, b - 1)
            for j in range(NCH - LAG, NCH):
                down(B - 1, j)

        @block.scalar
        def _(act):
            act.sem_inc(silu_done, 2)

            def high_part(b, j):
                n = NCH * b + j
                act.wait_ge(prod_done, n + 3)
                act.wait_ge(down_done, n + 1)
                act.activation(hc.high[:, j % RING, :], h[:, j % RING, :], ACT.Copy).then_inc(high_done, 1)

            def batch_row(b, exp_at):
                for j in range(NCH):
                    n = NCH * b + j
                    act.wait_ge(gate_ready, n + 1)
                    act.wait_ge(prod_done, n + 1)
                    act.activation(sg[:, j % 2, :], ps[:, 2 * (j % 2), :], ACT.Silu).then_inc(silu_done, 1)
                    if j >= 1:
                        high_part(b, j - 1)
                    if j == exp_at:
                        act.wait_ge(arg_ready, b + 1)
                        act.activation(ex[:, :, :], arg[:, :, :], ACT.Exp).then_inc(exp_done, 1)
                high_part(b, NCH - 1)

            batch_row(0, 4)
            with act.Fori(1, B) as b:
                batch_row(b, 0)

        @block.gpsimd
        def _(pool):
            pool.sem_inc(low_done, RING)
            with pool.Fori(0, B) as b:
                for j in range(NCH):
                    pool.wait_ge(high_done, NCH * b + j + 1)
                    pool.tensor_tensor(hc.low[:, j % RING, :], h[:, j % RING, :], hc.high[:, j % RING, :],
                                       ALU.subtract).then_inc(low_done, 1)

        @block.vector
        def _(dve):
            dve.sem_inc(prod_done, 2)
            dve.sem_inc(x_done, 1)
            c = Chain(dve, route_steps, 54)

            def product(b, j):
                n = NCH * b + j
                dve.wait_ge(silu_done, n + 3)
                dve.wait_ge(up_ready, n + 1)
                dve.wait_ge(low_done, n + 1)
                if j < FC:
                    dve.tensor_tensor(h[:, j % RING, :], sg[:, j % 2, :], ps[:, 2 * (j % 2) + 1, :],
                                      ALU.mult).then_inc(prod_done, 1)
                else:
                    ins = dve.tensor_tensor(h[:, j % RING, :].rearrange("f (s p r) -> f s r p", s=2, r=2),
                                            sg[:, j % 2, :].rearrange("f (s p r) -> f s r p", s=2, r=2),
                                            ps[:, 2 * (j % 2) + 1, :].rearrange("f (s r p) -> f s r p", s=2, r=2),
                                            ALU.mult)
                    ins.then_inc(prod_done, 1)

            def wide(ap, shape, axis):
                return ap.unsqueeze(axis).broadcast_to(shape)

            def route(b, part):
                if part == 0:
                    c.start(b)
                    c.do(dve.tensor_copy(sx[:, :, :], scores[:, bass.ds(2 * b, 2), :].rearrange("p s (r k) -> p s r k", r=2)))
                    c.do(dve.tensor_copy(sy[:, :, :], scores[:, bass.ds(2 * b + 2 * NT, 2), :].rearrange("p s (r k) -> p s r k", r=2)))
                    c.hold()
                    for u in range(U):
                        c.do(dve.max(tx[:, u, :], sx[:, u, :]))
                        c.do(dve.max(ty[:, u, :], sy[:, u, :]))
                    c.sync()
                    c.do(dve.tensor_tensor(pair[:, :, :, :], wide(tx[:, :, :], [P, U, K8, K8], 3),
                                           wide(ty[:, :, :], [P, U, K8, K8], 2), ALU.add))
                if part == 1:
                    c.hold()
                    for u in range(U):
                        c.do(dve.max_index(ix[:, u, :], tx[:, u, :], sx[:, u, :]))
                        c.do(dve.max_index(iy[:, u, :], ty[:, u, :], sy[:, u, :]))
                    for u in range(U):
                        c.do(dve.max(ts[:, u, :], pair[:, u, :, :].rearrange("p a b -> p (a b)")))
                    c.hold()
                if part == 2:
                    for u in range(U):
                        c.do(dve.match_replace(rest[:, u, :, :].rearrange("p a b -> p (a b)"), ts[:, u, :],
                                               pair[:, u, :, :].rearrange("p a b -> p (a b)"), -3e38))
                    c.do(dve.tensor_tensor(arg[:, :, LO], sx[:, :, LO], tx[:, :, 0:1].broadcast_to([P, U, LOWKEYS]), ALU.subtract))
                    c.do(dve.tensor_tensor(arg[:, :, HI], sy[:, :, :], ty[:, :, 0:1].broadcast_to([P, U, NKEYS]), ALU.subtract))
                    c.do(dve.tensor_tensor(arg[:, :, PR], pair[:, :, :, :].rearrange("p u a b -> p u (a b)"),
                                           ts[:, :, 0:1].broadcast_to([P, U, K8 * K8]), ALU.subtract))
                    c.sync()
                    dve.sem_inc(arg_ready, 1)
                if part == 3:
                    c.do(dve.tensor_tensor(pick[:, :, :, :], rest[:, :, :, :], pair[:, :, :, :], ALU.is_lt))
                    c.do(dve.tensor_copy(ixf[:, :, :], ix[:, :, :]))
                    c.do(dve.tensor_copy(iyf[:, :, :], iy[:, :, :]))
                    c.sync()
                    c.do(dve.reduce_sum(picks[:, :, :], pick[:, :, :, :], AX))
                    c.do(dve.tensor_tensor(hot_x[:, :, :, :], wide(ixf[:, :, :], [P, U, LOWKEYS, K8], 2),
                                           iota[:, 0:LOWKEYS].unsqueeze(1).unsqueeze(3).broadcast_to([P, U, LOWKEYS, K8]),
                                           ALU.is_equal))
                    c.do(dve.tensor_tensor(hot_y[:, :, :, :], wide(iyf[:, :, :], [P, U, NKEYS, K8], 2),
                                           iota[:, :].unsqueeze(1).unsqueeze(3).broadcast_to([P, U, NKEYS, K8]),
                                           ALU.is_equal))
                    c.sync()
                if part == 4:
                    c.do(dve.tensor_tensor(hot_y[:, :, :, :].rearrange("p u j b -> p (u j) b"),
                                           hot_y[:, :, :, :].rearrange("p u j b -> p (u j) b"),
                                           rankw[:, :].unsqueeze(1).broadcast_to([P, U * NKEYS, K8]), ALU.mult))
                    c.do(dve.tensor_tensor(hot_x[:, :, :, :], hot_x[:, :, :, :], wide(picks[:, :, :], [P, U, LOWKEYS, K8], 2),
                                           ALU.mult))
                    c.sync()
                    c.do(dve.reduce_sum(rank[:, :, :], hot_y[:, :, :, :], AX))
                    c.do(dve.reduce_sum(need[:, :, :], hot_x[:, :, :, :], AX))
                    c.sync()
                if part == 5:
                    dve.wait_ge(exp_done, b + 1)
                    c.step(dve.tensor_tensor(rest[:, :, :, :].rearrange("p u a b -> p u (a b)"), ex[:, :, PR],
                                             pick[:, :, :, :].rearrange("p u a b -> p u (a b)"), ALU.mult))
                    c.step(dve.reduce_sum(mass[:, :, :], rest[:, :, :, :], AX))
                    c.step(dve.reduce_sum(zsum[:, :], mass[:, :, :], AX))
                    c.do(dve.reciprocal(rz[:, :], zsum[:, :]))
                    c.step(dve.scalar_tensor_tensor(mass[:, :, :], ixf[:, :, :], LOWKEYS - 0.5, mass[:, :, :], ALU.is_ge, ALU.mult))
                    c.do(dve.reduce_sum(hi[:, :], mass[:, :, :], AX))
                    c.step(dve.tensor_tensor(arg[:, :, LO], ex[:, :, LO], rz[:, :].unsqueeze(2).broadcast_to([P, U, LOWKEYS]), ALU.mult))
                    c.step(dve.tensor_tensor(hi[:, :], hi[:, :], rz[:, :], ALU.mult))
                if part == 6:
                    c.do(dve.tensor_tensor(dense[:, :, :, :], wide(rank[:, :, :], [P, U, LOWKEYS, NKEYS], 2),
                                           wide(need[:, :, :], [P, U, LOWKEYS, NKEYS], 3), ALU.add))
                    c.do(dve.tensor_tensor(wts[:, :, :, :], wide(ex[:, :, HI], [P, U, LOWKEYS, NKEYS], 2),
                                           wide(arg[:, :, LO], [P, U, LOWKEYS, NKEYS], 3), ALU.mult))
                    c.sync()
                if part == 7:
                    c.step(dve.scalar_tensor_tensor(wts[:, :, :, :], dense[:, :, :, :], K8 + 0.5, wts[:, :, :, :],
                                                    ALU.is_gt, ALU.mult))
                    lastw = wts[:, :, LOWKEYS - 1, NKEYS - 1]
                    dve.tensor_tensor(lastw, lastw, hi[:, :], ALU.add).then_inc(w_ready, 1)
                    c.end()

            def add_to_x(b):
                dve.wait_ge(down_done, NCH * (b + 1) + RING)
                for k in range(2):
                    xk = x[:, bass.ds(4 * b + 2 * k, 2), :]
                    last = dve.tensor_tensor(xk, xk, ps[:, 4 + k, :].rearrange("p (t d) -> p t d", t=2), ALU.add)
                last.then_inc(x_done, 1)

            def batch_row(b, before, following):
                if before is not None:
                    c.resume(b)
                for j in range(NCH):
                    product(b, j)
                    if before is not None and j == LAG - 1:
                        add_to_x(before)
                    if before is None and j < FC:
                        route(b, j)
                    if before is not None and j < FC - EC:
                        route(b, EC + j)
                    if following is not None and j >= FC:
                        route(following, j - FC)

            batch_row(0, None, 1)
            with dve.Fori(1, B - 1) as b:
                batch_row(b, b - 1, b + 1)
            batch_row(B - 1, B - 2, None)
            add_to_x(B - 1)



PARTS = [0, 0, 1, 0, 1, 2]
K_PARTS = [0, 1, 0, 2, 1, 0]
STACK = 16 * len(PARTS)
SLOT = 32


def stack_rows(causal):
    first = STACK + (3 if causal else 0)
    return first, first + 3


class HeadStacks:

    def __init__(self, nc, name, key_heads, s):
        self.qs = s.sb("qs", [P, B, HEADS, T], BF16)
        self.ks = s.sb("ks", [P, B, key_heads, T], BF16)
        self.vv = s.sb("v", [P, B, NT, key_heads * HD])
        self.q_dram = nc.dram_tensor(name + "_q_parts", [B, D, 3, T], BF16).ap()
        self.k_dram = nc.dram_tensor(name + "_k_parts", [B, key_heads * HD, 3, T], BF16).ap()
        self.stack_loaded = s.sem("stack_loaded")

    def load_row(self, sp, b):
        for dst, dram, which in [(self.qs, self.q_dram, PARTS), (self.ks, self.k_dram, K_PARTS)]:
            for i, p in enumerate(which):
                sp.dma_start(dst[16 * i:16 * i + 16, b, :, :],
                             dram[b, :, p, :].rearrange("(h p) n -> p h n", p=HD)).then_inc(self.stack_loaded, 16)


def stack_count(causal, b):
    return 16 * (3 if causal else 1) * B + 16 * 2 * len(PARTS) * (b + 1)


def project_heads(nc, name, g, w, causal, qkv):
    x, ps, ident = g["x"], g["ps"], g["ident"]
    KH = HEADS if causal else 4
    R1, R2 = stack_rows(causal)
    NQ, NK = 2, KH * HD // P if causal else 1
    KP = min(P, KH * HD)
    NCH = NQ + NK
    NG = 2 if causal else 3
    CREDIT = 1
    with ExitStack() as stack:
        s = Scope(nc, name, stack, g["to_clear"])
        nb = NormBuffers(s)
        xn = s.sb("xn", [P, NT, D])
        xT = s.sb("xT", [P, DC, T])
        qk = s.sb("qk", [P, NCH, T])
        rot = None if causal else s.sb("rot", [P, T])
        part = s.sb("part", [P, 3, NCH, T], BF16)
        qs, ks, vv, stack_loaded = qkv.qs, qkv.ks, qkv.vv, qkv.stack_loaded
        norm_steps = s.sem("norm_steps")
        xn_ready, transposed, xt_ready = s.sem("xn_ready"), s.sem("transposed"), s.sem("xt_ready")
        proj_ready, proj_free = s.sem("proj_ready"), s.sem("proj_free")
        v_ready, v_free = s.sem("v_ready"), s.sem("v_free")
        qk_ready, rot_steps = s.sem("qk_ready"), s.sem("rot_steps")
        hi_ready, rest_ready, mid_ready, parts_ready = (s.sem("hi_ready"), s.sem("rest_ready"), s.sem("mid_ready"),
                                                        s.sem("parts_ready"))
        parts_stored, sp_waits = s.sem("parts_stored"), s.sem("sp_waits")
        block = stack.enter_context(nc.Block())


        @block.sync
        def _(sp):
            sp.sem_inc(parts_stored, CREDIT)
            for b in range(B):
                if causal:
                    sp.dma_start(ks[STACK:R1, b, :, :], w["bias_rows"]).then_inc(stack_loaded, 16)
                    sp.dma_start(qs[STACK:R1, b, :, :], w["one_rows"]).then_inc(stack_loaded, 16)
                sp.dma_start(ks[R1:R2, b, :, :], w["one_rows"][:, 0:KH, :]).then_inc(stack_loaded, 16)

            def hold(sem, value):
                sp.wait_ge(sem, value)
                sp.sem_inc(sp_waits, 1)

            def store_row(b):
                for ch in range(NCH):
                    dram, c, rows_ = (qkv.q_dram, ch, P) if ch < NQ else (qkv.k_dram, ch - NQ, KP)
                    hold(parts_ready, NCH * b + ch + 1 + NCH)
                    sp.dma_start(dram[b, c * P:c * P + rows_, :, :], part[0:rows_, :, ch, :]).then_inc(parts_stored, 16)
                hold(parts_stored, 16 * NCH * (b + 1) + CREDIT)

            with sp.Fori(0, B - 1) as b:
                store_row(b)
                hold(stack_loaded, stack_count(causal, b - 1))
                qkv.load_row(sp, b)
            store_row(B - 1)

        @block.gpsimd
        def _(pool):
            pool.sem_inc(parts_ready, NCH)

            def chunk(ch):
                p = P if ch < NQ else KP
                return qk[0:p, ch, :], part[0:p, 0, ch, :], part[0:p, 1, ch, :], part[0:p, 2, ch, :], p

            with pool.Fori(0, B) as b:
                if causal:
                    for ch in range(NCH):
                        rest, _, mid, lo, _ = chunk(ch)
                        pool.wait_ge(mid_ready, NCH * b + ch + 1)
                        pool.tensor_tensor(lo, rest, mid, ALU.subtract).then_inc(parts_ready, 1)
                else:
                    for ch in range(NCH + 1):
                        if ch < NCH:
                            f, hi_, _, _, _ = chunk(ch)
                            pool.wait_ge(hi_ready, NCH * b + ch + 1)
                            pool.tensor_tensor(f, f, hi_, ALU.subtract).then_inc(rest_ready, 1)
                        if ch >= 1:
                            rest, _, mid, lo, _ = chunk(ch - 1)
                            pool.wait_ge(mid_ready, NCH * b + ch)
                            pool.tensor_tensor(lo, rest, mid, ALU.subtract).then_inc(parts_ready, 1)

        @block.tensor
        def _(pe):
            pe.sem_inc(proj_free, NG)
            pe.sem_inc(v_free, 1)
            pe.wait_ge(g["loaded"], g["loads"][w["key"]])
            if causal:
                groups = [[(w["wq"], 0, P), (w["wq"], P, P)], [(w["wk"], 0, P), (w["wk"], P, P)]]
            else:
                groups = [[(w["wq"], 0, P), (w["wq2"], 0, P)], [(w["wq"], P, P), (w["wq2"], P, P)],
                          [(w["wk"], 0, KP), (w["wk2"], 0, KP)]]
            n_v = KH * HD
            with pe.Fori(0, B) as b:
                pe.wait_ge(xn_ready, b + 1)
                pe.wait_ge(v_free, b + 1)
                transpose_row(pe, ps, 0, xn, ident).then_inc(transposed, 1)
                pe.wait_ge(xt_ready, b + 1)
                for n, group in enumerate(groups):
                    pe.wait_ge(proj_free, NG * b + n + 1)
                    for k, (wt, f0, fn) in enumerate(group):
                        for c in range(DC):
                            last = pe.matmul(ps[0:fn, 2 + 2 * n + k, :], wt[:, c, f0:f0 + fn], xT[:, c, :],
                                             start=c == 0, stop=c == DC - 1)
                    last.then_inc(proj_ready, 1)
                for t in range(NT):
                    col = t * n_v
                    for c in range(DC):
                        last = pe.matmul(ps[:, col // T, col % T:col % T + n_v], xT[:, c, t * P:(t + 1) * P],
                                         w["wv"][:, c, :], start=c == 0, stop=c == DC - 1)
                last.then_inc(v_ready, 1)

        @block.scalar
        def _(act):
            def copy_transposed(b):
                act.wait_ge(transposed, b + 1)
                act.activation(xT[:, :, :], ps[:, 0:2, :], ACT.Copy).then_inc(xt_ready, 1)

            def cut(b):
                act.wait_ge(parts_stored, 16 * NCH * b + CREDIT)
                for ch in range(NCH + 1):
                    if ch < NCH and causal:
                        if ch % 2 == 0:
                            act.wait_ge(proj_ready, NG * b + ch // 2 + 1)
                        act.activation(part[:, 0, ch, :], ps[:, 2 + ch, :], ACT.Identity,
                                       bias=w["bqk"][:, ch:ch + 1]).then_inc(hi_ready, 1)
                    elif ch < NCH:
                        p = P if ch < NQ else KP
                        act.wait_ge(qk_ready, NCH * b + ch + 1)
                        act.activation(part[0:p, 0, ch, :], qk[0:p, ch, :], ACT.Copy).then_inc(hi_ready, 1)
                    if ch >= 1:
                        p = P if ch - 1 < NQ else KP
                        act.wait_ge(rest_ready, NCH * b + ch)
                        act.activation(part[0:p, 1, ch - 1, :], qk[0:p, ch - 1, :], ACT.Copy).then_inc(mid_ready, 1)

            act.wait_ge(g["loaded"], g["loads"][w["key"]])
            with act.Fori(0, B) as b:
                copy_transposed(b)
                cut(b)

        @block.vector
        def _(dve):
            c = Chain(dve, norm_steps, NormBuffers.STEPS)

            cr = Chain(dve, rot_steps, 9)

            def normalise(b):
                c.start(b)
                norm_stats(dve, c, g, b, nb)
                c.end()

            def take(b):
                if causal:
                    for ch in range(NCH):
                        dve.wait_ge(parts_ready, NCH * b + ch + 1)
                        dve.wait_ge(hi_ready, NCH * b + ch + 1)
                        dve.scalar_tensor_tensor(qk[:, ch, :], ps[:, 2 + ch, :], w["bqk"][:, ch:ch + 1], part[:, 0, ch, :],
                                                 ALU.add, ALU.subtract).then_inc(rest_ready, 1)
                        if ch % 2 == 1:
                            dve.wait_ge(rest_ready, NCH * b + ch + 1)
                            dve.sem_inc(proj_free, 1)
                else:
                    cr.start(b)
                    for n in range(NG):
                        p = P if n < NQ else KP
                        q = qk[0:p, n, :]
                        dve.wait_ge(parts_ready, NCH * b + n + 1)
                        dve.wait_ge(proj_ready, NG * b + n + 1)
                        cr.do(dve.tensor_tensor(q, ps[0:p, 2 + 2 * n, :], w["cos"][0:p, :], ALU.mult))
                        cr.step(dve.tensor_tensor(rot[0:p, :], ps[0:p, 3 + 2 * n, :], w["sin"][0:p, :], ALU.mult))
                        dve.sem_inc(proj_free, 1)
                        cr.step(dve.tensor_tensor(q, q, rot[0:p, :], ALU.add))
                        dve.sem_inc(qk_ready, 1)
                    cr.end()
                dve.wait_ge(v_ready, b + 1)
                src = ps[:, 0:2, :].rearrange("p b n -> p (b n)")[:, 0:NT * KH * HD].rearrange("p (t n) -> p t n", t=NT)
                if causal:
                    dve.tensor_tensor(vv[:, b, :, :], src, w["bv"][:, :].unsqueeze(1).broadcast_to([P, NT, KH * HD]),
                                      ALU.add).then_inc(v_free, 1)
                else:
                    dve.tensor_copy(vv[:, b, :, :], src).then_inc(v_free, 1)

            if causal:
                dve.wait_ge(g["x0_loaded"], 16)
            normalise(0)
            norm_apply(dve, x, 0, nb, xn).then_inc(xn_ready, 1)
            dve.wait_ge(g["loaded"], g["loads"][w["key"]])
            with dve.Fori(1, B) as b:
                normalise(b)
                dve.wait_ge(transposed, b)
                norm_apply(dve, x, b, nb, xn).then_inc(xn_ready, 1)
                take(b - 1)
            take(B - 1)


def attend(nc, name, g, w, causal, qkv):
    qs, ks, vv, stack_loaded = qkv.qs, qkv.ks, qkv.vv, qkv.stack_loaded
    x, ps, ident, identb = g["x"], g["ps"], g["ident"], g["identb"]
    KH = HEADS if causal else 4
    R1, R2 = stack_rows(causal)
    with ExitStack() as stack:
        s = Scope(nc, name, stack, g["to_clear"])
        negm = s.sb("negm", [P, NT, HEADS])
        mrest = s.sb("mrest", [HEADS, T])
        mpart = s.sb("mpart", [HEADS, 3, T], BF16)
        mpart_dram = nc.dram_tensor(name + "_maxima", [HEADS, 3, T], BF16).ap()
        va = s.sb("va", [P, NT, KH, SLOT])
        pr = s.sb("probs", [P, 8, T])
        ctxs = s.sb("ctxs", [P, T])
        rden = s.sb("rden", [P, NT, 4])
        ctx = s.sb("ctx", [P, NT, D])
        ctxT = s.sb("ctxT", [P, DC, T])

        den_steps, m_steps = s.sem("den_steps"), s.sem("m_steps")
        va_init, va_ready, biased = s.sem("va_init"), s.sem("va_ready"), s.sem("biased")
        r1_ready, r1_free = s.sem("r1_ready"), s.sem("r1_free")
        m_stored, sp_waits, mpart_ready, m_loaded = s.sem("m_stored"), s.sem("sp_waits"), s.sem("mpart_ready"), s.sem("m_loaded")
        s_ready, exp_done, pv_done = s.sem("s_ready"), s.sem("exp_done"), s.sem("pv_done")
        ctx_out, flipped, normalised = s.sem("ctx_out"), s.sem("flipped"), s.sem("normalised")
        merged, ctxt_ready, out_ready, x_done = s.sem("merged"), s.sem("ctxt_ready"), s.sem("out_ready"), s.sem("x_done")
        block = stack.enter_context(nc.Block())

        PAIRS = HEADS // 2 * NT
        PER1 = PAIRS + 2
        STEPS2 = 4 * NT
        CREDIT = 1
        SPAN, MAX_AT = 13, 14
        TAIL = 2

        def pairs_at(k):
            return range(PAIRS * k // SPAN, PAIRS * (k + 1) // SPAN) if k < SPAN else range(0)

        def rounds(eng, body):
            body(0, None)
            with eng.Fori(1, B) as i:
                body(i, i - 1)
            body(None, B - 1)

        def bank1(pos):
            return 2 * (pos % 2)

        def width1(qt):
            return (qt + 1) * P if causal else T

        def width2(kt):
            return T - kt * P if causal else T

        @block.sync
        def _(sp):
            def hold(sem, value):
                sp.wait_ge(sem, value)
                sp.sem_inc(sp_waits, 1)

            sp.sem_inc(m_loaded, CREDIT)
            hold(stack_loaded, stack_count(causal, B - 2))
            qkv.load_row(sp, B - 1)
            with sp.Fori(0, B) as b1:
                hold(mpart_ready, b1 + 1)
                sp.dma_start(mpart_dram, mpart[:, :, :]).then_inc(m_stored, 16)
                hold(m_stored, 16 * (b1 + 1))
                sp.dma_start(qs[R1:R2, b1, :, :], mpart_dram.rearrange("h i n -> i h n")).then_inc(m_loaded, 16)
            sp.wait_ge(m_loaded, 16 * B + CREDIT)

        if causal:
            @block.gpsimd
            def _(pool):
                pool.wait_ge(g["loaded"], g["loads"][w["key"]])
                with pool.Fori(0, B) as b:
                    xb = x[:, bass.ds(4 * b, NT), :]
                    pool.tensor_tensor(xb, xb, w["bo"][:, :].unsqueeze(1).broadcast_to([P, NT, D]),
                                       ALU.add).then_inc(biased, 1)

        @block.tensor
        def _(pe):
            pe.sem_inc(pv_done, 2)
            pe.wait_ge(g["loaded"], g["loads"][w["key"]])

            def item(b1, pos):
                pe.wait_ge(r1_free, PER1 * b1 + pos + 1)

            def score_pair(b1, n):
                hp, qt = n // NT, n % NT
                item(b1, n)
                for k in range(2):
                    hd = 2 * hp + k
                    last = pe.matmul(ps[:, bank1(n) + k, 0:width1(qt)], qs[0:R1, b1, hd, qt * P:(qt + 1) * P],
                                     ks[0:R1, b1, hd % KH, 0:width1(qt)], start=True, stop=True)
                    if causal:
                        last = pe.matmul(ps[:, bank1(n) + k, qt * P:(qt + 1) * P], identb[:, :], w["mask_qk"][:, :],
                                         start=False, stop=True, skip_group_check=True)
                last.then_inc(r1_ready, 1)

            def maxima(b1):
                pe.wait_ge(r1_free, PER1 * b1 + PAIRS + 2)
                for qt in range(NT):
                    last = pe.transpose(ps[0:HEADS, bank1(PAIRS), qt * P:(qt + 1) * P], negm[:, qt, :], ident[:, :])
                last.then_inc(r1_ready, 2)

            def scores_t(b2, k, js):
                grp, kt = k // NT, k % NT
                for j in js:
                    hd, m = 4 * grp + j, 4 * k + j
                    pe.wait_ge(exp_done, 4 * STEPS2 * b2 + m + 1)
                    last = pe.matmul(ps[:, 4 + j % 2, 0:width2(kt)], ks[0:R2, b2, hd % KH, kt * P:(kt + 1) * P],
                                     qs[0:R2, b2, hd, T - width2(kt):T], start=True, stop=True)
                    if causal:
                        last = pe.matmul(ps[:, 4 + j % 2, 0:P], identb[:, :], w["mask_kq"][:, :],
                                         start=False, stop=True, skip_group_check=True)
                    last.then_inc(s_ready, 1)

            def context(b2, k):
                grp, kt = k // NT, k % NT
                pe.wait_ge(exp_done, 4 * STEPS2 * b2 + 4 * k + 4 + 2)
                if kt == 0:
                    pe.wait_ge(ctx_out, 4 * b2 + grp + 1)
                if k == 0:
                    pe.wait_ge(x_done, b2 + 1)
                    pe.wait_ge(va_ready, b2 + 1)
                for j in range(4):
                    hd = 4 * grp + j
                    last = pe.matmul(ps[SLOT * j:SLOT * (j + 1), 6, T - width2(kt):T], va[:, kt, hd % KH, :],
                                     pr[:, 4 * (k % 2) + j, 0:width2(kt)], start=kt == 0, stop=kt == NT - 1,
                                     skip_group_check=True)
                last.then_inc(pv_done, 1)

            def flip(b2, grp):
                pe.wait_ge(ctx_out, 4 * b2 + grp + 2)
                pe.wait_ge(normalised, 4 * b2 + grp + 1)
                for t in range(NT):
                    last = pe.transpose(ps[:, 7, t * P:(t + 1) * P], ctxs[:, t * P:(t + 1) * P], ident[:, :])
                last.then_inc(flipped, 1)

            def merge(b2):
                pe.wait_ge(normalised, 4 * b2 + 5)
                transpose_row(pe, ps, 6, ctx, ident).then_inc(merged, 1)

            def project_out(b2):
                pe.wait_ge(ctxt_ready, b2 + 1)
                for t in range(NT):
                    for c in range(DC):
                        last = pe.matmul(ps[:, 6 + t // 2, (t % 2) * D:(t % 2 + 1) * D], ctxT[:, c, t * P:(t + 1) * P],
                                         w["wo"][:, c, :], start=c == 0, stop=c == DC - 1)
                last.then_inc(out_ready, 1)

            def body(b1, b2):
                if b1 is not None:
                    pe.wait_ge(stack_loaded, stack_count(causal, b1))
                if b2 is not None:
                    pe.wait_ge(m_loaded, 16 * (b2 + 1) + CREDIT)
                for k in range(STEPS2 + TAIL):
                    if b1 is not None and k == MAX_AT:
                        maxima(b1)
                    pairs = list(pairs_at(k)) if b1 is not None else []
                    if b2 is not None and k < STEPS2:
                        scores_t(b2, k, (0, 1))
                    if b2 is not None and 1 <= k <= STEPS2:
                        context(b2, k - 1)
                    for n in pairs[0:1]:
                        score_pair(b1, n)
                    if b2 is not None and k < STEPS2:
                        scores_t(b2, k, (2, 3))
                    if b2 is not None and k >= NT and k % NT == 1:
                        flip(b2, k // NT - 1)
                    for n in pairs[1:]:
                        score_pair(b1, n)
                if b2 is not None:
                    merge(b2)
                    project_out(b2)

            pe.wait_ge(va_init, 2)
            rounds(pe, body)

        @block.scalar
        def _(act):
            act.sem_inc(exp_done, 2)
            act.sem_inc(ctx_out, 1)
            act.sem_inc(flipped, 1)

            def copy_context(b2, grp):
                act.wait_ge(pv_done, 4 * (4 * b2 + grp) + 4 + 2)
                act.wait_ge(flipped, 4 * b2 + grp + 1)
                act.activation(ctxs[:, :], ps[:, 6, :], ACT.Copy).then_inc(ctx_out, 1)

            with act.Fori(0, B) as b2:
                act.wait_ge(pv_done, STEPS2 * b2 + 2)
                act.activation(va[:, :, :, 0:HD], vv[:, b2, :, :].rearrange("p t (h d) -> p t h d", h=KH),
                               ACT.Copy).then_inc(va_ready, 1)
                for k in range(STEPS2):
                    act.wait_ge(pv_done, STEPS2 * b2 + k + 1)
                    for j in range(4):
                        act.wait_ge(s_ready, 4 * (STEPS2 * b2 + k) + j + 1)
                        act.activation(pr[:, 4 * (k % 2) + j, 0:width2(k % NT)], ps[:, 4 + j % 2, 0:width2(k % NT)],
                                       ACT.Exp, scale=HD ** -0.5).then_inc(exp_done, 1)
                    if k >= NT and k % NT == 0:
                        copy_context(b2, k // NT - 1)
                copy_context(b2, 3)
                act.wait_ge(merged, b2 + 1)
                act.activation(ctxT[:, :, :], ps[:, 6:8, :], ACT.Copy).then_inc(ctxt_ready, 1)

        @block.vector
        def _(dve):
            dve.sem_inc(r1_free, 2)
            dve.sem_inc(normalised, 1)
            dve.sem_inc(x_done, 1)
            dve.memset(va[:, :, :, HD:SLOT], 0.0).then_inc(va_init, 1)
            dve.wait_ge(va_init, 1)
            dve.memset(va[:, :, :, HD:HD + 1], 1.0).then_inc(va_init, 1)
            cden = Chain(dve, den_steps, 1)
            cm = Chain(dve, m_steps, 4)

            def take(b1, pos):
                dve.wait_ge(r1_ready, PER1 * b1 + pos + 1)

            def row_max(b1, n):
                hp, qt = n // NT, n % NT
                take(b1, n)
                dve.tensor_reduce(negm[:, qt, 2 * hp:2 * hp + 2], ps[:, bank1(n):bank1(n) + 2, 0:width1(qt)],
                                  AX, ALU.max, negate=True).then_inc(r1_free, 1)

            def max_rows(b1):
                take(b1, PAIRS)
                dve.wait_ge(m_loaded, 16 * b1 + CREDIT)
                cm.start(b1)
                m = ps[0:HEADS, bank1(PAIRS), :]
                cm.step(dve.tensor_copy(mpart[:, 0, :], m))
                cm.step(dve.tensor_tensor(mrest[:, :], m, mpart[:, 0, :], ALU.subtract))
                dve.sem_inc(r1_free, 2)
                cm.step(dve.tensor_copy(mpart[:, 1, :], mrest[:, :]))
                cm.step(dve.tensor_tensor(mpart[:, 2, :], mrest[:, :], mpart[:, 1, :], ALU.subtract))
                cm.end()
                dve.sem_inc(mpart_ready, 1)

            def normalise(b2, grp):
                dve.wait_ge(flipped, 4 * b2 + grp + 2)
                cden.start(4 * b2 + grp)
                got = ps[:, 7, :].rearrange("p (t j s) -> p t j s", t=NT, j=4)
                cden.step(dve.reciprocal(rden[:, :, :], got[:, :, :, HD]))
                dve.tensor_tensor(ctx[:, :, 4 * HD * grp:4 * HD * (grp + 1)].rearrange("p t (j d) -> p t j d", j=4),
                                  got[:, :, :, 0:HD], rden[:, :, :].unsqueeze(3).broadcast_to([P, NT, 4, HD]),
                                  ALU.mult).then_inc(normalised, 1)

            def add_to_x(b2):
                dve.wait_ge(out_ready, b2 + 1)
                if causal:
                    dve.wait_ge(biased, B)
                xb = x[:, bass.ds(4 * b2, NT), :]
                dve.tensor_tensor(xb, xb, ps[:, 6:8, :].rearrange("p b (t d) -> p (b t) d", t=2),
                                  ALU.add).then_inc(x_done, 1)

            def body(b1, b2):
                for k in range(STEPS2 + TAIL):
                    if b1 is not None and k == MAX_AT:
                        max_rows(b1)
                    if b2 is not None and k >= NT and k % NT == 1:
                        normalise(b2, k // NT - 1)
                    if b1 is not None:
                        for n in pairs_at(k):
                            row_max(b1, n)
                if b2 is not None:
                    add_to_x(b2)

            rounds(dve, body)



def feature_attention(nc, name, g):
    x, ps, ident = g["x"], g["ps"], g["ident"]
    with ExitStack() as stack:
        s = Scope(nc, name, stack, g["to_clear"])
        nb = NormBuffers(s)
        xn = s.sb("xn", [P, NT, D])
        xT = s.sb("xT", [P, DC, T])
        negm = s.sb("negm", [P, DC])
        pr = s.sb("probs", [P, DC, D])
        den, rden = s.sb("den", [P, DC]), s.sb("rden", [P, DC])
        attT = s.sb("attT", [P, DC, D])
        norm_steps, soft_steps = s.sem("norm_steps"), s.sem("soft_steps")
        xn_ready, e_ready, tr_ready, xt_ready = s.sem("xn_ready"), s.sem("e_ready"), s.sem("tr_ready"), s.sem("xt_ready")
        max_ready, exp_done, att_ready, at_ready = s.sem("max_ready"), s.sem("exp_done"), s.sem("att_ready"), s.sem("at_ready")
        attt_ready, out_ready, x_done = s.sem("attt_ready"), s.sem("out_ready"), s.sem("x_done")
        block = stack.enter_context(nc.Block())


        @block.tensor
        def _(pe):
            pe.sem_inc(exp_done, 2)
            pe.wait_ge(g["loaded"], g["loads"]["ident"])

            def energy(b):
                pe.wait_ge(xn_ready, b + 1)
                pe.wait_ge(exp_done, 2 * b + 2)
                for i in range(DC):
                    for t in range(NT):
                        last = pe.matmul(ps[:, 0, i * D:(i + 1) * D], xn[:, t, i * P:(i + 1) * P], xn[:, t, :],
                                         start=t == 0, stop=t == NT - 1)
                last.then_inc(e_ready, 1)

            def result(b):
                pe.wait_ge(att_ready, b + 1)
                for j in range(DC):
                    for i in range(DC):
                        last = pe.transpose(ps[:, 3, j * D + i * P:j * D + (i + 1) * P], pr[:, i, j * P:(j + 1) * P],
                                            ident[:, :])
                last.then_inc(at_ready, 1)
                pe.wait_ge(xt_ready, b + 1)
                pe.wait_ge(attt_ready, b + 1)
                pe.wait_ge(x_done, b + 1)
                for t in range(NT):
                    for j in range(DC):
                        last = pe.matmul(ps[:, 4 + t // 2, (t % 2) * D:(t % 2 + 1) * D], xT[:, j, t * P:(t + 1) * P],
                                         attT[:, j, :], start=j == 0, stop=j == DC - 1)
                last.then_inc(out_ready, 1)

            energy(0)
            transpose_row(pe, ps, 1, xn, ident).then_inc(tr_ready, 1)
            with pe.Fori(1, B) as b:
                energy(b)
                result(b - 1)
                transpose_row(pe, ps, 1, xn, ident).then_inc(tr_ready, 1)
            result(B - 1)

        @block.scalar
        def _(act):
            def exp_and_copy(b):
                act.wait_ge(max_ready, b + 1)
                for i in range(DC):
                    act.activation(pr[:, i, :], ps[:, 0, i * D:(i + 1) * D], ACT.Exp, bias=negm[:, i:i + 1],
                                   accum_out=den[:, i:i + 1]).then_inc(exp_done, 1)
                act.wait_ge(tr_ready, b + 1)
                act.activation(xT[:, :, :], ps[:, 1:3, :], ACT.Copy).then_inc(xt_ready, 1)

            def copy_attention(b):
                act.wait_ge(at_ready, b + 1)
                act.activation(attT[:, :, :], ps[:, 3, :].rearrange("p (j i) -> p j i", j=DC), ACT.Copy).then_inc(attt_ready, 1)

            exp_and_copy(0)
            with act.Fori(1, B) as b:
                copy_attention(b - 1)
                exp_and_copy(b)
            copy_attention(B - 1)

        @block.vector
        def _(dve):
            dve.sem_inc(x_done, 1)
            cn = Chain(dve, norm_steps, NormBuffers.STEPS)
            cs = Chain(dve, soft_steps, 1)

            def normalise(b):
                cn.start(b)
                norm_stats(dve, cn, g, b, nb)
                cn.end()

            def add_to_x(b):
                dve.wait_ge(out_ready, b + 1)
                xb = x[:, bass.ds(4 * b, NT), :]
                dve.tensor_tensor(xb, xb, ps[:, 4:6, :].rearrange("p k (t d) -> p (k t) d", t=2), ALU.add).then_inc(x_done, 1)

            def batch_row(b, following, before):
                dve.wait_ge(e_ready, b + 1)
                dve.tensor_reduce(negm[:, :], ps[:, 0, :].rearrange("p (i j) -> p i j", i=DC), AX, ALU.max,
                                  negate=True).then_inc(max_ready, 1)
                if following is not None:
                    normalise(following)
                dve.wait_ge(exp_done, 2 * b + 4)
                cs.start(b)
                cs.step(dve.reciprocal(rden[:, :], den[:, :]))
                for i in range(DC):
                    last = dve.tensor_scalar(pr[:, i, :], pr[:, i, :], rden[:, i:i + 1], None, ALU.mult)
                last.then_inc(att_ready, 1)
                if following is not None:
                    dve.wait_ge(tr_ready, b + 1)
                    norm_apply(dve, x, following, nb, xn).then_inc(xn_ready, 1)
                if before is not None:
                    add_to_x(before)

            normalise(0)
            norm_apply(dve, x, 0, nb, xn).then_inc(xn_ready, 1)
            batch_row(0, 1, None)
            with dve.Fori(1, B - 1) as b:
                batch_row(b, b + 1, b - 1)
            batch_row(B - 1, None, B - 2)
            add_to_x(B - 1)



def gated_scan(nc, name, g, w_act, w_val, w_rec, key):
    x, ps, ident = g["x"], g["ps"], g["ident"]
    with ExitStack() as outer:
        so = Scope(nc, name, outer)
        zz = so.sb("z", [P, 2, B, T])
        r4 = so.sb("r4", [P, B, NT * D])
        kv = so.sb("kv", [P, 2, 2, T])
        with ExitStack() as stack:
            s = Scope(nc, name + "g", stack)
            nb = NormBuffers(s)
            xn = s.sb("xn", [P, NT, D])
            xT = s.sb("xT", [P, DC, T + 1])
            z = s.sb("zrow", [P, 2, T])
            sq = s.sb("sq", [P, 2, T])
            mag, peak, rpeak = s.sb("mag", [P, T]), s.sb("peak", [P, T]), s.sb("rpeak", [P, T])
            rr = s.sb("rr", [P, NT * D])
            norm_steps, z_steps = s.sem("norm_steps"), s.sem("z_steps")
            zero_done = s.sem("zero_done")
            xn_ready, transposed, xt_ready = s.sem("xn_ready"), s.sem("transposed"), s.sem("xt_ready")
            act_ready, rec_ready = s.sem("act_ready"), s.sem("rec_ready")
            zsig_done, rsig_done = s.sem("zsig_done"), s.sem("rsig_done")
            sq_ready, mag_done, z_done = s.sem("sq_ready"), s.sem("mag_done"), s.sem("z_done")
            block = stack.enter_context(nc.Block())


            @block.tensor
            def _(pe):
                pe.sem_inc(zsig_done, 1)
                pe.sem_inc(rsig_done, 1)
                pe.wait_ge(g["loaded"], g["loads"][key])
                pe.wait_ge(zero_done, 1)
                with pe.Fori(0, B) as b:
                    pe.wait_ge(xn_ready, b + 1)
                    transpose_row(pe, ps, 0, xn, ident).then_inc(transposed, 1)
                    pe.wait_ge(xt_ready, b + 1)
                    pe.wait_ge(zsig_done, b + 1)
                    for part in range(2):
                        for k in range(2 * DC):
                            shift = k // DC
                            last = pe.matmul(ps[:, 2 + part, :], w_act[:, k, part * P:(part + 1) * P],
                                             xT[:, k % DC, shift:shift + T], start=k == 0, stop=k == 2 * DC - 1)
                    last.then_inc(act_ready, 1)
                    pe.wait_ge(rsig_done, b + 1)
                    for t in range(NT):
                        for k in range(2 * DC):
                            c0 = t * P + k // DC
                            last = pe.matmul(ps[:, 4 + t // 2, (t % 2) * D:(t % 2 + 1) * D], xT[:, k % DC, c0:c0 + P],
                                             w_rec[:, k, :], start=k == 0, stop=k == 2 * DC - 1)
                    last.then_inc(rec_ready, 1)

            @block.scalar
            def _(act):
                act.sem_inc(z_done, 1)

                def copy_transposed(b):
                    act.wait_ge(transposed, b + 1)
                    act.activation(xT[:, :, 1:T + 1], ps[:, 0:DC, :], ACT.Copy).then_inc(xt_ready, 1)

                def sigmoid_z(b):
                    act.wait_ge(act_ready, b + 1)
                    act.wait_ge(z_done, b + 1)
                    act.activation(z[:, :, :], ps[:, 2:4, :], ACT.Sigmoid).then_inc(zsig_done, 1)

                def sigmoid_r(b):
                    act.wait_ge(rec_ready, b + 1)
                    act.activation(rr[:, :], ps[:, 4:6, :].rearrange("p b n -> p (b n)"), ACT.Sigmoid).then_inc(rsig_done, 1)

                def magnitude(b):
                    act.wait_ge(sq_ready, b + 1)
                    act.activation(mag[:, :], sq[:, 0, :], ACT.Sqrt).then_inc(mag_done, 1)

                copy_transposed(0)
                sigmoid_z(0)
                with act.Fori(1, B) as b:
                    copy_transposed(b)
                    sigmoid_r(b - 1)
                    magnitude(b - 1)
                    sigmoid_z(b)
                sigmoid_r(B - 1)
                magnitude(B - 1)

            @block.vector
            def _(dve):
                dve.memset(xT[:, :, 0:1], 0.0).then_inc(zero_done, 1)
                cn = Chain(dve, norm_steps, NormBuffers.STEPS)
                cz = Chain(dve, z_steps, 7)

                def normalise(b):
                    cn.start(b)
                    norm_stats(dve, cn, g, b, nb)
                    cn.end()

                def gates(b):
                    cz.start(b)
                    dve.wait_ge(zsig_done, b + 2)
                    cz.step(dve.tensor_scalar(z[:, :, :], z[:, :, :], 0.5, None, ALU.max))
                    cz.step(dve.tensor_tensor(sq[:, :, :], z[:, :, :], z[:, :, :], ALU.mult))
                    dve.tensor_tensor(sq[:, 0, :], sq[:, 0, :], sq[:, 1, :], ALU.add).then_inc(sq_ready, 1)
                    dve.wait_ge(rsig_done, b + 2)
                    cz.step(dve.tensor_scalar(rr[:, :], rr[:, :], 0.5, None, ALU.max))
                    cz.step(dve.tensor_tensor(rr[:, :], rr[:, :], rr[:, :], ALU.mult))
                    cz.do(dve.tensor_tensor(r4[:, b, :], rr[:, :], rr[:, :], ALU.mult))
                    dve.wait_ge(mag_done, b + 1)
                    cz.step(dve.tensor_tensor_scan(peak[:, :], mag[:, :], mag[:, :], 0.0, ALU.max, ALU.max))
                    cz.step(dve.reciprocal(rpeak[:, :], peak[:, :]))
                    cz.end()
                    dve.tensor_tensor(zz[:, :, b, :], z[:, :, :], rpeak[:, :].unsqueeze(1).broadcast_to([P, 2, T]),
                                      ALU.mult).then_inc(z_done, 1)
                    dve.wait_ge(z_done, b + 2)

                normalise(0)
                norm_apply(dve, x, 0, nb, xn).then_inc(xn_ready, 1)
                with dve.Fori(1, B) as b:
                    normalise(b)
                    dve.wait_ge(transposed, b)
                    norm_apply(dve, x, b, nb, xn).then_inc(xn_ready, 1)
                    gates(b - 1)
                gates(B - 1)

        with ExitStack() as stack:
            s = Scope(nc, name + "s", stack)
            S1, S2 = 8, 8
            S3 = T // (S1 * S2)
            tmp = [s.sb(f"t{i}", [P, B * T]) for i in range(4)]
            scan_steps = s.sem("scan_steps")
            taken, prefix_done, kv_ready, out_ready, x_done = s.sem("taken"), s.sem("prefix_done"), s.sem("kv_ready"), s.sem("out_ready"), s.sem("x_done")
            out_steps = s.sem("out_steps")
            prod = s.sb("prod", [P, NT * D])
            row_steps = s.sem("row_steps")
            block = stack.enter_context(nc.Block())

            @block.vector
            def _(dve):
                c = Chain(dve, scan_steps, 0)
                c.start(0)

                def multiply(part, carry, shape, c=c):
                    n = int(np.prod(shape))
                    t = [a[:, 0:n] for a in tmp]
                    if len(shape) == 2:
                        t = [a.rearrange("p (a b) -> p a b", a=shape[0]) for a in t]
                    if len(shape) == 3:
                        t = [a.rearrange("p (a b c) -> p a b c", a=shape[0], b=shape[1]) for a in t]
                    for k, (i, j) in enumerate([(0, 0), (1, 1), (0, 1), (1, 0)]):
                        c.do(dve.tensor_tensor(t[k], carry(i), part(j), ALU.mult))
                    c.sync()
                    c.do(dve.tensor_tensor(part(0), t[0], t[1], ALU.subtract))
                    c.do(dve.tensor_tensor(part(1), t[2], t[3], ALU.add))
                    c.sync()

                seg = [zz[:, k, :, :].rearrange("p b (n s) -> p (b n) s", s=S1) for k in range(2)]
                for i in range(1, S1):
                    multiply(lambda k: seg[k][:, :, i], lambda k: seg[k][:, :, i - 1], (B * T // S1,))
                tot = [zz[:, k, :, :].rearrange("p b (m q s) -> p (b m) q s", s=S1, q=S2)[:, :, :, S1 - 1] for k in range(2)]
                for i in range(1, S2):
                    multiply(lambda k: tot[k][:, :, i], lambda k: tot[k][:, :, i - 1], (B * S3,))
                grp = [zz[:, k, :, :].rearrange("p b (m r) -> p b m r", m=S3)[:, :, :, S1 * S2 - 1] for k in range(2)]
                for i in range(1, S3):
                    multiply(lambda k: grp[k][:, :, i], lambda k: grp[k][:, :, i - 1], (B,))
                tot4 = [zz[:, k, :, :].rearrange("p b (m q s) -> p b m q s", s=S1, q=S2)[:, :, :, :, S1 - 1] for k in range(2)]
                multiply(lambda k: tot4[k][:, :, 1:S3, 0:S2 - 1],
                         lambda k: grp[k][:, :, 0:S3 - 1].unsqueeze(3).broadcast_to([P, B, S3 - 1, S2 - 1]),
                         (B, S3 - 1, S2 - 1))
                seg4 = [zz[:, k, :, :].rearrange("p b (n s) -> p b n s", s=S1) for k in range(2)]
                NS = T // S1
                dve.sem_inc(taken, 2)
                cr = Chain(dve, row_steps, 6)
                co = Chain(dve, out_steps, 1)

                def finish(b):
                    cr.start(b)
                    multiply(lambda k: seg4[k][:, b, 1:NS, 0:S1 - 1],
                             lambda k: seg4[k][:, b, 0:NS - 1, S1 - 1:S1].broadcast_to([P, NS - 1, S1 - 1]),
                             (NS - 1, S1 - 1), cr)
                    cr.end()
                    dve.sem_inc(prefix_done, 1)

                def add_to_x(b, r):
                    dve.wait_ge(out_ready, b + 1 + 2)
                    co.start(b)
                    co.step(dve.tensor_tensor(prod[:, :], ps[:, 2 * r:2 * r + 2, :].rearrange("p b n -> p (b n)"), r4[:, b, :], ALU.mult))
                    dve.sem_inc(taken, 1)
                    xb = x[:, bass.ds(4 * b, NT), :]
                    dve.tensor_tensor(xb, xb, prod[:, :].rearrange("p (t d) -> p t d", t=NT), ALU.add).then_inc(x_done, 1)
                    dve.wait_ge(x_done, b + 1)

                finish(0)
                finish(1)
                with dve.Fori(0, B // 2 - 1) as i:
                    for r in range(2):
                        add_to_x(2 * i + r, r)
                        finish(2 * i + 2 + r)
                for r in range(2):
                    add_to_x(B - 2 + r, r)

            @block.scalar
            def _(act):
                act.sem_inc(out_ready, 2)
                with act.Fori(0, B // 2) as i:
                    for r in range(2):
                        b = 2 * i + r
                        act.wait_ge(prefix_done, b + 1)
                        act.wait_ge(out_ready, b + 1)
                        act.activation(kv[:, r, :, :], zz[:, :, b, :], ACT.Copy).then_inc(kv_ready, 1)

            @block.tensor
            def _(pe):
                with pe.Fori(0, B // 2) as i:
                    for r in range(2):
                        b = 2 * i + r
                        pe.wait_ge(kv_ready, b + 1)
                        pe.wait_ge(taken, b + 1)
                        for t in range(NT):
                            for k in range(2):
                                last = pe.matmul(ps[:, 2 * r + t // 2, (t % 2) * D:(t % 2 + 1) * D],
                                                 kv[:, r, k, t * P:(t + 1) * P], w_val[:, k, :], start=k == 0, stop=k == 1)
                        last.then_inc(out_ready, 1)



def stages(nc, a, out):
    with ExitStack() as stack:
        def place(names, into):
            return {n: into.enter_context(nc.sbuf_tensor("sb_" + n, list(a[n].shape), a[n].dtype)) for n in names}

        x = stack.enter_context(nc.sbuf_tensor("x", [P, B * NT, D], F32))
        ps = stack.enter_context(nc.psum_tensor("ps", [P, 8, T], F32))
        loaded = stack.enter_context(nc.semaphore("loaded"))
        x0_loaded = stack.enter_context(nc.semaphore("x0_loaded"))
        common = ["ident", "identb", "iota", "rankw"]
        heads0 = ["a0_wq", "a0_wk", "a0_bqk", "a0_wv", "a0_bv"]
        att0 = ["a0_wo", "a0_bo", "mask_qk", "mask_kq"]
        ffn0 = ["f0_gate", "f0_up", "f0_down", "f0_de", "f0_ue"]
        att1 = ["a1_wq", "a1_wq2", "a1_wk", "a1_wk2", "a1_wv", "a1_wo", "cos", "sin"]
        ffn1 = ["f1_gate", "f1_up", "f1_down"]
        scan = ["s_act", "s_rec", "s_val"]

        sb, loads, issued = {}, {}, [0]
        sb.update(place(common, stack))

        def place_halves(names, into):
            return {n: Halves(*(into.enter_context(nc.sbuf_tensor(f"{n}_{part}", list(a[n].shape), F32R))
                                for part in ("high", "low"))) for n in names}

        def clear_semaphores():
            nc.clear_and_free_semaphores(g["to_clear"])
            g["to_clear"].clear()

        def w_of(prefix, names):
            return {n[len(prefix):]: sb[n] for n in names if n.startswith(prefix)}

        def load(sp, names, key):
            for n in names:
                sp.dma_start(sb[n][:], a[n]).then_inc(loaded, 16)
            issued[0] += 16 * len(names)
            loads[key] = issued[0]

        g = dict(x=x, to_clear=[], x0_loaded=x0_loaded, ps=ps, loaded=loaded, loads=loads, ident=sb["ident"], identb=sb["identb"],
                 iota=sb["iota"], rankw=sb["rankw"])

        def stacks(name, key_heads, into):
            return HeadStacks(nc, name, key_heads, Scope(nc, name, into, g["to_clear"]))

        with ExitStack() as first:
            sb.update(place(att0, first))
            qkv = stacks("attn0", HEADS, first)
            with ExitStack() as heads:
                sb.update(place(heads0, heads))
                with nc.Block() as block:
                    @block.sync
                    def _(sp):
                        sp.dma_start(x[:, 0:NT, :], a["x"][:, 0:NT, :]).then_inc(x0_loaded, 16)
                        load(sp, common + heads0 + att0, "att0")
                        sp.dma_start(x[:, NT:, :], a["x"][:, NT:, :]).then_inc(loaded, 16)
                        issued[0] += 16
                        loads["att0"] = issued[0]
                        loads["ident"] = issued[0]
                w = dict(w_of("a0_", heads0 + att0), bias_rows=a["bias_rows"], one_rows=a["one_rows"],
                         mask_qk=sb["mask_qk"], mask_kq=sb["mask_kq"], key="att0")
                project_heads(nc, "heads0", g, w, True, qkv)
            attend(nc, "attn0", g, w, True, qkv)
        clear_semaphores()

        early = stack.enter_context(ExitStack())
        sb.update(place(["f0_kb"], early))
        with nc.Block() as block:
            @block.sync
            def _(sp):
                load(sp, ["f0_kb"], "router")
        halves = place_halves(["f0_wq", *ffn0], early)
        experts = dict({n[3:]: w for n, w in halves.items()}, kb=sb["f0_kb"])
        expert_feed_forward(nc, "moe0", g, experts, cut=[(a[n], halves[n]) for n in ffn0],
                            cut_first=[(a["f0_wq"], halves["f0_wq"])])
        feature_attention(nc, "feat", g)
        expert_feed_forward(nc, "moe1", g, experts, cut=[], cut_first=[])
        early.close()
        clear_semaphores()

        sb.update(place(scan, stack))
        second = stack.enter_context(ExitStack())
        sb.update(place(att1, second))
        with nc.Block() as block:
            @block.sync
            def _(sp):
                load(sp, att1, "att1")
                sp.wait_ge(loaded, issued[0])
                load(sp, scan, "scan")
        qkv = stacks("attn1", 4, second)
        w = dict(w_of("a1_", att1), cos=sb["cos"], sin=sb["sin"], one_rows=a["one_rows"], key="att1")
        project_heads(nc, "heads1", g, w, False, qkv)
        attend(nc, "attn1", g, w, False, qkv)
        second.close()
        halves = place_halves(ffn1, stack)
        sparse_feed_forward(nc, "mlp0", g, *halves.values(), cut=[(a[n], halves[n]) for n in ffn1])
        gated_scan(nc, "scan", g, sb["s_act"], sb["s_val"], sb["s_rec"], "scan")
        sparse_feed_forward(nc, "mlp1", g, *halves.values(), cut=[], out=out)


def bf16_bits(v):
    bits = v.astype(np.float32).view(np.uint32)
    bits = (bits + 0x7FFF + ((bits >> 16) & 1)) & np.uint32(0xFFFF0000)
    return (bits >> 16).astype(np.uint16), v - bits.view(np.float32)


def bf16_parts(v):
    got = []
    for _ in range(3):
        bits, v = bf16_bits(v)
        got.append(bits)
    return np.stack(got)


def shape_constants():
    slopes = 1.0 / 2.0 ** (np.arange(1, HEADS + 1, dtype=np.float32) * np.float32(8.0 / HEADS))
    bias = (np.arange(1 - T, 1, dtype=np.float32)[None, :] * slopes[:, None]).astype(np.float32)
    upper = np.triu(np.full((P, P), -BIG, np.float32), 1)
    freqs = (1.0 / 10000.0 ** (np.arange(HD // 2, dtype=np.float32) / (HD // 2))).astype(np.float32)
    angles = (np.arange(T, dtype=np.float32)[:, None] * freqs).astype(np.float64)
    i = (np.arange(P) % HD) // 2
    sign = np.where(np.arange(P) % 2 == 0, -1.0, 1.0)
    return {
        "ident": np.eye(P, dtype=np.float32), "identb": bf16_bits(np.eye(P, dtype=np.float32))[0],
        "mask_qk": bf16_bits(upper)[0], "mask_kq": bf16_bits(np.ascontiguousarray(upper.T))[0],
        "bias_rows": bf16_parts(np.float32(HD ** 0.5) * bias), "one_rows": bf16_bits(np.ones((3, HEADS, T), np.float32))[0],
        "iota": np.tile(np.arange(NKEYS, dtype=np.float32), (P, 1)),
        "rankw": np.tile(TOPK - np.arange(TOPK, dtype=np.float32), (P, 1)),
        "cos": np.cos(angles).T[i].astype(np.float32),
        "sin": (np.sin(angles).T[i] * sign[:, None]).astype(np.float32),
    }


def rows(w):
    return np.ascontiguousarray(w.reshape(w.shape[0] // P, P, w.shape[1]).transpose(1, 0, 2))


def swapped(w):
    return w.reshape(w.shape[0], -1, 2)[:, :, ::-1].reshape(w.shape)


def laid_out(v):
    half = INTER // 2
    member = np.array([4 * (P * hf + p) + r for hf in range(2) for r in range(4) for p in range(P)])
    paired = np.array([2 * p + part for part in range(2) for p in range(P)])
    kb = np.zeros((P, B, P), np.float32)
    for b in range(B):
        for r in range(2):
            kb[NKEYS * r:NKEYS * (r + 1), b, NKEYS * r:NKEYS * (r + 1)] = v["L0_ffn_keys"][b // 2]
    wqkv, bqkv = v["L0_attn_a_Wqkv"].T, v["L0_attn_a_b_qkv"]
    return {
        "x": np.ascontiguousarray(v["L0_attn_a_x"].reshape(B * NT, P, D).transpose(1, 0, 2)),
        "a0_wq": rows(wqkv[:, 0:D]), "a0_wk": rows(wqkv[:, D:2 * D]), "a0_wv": rows(wqkv[:, 2 * D:]),
        "a0_bqk": np.ascontiguousarray(bqkv[:2 * D].reshape(4, P).T), "a0_bv": np.tile(bqkv[2 * D:], (P, 1)),
        "a0_wo": rows(v["L0_attn_a_Wout"].T), "a0_bo": np.tile(v["L0_attn_a_b_out"], (P, 1)),
        "f0_wq": rows(v["L0_ffn_W_q"]), "f0_kb": kb,
        "f0_gate": rows(v["L0_ffn_gate_w"]), "f0_up": rows(v["L0_ffn_up_w"]), "f0_down": rows(v["L0_ffn_down_w"]),
        "f0_de": rows(v["L0_ffn_down_embed"].T), "f0_ue": rows(v["L0_ffn_up_embed"]),
        "a1_wq": rows(v["L1_attn_a_W_q"]), "a1_wq2": rows(swapped(v["L1_attn_a_W_q"])),
        "a1_wk": rows(v["L1_attn_a_W_k"]), "a1_wk2": rows(swapped(v["L1_attn_a_W_k"])),
        "a1_wv": rows(v["L1_attn_a_W_v"]), "a1_wo": rows(v["L1_attn_a_W_o"]),
        "f1_gate": rows(v["L1_ffn_w_gate"][:, member]), "f1_up": rows(v["L1_ffn_w_up"][:, member]),
        "f1_down": rows(v["L1_ffn_w_down"][member]),
        "s_act": rows(v["L1_attn_b_W_act"].T[:, paired]), "s_rec": rows(v["L1_attn_b_W_rec"].T),
        "s_val": rows(v["L1_attn_b_W_val"].T[paired]),
    }


def kernel(**inputs):
    import concourse.bacc as _bacc
    from concourse.bass_utils import run_bass_kernel_spmd as _run

    nc = _bacc.Bacc("TRN2", target_bir_lowering=False, num_devices=1)
    arrays = laid_out({k: np.asarray(v) for k, v in inputs.items()})
    arrays.update(shape_constants())
    a = {}
    for name, v in arrays.items():
        ap = nc.dram_tensor(f"in_{name}", v.shape, mybir.dt.from_np(v.dtype), kind="ExternalInput").ap()
        a[name] = ap.bitcast(BF16) if v.dtype == np.uint16 else ap
    out = nc.dram_tensor("out_x", (P, B * NT, D), F32, kind="ExternalOutput").ap()
    stages(nc, a, out)
    r = _run(nc, [{f"in_{name}": v for name, v in arrays.items()}], core_ids=[0])
    got = r.results[0]["out_x"]
    return np.ascontiguousarray(got.transpose(1, 0, 2)).reshape(B, T, D)
```
